# Optimizing a Trainium2 kernel written in Bass

```python
import numpy as np
import jax
import jax.numpy as jnp

def _softmax(x, axis=-1):
    return jax.nn.softmax(x, axis=axis)

def _gelu(x):
    return jax.nn.gelu(x, approximate=True)

def _silu(x):
    return jax.nn.silu(x)

def _sigmoid(x):
    return jax.nn.sigmoid(x)

def _layernorm(x, axis=-1, eps=1e-05):
    m = jnp.mean(x, axis=axis, keepdims=True)
    v = jnp.var(x, axis=axis, keepdims=True)
    return (x - m) / jnp.sqrt(v + eps)

def _scatter_add(tgt, idx, src, axis=0):
    return tgt.at[idx].add(src)

def _segment_sum(src, seg, n):
    return jax.ops.segment_sum(src, seg, n)
kernel_name = 'mk_sandwich_d2_jaxref_r8_917bb6'

def setup_inputs(seed: int=0):
    np.random.seed(seed)
    _w = jnp.asarray

    def _L0_attn_setup():
        import jax, jax.numpy as jnp
        import numpy as np
        BLOCK = 32
        NUM_HEADS = 16
        HEAD_DIM = 128
        FP4_GRID = jnp.array([0.0, 0.5, 1.0, 1.5, 2.0, 3.0, 4.0, 6.0], dtype=jnp.float32)

        def quantize_to_mxfp4(w, block_size=BLOCK):
            D, F = w.shape
            blocks = w.reshape(D // block_size, block_size, F)
            amax = jnp.max(jnp.abs(blocks), axis=1)
            e = jnp.floor(jnp.log2(jnp.maximum(amax, 1e-12) / 6.0))
            scale = jnp.exp2(e)
            v = blocks / scale[:, None, :]
            idx = jnp.argmin(jnp.abs(jnp.abs(v)[..., None] - FP4_GRID), axis=-1)
            codes = jnp.sign(v) * FP4_GRID[idx]
            return (codes.reshape(D, F).astype(jnp.float32), scale.astype(jnp.float32))

        def _mxfp4_matmul(x, codes, scales, block_size=BLOCK):
            w = codes * jnp.repeat(scales, block_size, axis=0)
            return x @ w
        key = jax.random.key(seed)
        ks = jax.random.split(key, 9)
        B, S, D = (2, 256, 256)
        feat = NUM_HEADS * HEAD_DIM
        x = jax.random.normal(ks[0], (B, S, D), dtype=jnp.float32)

        def make_w(k, din, dout):
            w = jax.random.normal(k, (din, dout), dtype=jnp.float32) * (1.0 / np.sqrt(din))
            return quantize_to_mxfp4(w, BLOCK)
        wq_codes, wq_scales = make_w(ks[1], D, feat)
        wk_codes, wk_scales = make_w(ks[2], D, feat)
        wv_codes, wv_scales = make_w(ks[3], D, feat)
        wo_codes, wo_scales = make_w(ks[4], feat, D)
        bq = jnp.zeros((feat,), jnp.float32)
        bk = jnp.zeros((feat,), jnp.float32)
        bv = jnp.zeros((feat,), jnp.float32)
        bo = jnp.zeros((D,), jnp.float32)
        return {'x': x, 'wq_codes': wq_codes, 'wq_scales': wq_scales, 'bq': bq, 'wk_codes': wk_codes, 'wk_scales': wk_scales, 'bk': bk, 'wv_codes': wv_codes, 'wv_scales': wv_scales, 'bv': bv, 'wo_codes': wo_codes, 'wo_scales': wo_scales, 'bo': bo}
    _L0_attn_in = _L0_attn_setup()

    def _L0_ffn_setup():
        import jax, jax.numpy as jnp
        import numpy as np
        HIDDEN = 256
        INTER = 704
        B, S = (2, 256)

        def _ternary(key, shape):
            return jax.random.randint(key, shape, -1, 2).astype(jnp.float32)
        key = jax.random.key(seed)
        ks = jax.random.split(key, 7)
        x = jax.random.normal(ks[0], (B, S, HIDDEN), dtype=jnp.float32)
        gate_w = _ternary(ks[1], (INTER, HIDDEN))
        up_w = _ternary(ks[2], (INTER, HIDDEN))
        down_w = _ternary(ks[3], (HIDDEN, INTER))
        gate_s = jax.random.uniform(ks[4], (INTER,), minval=0.01, maxval=0.1, dtype=jnp.float32)
        up_s = jax.random.uniform(ks[5], (INTER,), minval=0.01, maxval=0.1, dtype=jnp.float32)
        down_s = jax.random.uniform(ks[6], (HIDDEN,), minval=0.01, maxval=0.1, dtype=jnp.float32)
        return {'x': x, 'gate_w': gate_w, 'up_w': up_w, 'down_w': down_w, 'gate_s': gate_s, 'up_s': up_s, 'down_s': down_s}
    _L0_ffn_in = _L0_ffn_setup()

    def _L1_attn_setup():
        import jax, jax.numpy as jnp
        import numpy as np
        B, T, C = (4, 256, 256)
        N_HEAD = 16
        HEAD_DIM = C // N_HEAD
        key = jax.random.key(seed)
        k1, k2, k3, k4, k5 = jax.random.split(key, 5)
        s = 1.0 / np.sqrt(C)
        return {'x': jax.random.normal(k1, (B, T, C), dtype=jnp.float32), 'w_attn': jax.random.normal(k2, (C, 3 * C), dtype=jnp.float32) * s, 'b_attn': jax.random.normal(k3, (3 * C,), dtype=jnp.float32) * 0.02, 'w_proj': jax.random.normal(k4, (C, C), dtype=jnp.float32) * s, 'b_proj': jax.random.normal(k5, (C,), dtype=jnp.float32) * 0.02}
    _L1_attn_in = _L1_attn_setup()

    def _L1_ffn_setup():
        import jax, jax.numpy as jnp
        import numpy as np
        H = 256
        IM = 128
        E = 16
        K = 8
        N_SHARED = 2
        IS = IM * N_SHARED
        B, L = (1, 256)
        SCALE = 2.5
        W_INIT = 0.02
        key = jax.random.key(seed)
        ks = jax.random.split(key, 9)
        return {'hidden_states': jax.random.normal(ks[0], (B, L, H), jnp.float32), 'gate_w': jax.random.normal(ks[1], (E, H), jnp.float32) * W_INIT, 'Wg': jax.random.normal(ks[2], (E, H, IM), jnp.float32) * W_INIT, 'Wu': jax.random.normal(ks[3], (E, H, IM), jnp.float32) * W_INIT, 'Wd': jax.random.normal(ks[4], (E, IM, H), jnp.float32) * W_INIT, 'sWg': jax.random.normal(ks[5], (H, IS), jnp.float32) * W_INIT, 'sWu': jax.random.normal(ks[6], (H, IS), jnp.float32) * W_INIT, 'sWd': jax.random.normal(ks[7], (IS, H), jnp.float32) * W_INIT}
    _L1_ffn_in = _L1_ffn_setup()
    _d = {'L0_attn_x': _L0_attn_in['x'], 'L0_attn_wq_codes': _L0_attn_in['wq_codes'], 'L0_attn_wq_scales': _L0_attn_in['wq_scales'], 'L0_attn_bq': _L0_attn_in['bq'], 'L0_attn_wk_codes': _L0_attn_in['wk_codes'], 'L0_attn_wk_scales': _L0_attn_in['wk_scales'], 'L0_attn_bk': _L0_attn_in['bk'], 'L0_attn_wv_codes': _L0_attn_in['wv_codes'], 'L0_attn_wv_scales': _L0_attn_in['wv_scales'], 'L0_attn_bv': _L0_attn_in['bv'], 'L0_attn_wo_codes': _L0_attn_in['wo_codes'], 'L0_attn_wo_scales': _L0_attn_in['wo_scales'], 'L0_attn_bo': _L0_attn_in['bo'], 'L0_ffn_gate_w': _L0_ffn_in['gate_w'], 'L0_ffn_up_w': _L0_ffn_in['up_w'], 'L0_ffn_down_w': _L0_ffn_in['down_w'], 'L0_ffn_gate_s': _L0_ffn_in['gate_s'], 'L0_ffn_up_s': _L0_ffn_in['up_s'], 'L0_ffn_down_s': _L0_ffn_in['down_s'], 'L1_attn_w_attn': _L1_attn_in['w_attn'], 'L1_attn_b_attn': _L1_attn_in['b_attn'], 'L1_attn_w_proj': _L1_attn_in['w_proj'], 'L1_attn_b_proj': _L1_attn_in['b_proj'], 'L1_ffn_gate_w': _L1_ffn_in['gate_w'], 'L1_ffn_Wg': _L1_ffn_in['Wg'], 'L1_ffn_Wu': _L1_ffn_in['Wu'], 'L1_ffn_Wd': _L1_ffn_in['Wd'], 'L1_ffn_sWg': _L1_ffn_in['sWg'], 'L1_ffn_sWu': _L1_ffn_in['sWu'], 'L1_ffn_sWd': _L1_ffn_in['sWd']}
    _x0 = _d['L0_attn_x']
    _d['L0_attn_x'] = jax.random.normal(jax.random.fold_in(jax.random.key(seed), 1), (2, 1024, 256), dtype=_x0.dtype)
    del _x0
    return _d

def reference(L0_attn_x, L0_attn_wq_codes, L0_attn_wq_scales, L0_attn_bq, L0_attn_wk_codes, L0_attn_wk_scales, L0_attn_bk, L0_attn_wv_codes, L0_attn_wv_scales, L0_attn_bv, L0_attn_wo_codes, L0_attn_wo_scales, L0_attn_bo, L0_ffn_gate_w, L0_ffn_up_w, L0_ffn_down_w, L0_ffn_gate_s, L0_ffn_up_s, L0_ffn_down_s, L1_attn_w_attn, L1_attn_b_attn, L1_attn_w_proj, L1_attn_b_proj, L1_ffn_gate_w, L1_ffn_Wg, L1_ffn_Wu, L1_ffn_Wd, L1_ffn_sWg, L1_ffn_sWu, L1_ffn_sWd):

    def _L0_attn_ref(x, wq_codes, wq_scales, bq, wk_codes, wk_scales, bk, wv_codes, wv_scales, bv, wo_codes, wo_scales, bo):
        import jax, jax.numpy as jnp
        import numpy as np
        BLOCK = 32
        NUM_HEADS = 16
        HEAD_DIM = 128
        FP4_GRID = jnp.array([0.0, 0.5, 1.0, 1.5, 2.0, 3.0, 4.0, 6.0], dtype=jnp.float32)

        def quantize_to_mxfp4(w, block_size=BLOCK):
            D, F = w.shape
            blocks = w.reshape(D // block_size, block_size, F)
            amax = jnp.max(jnp.abs(blocks), axis=1)
            e = jnp.floor(jnp.log2(jnp.maximum(amax, 1e-12) / 6.0))
            scale = jnp.exp2(e)
            v = blocks / scale[:, None, :]
            idx = jnp.argmin(jnp.abs(jnp.abs(v)[..., None] - FP4_GRID), axis=-1)
            codes = jnp.sign(v) * FP4_GRID[idx]
            return (codes.reshape(D, F).astype(jnp.float32), scale.astype(jnp.float32))

        def _mxfp4_matmul(x, codes, scales, block_size=BLOCK):
            w = codes * jnp.repeat(scales, block_size, axis=0)
            return x @ w
        B, S, D = x.shape
        q = _mxfp4_matmul(x, wq_codes, wq_scales) + bq
        k = _mxfp4_matmul(x, wk_codes, wk_scales) + bk
        v = _mxfp4_matmul(x, wv_codes, wv_scales) + bv
        q = q.reshape(B, S, NUM_HEADS, HEAD_DIM)
        k = k.reshape(B, S, NUM_HEADS, HEAD_DIM)
        v = v.reshape(B, S, NUM_HEADS, HEAD_DIM)
        scores = jnp.einsum('bqhd,bkhd->bhqk', q, k) / jnp.sqrt(jnp.float32(HEAD_DIM))
        attn = jax.nn.softmax(scores, axis=-1)
        out = jnp.einsum('bhqk,bkhd->bqhd', attn, v).reshape(B, S, NUM_HEADS * HEAD_DIM)
        return _mxfp4_matmul(out, wo_codes, wo_scales) + bo

    def _L0_ffn_ref(x, gate_w, up_w, down_w, gate_s, up_s, down_s):
        import jax, jax.numpy as jnp
        import numpy as np
        HIDDEN = 256
        INTER = 704
        B, S = (2, 256)

        def _ternary(key, shape):
            return jax.random.randint(key, shape, -1, 2).astype(jnp.float32)
        b, s, h = x.shape
        xf = x.reshape(b * s, h)
        g = jnp.einsum('th,ih->ti', xf, gate_w) * gate_s
        u = jnp.einsum('th,ih->ti', xf, up_w) * up_s
        hdn = jax.nn.silu(g) * u
        out = jnp.einsum('ti,hi->th', hdn, down_w) * down_s
        return out.reshape(b, s, -1)

    def _L1_attn_ref(x, w_attn, b_attn, w_proj, b_proj):
        import jax, jax.numpy as jnp
        import numpy as np
        B, T, C = (4, 256, 256)
        N_HEAD = 16
        HEAD_DIM = C // N_HEAD
        Bsz, Tlen, Cdim = x.shape
        qkv = x @ w_attn + b_attn
        q, k, v = jnp.split(qkv, 3, axis=-1)

        def heads(t):
            return t.reshape(Bsz, Tlen, N_HEAD, HEAD_DIM).transpose(0, 2, 1, 3)
        q, k, v = (heads(q), heads(k), heads(v))
        scale = 1.0 / np.sqrt(HEAD_DIM).astype(np.float32)
        att = jnp.einsum('bhqd,bhkd->bhqk', q, k) * scale
        causal = jnp.tril(jnp.ones((Tlen, Tlen), dtype=bool))
        att = jnp.where(causal, att, -jnp.inf)
        att = jax.nn.softmax(att, axis=-1)
        y = jnp.einsum('bhqk,bhkd->bhqd', att, v)
        y = y.transpose(0, 2, 1, 3).reshape(Bsz, Tlen, Cdim)
        return y @ w_proj + b_proj

    def _L1_ffn_ref(hidden_states, gate_w, Wg, Wu, Wd, sWg, sWu, sWd):
        import jax, jax.numpy as jnp
        import numpy as np
        H = 256
        IM = 128
        E = 16
        K = 8
        N_SHARED = 2
        IS = IM * N_SHARED
        B, L = (1, 256)
        SCALE = 2.5
        W_INIT = 0.02
        orig_shape = hidden_states.shape
        h = hidden_states.reshape(-1, H)
        T = h.shape[0]
        shared = jax.nn.silu(h @ sWg) * (h @ sWu) @ sWd
        router_logits = h @ gate_w.T
        routing_weights = jax.nn.sigmoid(router_logits)
        topk_w, topk_idx = jax.lax.top_k(routing_weights, K)
        topk_w = topk_w / (jnp.sum(topk_w, axis=-1, keepdims=True) + 1e-06)
        topk_w = topk_w * SCALE
        comb = jnp.zeros((T, E), h.dtype).at[jnp.arange(T)[:, None], topk_idx].add(topk_w)
        g = jnp.einsum('th,ehi->eti', h, Wg)
        u = jnp.einsum('th,ehi->eti', h, Wu)
        eo = jnp.einsum('eti,eih->eth', jax.nn.silu(g) * u, Wd)
        routed = jnp.einsum('eth,te->th', eo, comb)
        return (shared + routed).reshape(orig_shape)
    x = L0_attn_x
    x = x + _layernorm(_L0_attn_ref(_layernorm(x, axis=-1), L0_attn_wq_codes, L0_attn_wq_scales, L0_attn_bq, L0_attn_wk_codes, L0_attn_wk_scales, L0_attn_bk, L0_attn_wv_codes, L0_attn_wv_scales, L0_attn_bv, L0_attn_wo_codes, L0_attn_wo_scales, L0_attn_bo), axis=-1)
    x = x + _layernorm(_L0_ffn_ref(_layernorm(x, axis=-1), L0_ffn_gate_w, L0_ffn_up_w, L0_ffn_down_w, L0_ffn_gate_s, L0_ffn_up_s, L0_ffn_down_s), axis=-1)
    x = x + _layernorm(_L1_attn_ref(_layernorm(x, axis=-1), L1_attn_w_attn, L1_attn_b_attn, L1_attn_w_proj, L1_attn_b_proj), axis=-1)
    x = x + _layernorm(_L1_ffn_ref(_layernorm(x, axis=-1), L1_ffn_gate_w, L1_ffn_Wg, L1_ffn_Wu, L1_ffn_Wd, L1_ffn_sWg, L1_ffn_sWu, L1_ffn_sWd), axis=-1)
    return x

_drawn_inputs = setup_inputs


def setup_inputs(seed=0):
    import zlib

    import numpy as np

    out = dict(_drawn_inputs(seed))
    spreads = {'L0_attn_bq': (0.0, 0.1),
     'L0_attn_bk': (0.0, 0.1),
     'L0_attn_bv': (0.0, 0.1),
     'L0_attn_bo': (0.0, 0.1)}
    factors = {}
    for name, (base, spread) in spreads.items():
        noise = np.random.default_rng([zlib.crc32(name.encode()), seed]).standard_normal(out[name].shape)
        drawn = base * np.exp(spread * noise) if base else spread * noise
        out[name] = jnp.asarray(drawn.astype(out[name].dtype))
    for name, factor in factors.items():
        out[name] = (out[name] * factor).astype(out[name].dtype)
    return out
```

```python
from contextlib import ExitStack

import concourse.bass as bass
from concourse import mybir

F32 = mybir.dt.float32
F32R = mybir.dt.float32r
F16 = mybir.dt.float16
BF16 = mybir.dt.bfloat16
ALU = mybir.AluOpType
ACT = mybir.ActivationFunctionType
AX = mybir.AxisListType

P = 128
BATCH, SEQ, C = 2, 1024, 256
TOK = BATCH * SEQ
TT = TOK // P
KC = C // P
NB = 512
GT = NB // P
EPS = 1e-5

H0, D0 = 16, 128
FP4_BLOCK = 32
H1, D1 = 16, 16
D1P = 32
IM = 128
INTER0 = 704
N_FFN0 = -(-INTER0 // IM)
N_EXPERT, N_TOP, N_SHARED = 16, 8, 2
ROUTE_SCALE = 2.5

PASSES = ((0, 0), (0, 1), (1, 0))


class Count:

    def __init__(self, sem, base=0):
        self.sem, self.base, self.n = sem, base, 0

    def inc(self, ins):
        ins.then_inc(self.sem, 1)
        self.n += 1

    def wait(self, eng):
        eng.wait_ge(self.sem, self.base + self.n)

    def step(self, eng, ins):
        self.inc(ins)
        self.wait(eng)


class Core:
    pass


class Stage:

    def __init__(self, nc, ctx, name):
        self.nc, self.ctx, self.name = nc, ctx, name

    def sb(self, n, shape, dt=F32):
        return self.ctx.enter_context(self.nc.sbuf_tensor(f"{self.name}_{n}", shape, dt))

    def halves(self, n, shape):
        return [self.sb(f"{n}_{h}", shape, F32R) for h in ("hi", "lo")]

    def sem(self, n):
        return self.ctx.enter_context(self.nc.semaphore(f"{self.name}_{n}"))


def three_passes(nc, out, stationary, moving, start=True, stop=True):
    for n, (s, m) in enumerate(PASSES):
        ins = nc.tensor.matmul(out, stationary[s], moving[m], start=start and n == 0,
                               stop=stop and n == len(PASSES) - 1)
    return ins


def project(nc, out, stationary, moving):
    for kt in range(KC):
        ins = three_passes(nc, out, stationary(kt), moving(kt), start=kt == 0, stop=kt == KC - 1)
    return ins


def norm_stage(nc, k, name, *, sublayer=True, load=False, post=None, following=True, plain=False, out=None):
    groups = TT // GT
    with ExitStack() as ctx:
        st = Stage(nc, ctx, name)
        stats = st.sb("stats", [P, TT, 6])
        mean_var = st.sb("mean_var", [P, TT, 2])
        veps = st.sb("veps", [P, TT])
        rstd = st.sb("rstd", [P, TT])
        power = st.sb("power", [P, TT])
        normed = st.sb("normed", [P, TT, C])
        turned = st.sb("turned", [P, 2, KC, NB])
        row = st.sb("row", [P, C])
        loaded, row_loaded = st.sem("loaded"), st.sem("row_loaded")
        own, x_ready, stored = (st.sem(n) for n in ("own", "x_ready", "stored"))
        power_set, var_ready, rstd_ready = (st.sem(n) for n in ("power_set", "var_ready", "rstd_ready"))
        normed_ready, turned_ready = st.sem("normed_ready"), st.sem("turned_ready")
        copied, lo_done = st.sem("copied"), st.sem("lo_done")
        block = ctx.enter_context(nc.Block())
        rows_out = k.acc if plain else normed

        @block.sync
        def _(sp):
            if post:
                sp.dma_start(row[:], post[0].partition_broadcast(P)).then_inc(row_loaded, 16)
            if load:
                x_rows = k.x_dram.rearrange("(g t p) c -> g p t c", t=GT, p=P)
                for g in range(groups):
                    sp.dma_start(k.x[:, g * GT:(g + 1) * GT, :], x_rows[g]).then_inc(loaded, 16)
            if not following:
                out_rows = out.rearrange("(g t p) c -> g p t c", t=GT, p=P)
                for g in range(groups):
                    sp.wait_ge(x_ready, g + 1)
                    sp.dma_start(out_rows[g], k.x[:, g * GT:(g + 1) * GT, :]).then_inc(stored, 16)
                sp.wait_ge(stored, 16 * groups)

        @block.vector
        def _(dve):
            if plain:
                return
            link = Count(own)

            def statistics(src, g):
                for t in range(g * GT, (g + 1) * GT):
                    link.inc(nc.vector.bn_stats(stats[:, t, :], src[:, t, :]))
                link.wait(dve)
                for t in range(g * GT, (g + 1) * GT):
                    link.inc(nc.vector.bn_aggr(mean_var[:, t, :], stats[:, t, :]))

            def variances():
                link.wait(dve)
                nc.vector.tensor_scalar(veps[:], mean_var[:, :, 1], EPS, None, ALU.add).then_inc(var_ready, 1)

            def normalise(src, g):
                for t in range(g * GT, (g + 1) * GT):
                    ins = nc.vector.tensor_scalar(normed[:, t, :], src[:, t, :], mean_var[:, t, 0:1],
                                                  rstd[:, t:t + 1], ALU.subtract, ALU.mult)
                return ins

            nc.vector.memset(power[:], -0.5).then_inc(power_set, 1)
            if sublayer:
                if post:
                    dve.wait_ge(row_loaded, 16)
                for g in range(groups):
                    if post:
                        acc = k.acc[:, g * GT:(g + 1) * GT, :]
                        link.step(dve, nc.vector.tensor_tensor(
                            acc, acc, row[:].unsqueeze(1).broadcast_to([P, GT, C]), post[1]))
                    statistics(k.acc, g)
                variances()
                dve.wait_ge(rstd_ready, 1)
                if load:
                    dve.wait_ge(loaded, 16 * groups)
                for g in range(groups):
                    link.step(dve, normalise(k.acc, g))
                    x = k.x[:, g * GT:(g + 1) * GT, :]
                    ins = nc.vector.tensor_tensor(x, x, normed[:, g * GT:(g + 1) * GT, :], ALU.add)
                    if following:
                        link.step(dve, ins)
                        statistics(k.x, g)
                    else:
                        ins.then_inc(x_ready, 1)
            else:
                dve.wait_ge(loaded, 16 * groups)
                for g in range(groups):
                    statistics(k.x, g)
            if following:
                variances()
                dve.wait_ge(rstd_ready, 1 + int(sublayer))
                for g in range(groups):
                    normalise(k.x, g).then_inc(normed_ready, 1)

        @block.gpsimd
        def _(pool):
            if not plain:
                pool.wait_ge(power_set, 1)
                for n in range(int(sublayer) + int(following)):
                    pool.wait_ge(var_ready, n + 1)
                    nc.gpsimd.tensor_tensor(rstd[:], veps[:], power[:], ALU.pow).then_inc(rstd_ready, 1)
            if following:
                for g in range(groups):
                    pool.wait_ge(copied, g + 1)
                    for kt in range(KC):
                        part = slice(g * NB, (g + 1) * NB)
                        ins = nc.gpsimd.tensor_tensor(k.xT[1][:, kt, part], turned[:, g % 2, kt, :],
                                                      k.xT[0][:, kt, part].bitcast(F32), ALU.subtract)
                    ins.then_inc(lo_done, 1)

        @block.tensor
        def _(pe):
            if following:
                for g in range(groups):
                    if not plain:
                        pe.wait_ge(normed_ready, g + 1)
                    if g >= 2:
                        pe.wait_ge(copied, g - 1)
                    for kt in range(KC):
                        for j in range(GT):
                            ins = nc.tensor.transpose(k.psum[:, g % 2 * KC + kt, j * P:(j + 1) * P],
                                                      rows_out[:, g * GT + j, kt * P:(kt + 1) * P], k.ident[:])
                    ins.then_inc(turned_ready, 1)

        @block.scalar
        def _(act):
            if following:
                for g in range(groups):
                    act.wait_ge(turned_ready, g + 1)
                    bank = k.psum[:, g % 2 * KC:(g % 2 + 1) * KC, :]
                    nc.scalar.activation(k.xT[0][:, :, g * NB:(g + 1) * NB], bank, ACT.Copy)
                    if g >= 2:
                        act.wait_ge(lo_done, g - 1)
                    nc.scalar.activation(turned[:, g % 2], bank, ACT.Copy).then_inc(copied, 1)


HP = 2
WQKV = 3 * KC * HP * D0
WO = HP * C
ST = SEQ // P
QG = ST // GT


def attention0_stage(nc, k, name, ins):
    scale = float(D0) ** -0.5
    tiles = HP * ST
    groups = tiles // GT
    qk_uses, v_uses = HP * 2 * SEQ // NB, ST * HP * D0 // NB
    uses = qk_uses + v_uses + 2 * tiles
    passes = H0 // HP
    scale_rows = FP4_BLOCK
    with ExitStack() as ctx:
        st = Stage(nc, ctx, name)
        codes = st.sb("codes", [P, WQKV + WO])
        scales = st.sb("scales", [P, WQKV + WO])
        scale_row = st.sb("scale_row", [P, 1])
        bias_in = st.sb("bias_in", [P, 2 * HP])
        bias_qk = st.sb("bias_qk", [P, 2 * HP])
        bias_v_in = st.sb("bias_v_in", [P, HP * D0])
        bias_v = st.sb("bias_v", [P, HP * D0])
        w = st.halves("w", [P, 3, KC, HP * D0])
        wo = st.halves("wo", [P, HP, C])
        q = st.halves("q", [P, HP, SEQ])
        key = st.halves("key", [P, HP, SEQ])
        v = st.halves("v", [P, ST, HP * D0])
        prob = st.sb("prob", [P, 2, SEQ])
        v_whole = prob[:, 1, :].rearrange("p (a n) -> p a n", a=2)
        probT = st.halves("probT", [P, 2, ST, NB])
        o = st.halves("o", [P, NB])
        neg_max = st.sb("neg_max", [P, 2])
        total = st.sb("total", [P, tiles])
        over_total = st.sb("over_total", [P, tiles])
        landed, staged_free, w_ready, wo_ready = (st.sem(n) for n in ("landed", "staged_free", "w_ready", "wo_ready"))
        ring_full, ring_hi, ring_free = (st.sem(n) for n in ("ring_full", "ring_hi", "ring_free"))
        scale_set = st.sem("scale_set")
        v_hi_done, v_done = st.sem("v_hi_done"), st.sem("v_done")
        score_full, max_ready, exp_done = (st.sem(n) for n in ("score_full", "max_ready", "exp_done"))
        o_full, o_hi_done, o_done = (st.sem(n) for n in ("o_full", "o_hi_done", "o_done"))
        out_full, out_done, own, split = (st.sem(n) for n in ("out_full", "out_done", "own", "split"))
        block = ctx.enter_context(nc.Block())

        ring = lambda n: k.psum[:, 4 + n % 2, :]
        scores = lambda i: k.psum[:, i % 2 * 2:i % 2 * 2 + 2, :]
        o_bank, out_bank = k.psum[:, 6, :], k.psum[:, 7, :]
        turn_use = lambda i, half: qk_uses + v_uses + 2 * i + half

        def qk_chunk(n):
            return n // (SEQ // NB) % 2, n // (2 * SEQ // NB), n % (SEQ // NB)

        @block.sync
        def _(sp):
            def load(m):
                at = m * HP * D0
                part = bass.ds(at, HP * D0)
                n = 0
                for which, x in enumerate("qkv"):
                    to = slice(which * KC * HP * D0, (which + 1) * KC * HP * D0)
                    sp.dma_start(codes[:, to].rearrange("p (k n) -> p k n", k=KC),
                                 ins[f"w{x}_codes"].rearrange("(k p) n -> p k n", p=P)[:, :, part]).then_inc(landed, 16)
                    rows = ins[f"w{x}_scales"].rearrange("(k b) n -> b k n", k=KC)
                    for b in range(P // scale_rows):
                        sp.dma_start(scales[b * scale_rows:(b + 1) * scale_rows, to].rearrange("p (k n) -> p k n", k=KC),
                                     rows[b:b + 1, :, part].squeeze(0).partition_broadcast(scale_rows)).then_inc(landed, 16)
                        n += 1
                    n += 1
                sp.dma_start(codes[:, WQKV:].rearrange("p (h n) -> p h n", h=HP),
                             ins["wo_codes"].rearrange("(h p) n -> p h n", p=P)[:, bass.ds(m * HP, HP), :]).then_inc(landed, 16)
                rows = ins["wo_scales"].rearrange("(h b) n -> b h n", b=P // scale_rows)
                for b in range(P // scale_rows):
                    sp.dma_start(scales[b * scale_rows:(b + 1) * scale_rows, WQKV:].rearrange("p (h n) -> p h n", h=HP),
                                 rows[b:b + 1, bass.ds(m * HP, HP), :].squeeze(0).partition_broadcast(scale_rows)).then_inc(landed, 16)
                for which, x in enumerate("qk"):
                    sp.dma_start(bias_in[:, which * HP:(which + 1) * HP],
                                 ins[f"b{x}"][:, bass.ds(m * HP, HP)]).then_inc(landed, 16)
                sp.dma_start(bias_v_in[:], ins["bv"][part].partition_broadcast(P)).then_inc(landed, 16)

            with sp.Fori(0, passes) as m:
                sp.wait_ge(staged_free, m + 1)
                load(m)
        loads = 16 * (3 * (1 + P // scale_rows) + 1 + P // scale_rows + 2 + 1)

        @block.gpsimd
        def _(pool):
            pool.nop().then_inc(staged_free, 1)
            nc.gpsimd.memset(scale_row[:], scale).then_inc(scale_set, 1)
            pool.wait_ge(scale_set, 1)
            for _ in range(2):
                pool.nop().then_inc(v_done, 1)

            def split_weights(m, first=False):
                pool.wait_ge(landed, (m + 1) * loads)
                flat = lambda t: t[:].rearrange("p a b c -> p (a b c)")
                nq = KC * HP * D0
                n = m * 8
                nc.gpsimd.tensor_tensor(scales[:, 0:nq], scales[:, 0:nq], scale_row[:].broadcast_to([P, nq]), ALU.mult).then_inc(split, 1)
                nc.gpsimd.tensor_scalar(bias_in[:, 0:HP], bias_in[:, 0:HP], scale, 1.0, ALU.mult, ALU.mult).then_inc(split, 1)
                pool.wait_ge(split, n + 2)
                if not first:
                    pool.wait_ge(ring_full, (2 * (m - 1) + 1) * uses + qk_uses + v_uses)
                nc.gpsimd.tensor_tensor(flat(w[0]), codes[:, 0:WQKV], scales[:, 0:WQKV], ALU.mult).then_inc(split, 1)
                nc.gpsimd.tensor_scalar(bias_qk[:], bias_in[:], 1.0, 1.0, ALU.mult, ALU.mult)
                nc.gpsimd.tensor_scalar(bias_v[:], bias_v_in[:], 1.0, 1.0, ALU.mult, ALU.mult)
                if not first:
                    pool.wait_ge(out_full, 2 * groups * 2 * m)
                nc.gpsimd.tensor_tensor(wo[0][:].rearrange("p a b -> p (a b)"), codes[:, WQKV:], scales[:, WQKV:],
                                        ALU.mult).then_inc(split, 1)
                pool.wait_ge(split, n + 4)
                nc.gpsimd.tensor_tensor(codes[:], codes[:], scales[:], ALU.mult).then_inc(split, 1)
                pool.wait_ge(split, n + 5)
                nc.gpsimd.tensor_tensor(flat(w[1]), codes[:, 0:WQKV], flat(w[0]).bitcast(F32), ALU.subtract).then_inc(w_ready, 1)
                nc.gpsimd.tensor_tensor(wo[1][:].rearrange("p a b -> p (a b)"), codes[:, WQKV:],
                                        wo[0][:].rearrange("p a b -> p (a b)").bitcast(F32), ALU.subtract).then_inc(wo_ready, 1)
                pool.wait_ge(wo_ready, m + 1)
                pool.nop().then_inc(staged_free, 1)
                for _ in range(3):
                    pool.nop().then_inc(split, 1)

            def v_lo(m):
                for half in range(2):
                    for n in range(v_uses):
                        use = (m * 2 + half) * v_uses + n
                        pool.wait_ge(v_hi_done, use + 1)
                        to = slice(n * GT // HP, (n + 1) * GT // HP)
                        nc.gpsimd.tensor_tensor(v[1][:, to, :].rearrange("p t d -> p (t d)"), v_whole[:, n % 2, :],
                                                v[0][:, to, :].rearrange("p t d -> p (t d)").bitcast(F32),
                                                ALU.subtract).then_inc(v_done, 1)

            split_weights(0, first=True)
            with pool.Fori(0, passes - 1) as m:
                v_lo(m)
                split_weights(m + 1)
            v_lo(passes - 1)

        @block.tensor
        def _(pe):
            def take_ring(half, n):
                use = half * uses + n
                pe.wait_ge(ring_free, use + 1)

            def project_qk(half, b):
                for n in range(qk_uses):
                    which, head, c = qk_chunk(n)
                    cols = slice(head * D0, (head + 1) * D0)
                    tokens = slice(b * SEQ + c * NB, b * SEQ + (c + 1) * NB)
                    take_ring(half, n)
                    project(nc, ring(n), lambda kt: [h[:, which, kt, cols] for h in w],
                            lambda kt: [h[:, kt, tokens] for h in k.xT]).then_inc(ring_full, 1)

            def project_v(half, b):
                for n in range(v_uses):
                    take_ring(half, qk_uses + n)
                    for j in range(2):
                        t = b * ST + 2 * n + j
                        mm = project(nc, ring(n)[:, j * HP * D0:(j + 1) * HP * D0],
                                     lambda kt: [h[:, kt, t * P:(t + 1) * P] for h in k.xT],
                                     lambda kt: [h[:, 2, kt, :] for h in w])
                    mm.then_inc(ring_full, 1)

            def score(half, i):
                head, t = i // ST, i % ST
                pe.wait_ge(exp_done, half * tiles + i + 1)
                for c in range(SEQ // NB):
                    mm = three_passes(nc, scores(i)[:, c, :], [h[:, head, t * P:(t + 1) * P] for h in q],
                                      [h[:, head, c * NB:(c + 1) * NB] for h in key])
                mm.then_inc(score_full, 1)

            def turn(half, i):
                pe.wait_ge(exp_done, half * tiles + i + 3)
                for half_tile in range(2):
                    use = turn_use(i, half_tile)
                    take_ring(half, use)
                    for j in range(GT):
                        kt = half_tile * GT + j
                        mm = nc.tensor.transpose(ring(use)[:, j * P:(j + 1) * P], prob[:, i % 2, kt * P:(kt + 1) * P], k.ident[:])
                    mm.then_inc(ring_full, 1)

            def weighted_v(half, g, part):
                head = g // QG
                if part == 0:
                    pe.wait_ge(ring_free, half * uses + turn_use((g + 1) * GT - 1, 1) + 3)
                    pe.wait_ge(o_done, half * groups + g + 1)
                    if g == 0:
                        pe.wait_ge(v_done, (half + 1) * v_uses + 2)
                n = ST // GT
                for kt in range(part * n, (part + 1) * n):
                    mm = three_passes(nc, o_bank, [h[:, kt, head * D0:(head + 1) * D0] for h in v],
                                      [h[:, g % 2, kt, :] for h in probT], start=kt == 0, stop=kt == ST - 1)
                if part == GT - 1:
                    mm.then_inc(o_full, 1)

            def output(half, g, part):
                use = (half * groups + g) * 2 + part
                if part == 0:
                    pe.wait_ge(o_done, half * groups + g + 2)
                pe.wait_ge(out_done, use + 1)
                for j in range(2):
                    t = part * 2 + j
                    mm = three_passes(nc, out_bank[:, j * C:(j + 1) * C], [h[:, t * P:(t + 1) * P] for h in o],
                                      [h[:, g // QG, :] for h in wo])
                mm.then_inc(out_full, 1)

            with pe.Fori(0, passes) as m:
                for b in range(BATCH):
                    half = m * BATCH + b
                    if b == 0:
                        pe.wait_ge(w_ready, m + 1)
                    project_qk(half, b)
                    if b == 0:
                        pe.wait_ge(wo_ready, m + 1)
                    else:
                        for part in range(2):
                            output(half - 1, groups - 1, part)
                    pe.wait_ge(ring_free, half * uses + qk_uses + 2)
                    score(half, 0)
                    project_v(half, b)
                    for i in range(tiles):
                        g, j = i // GT, i % GT
                        if i + 1 < tiles:
                            score(half, i + 1)
                        turn(half, i)
                        if g >= 2 and j % 2:
                            output(half, g - 2, j // 2)
                        if g >= 1:
                            weighted_v(half, g - 1, j)
                    for part in range(GT):
                        if part % 2 == 0:
                            output(half, groups - 2, part // 2)
                        weighted_v(half, groups - 1, part)
                for part in range(2):
                    output(half, groups - 1, part)

        @block.scalar
        def _(act):
            for _ in range(2):
                act.nop().then_inc(exp_done, 1)

            def exp(half, i):
                act.wait_ge(max_ready, half * tiles + i + 1)
                if i >= 2:
                    act.wait_ge(ring_full, half * uses + turn_use(i - 2, 1) + 1)
                if i == 1:
                    act.wait_ge(v_done, (half + 1) * v_uses + 2)
                nc.scalar.activation(prob[:, i % 2, :], scores(i).rearrange("p a b -> p (a b)"), ACT.Exp,
                                     bias=neg_max[:, i % 2:i % 2 + 1],
                                     accum_out=total[:, i:i + 1]).then_inc(exp_done, 1)

            with act.Fori(0, passes) as m:
                for b in range(BATCH):
                    half = m * BATCH + b
                    hi_base = half * (qk_uses + 2 * tiles)
                    for n in range(qk_uses):
                        which, head, c = qk_chunk(n)
                        act.wait_ge(ring_full, half * uses + n + 1)
                        nc.scalar.activation((q, key)[which][0][:, head, c * NB:(c + 1) * NB], ring(n), ACT.Identity,
                                             bias=bias_qk[:, which * HP + head:which * HP + head + 1]).then_inc(ring_hi, 1)
                    exp(half, 0)
                    for n in range(v_uses):
                        act.wait_ge(ring_free, half * uses + qk_uses + n + 3)
                        to = slice(n * GT // HP, (n + 1) * GT // HP)
                        nc.scalar.activation(v[0][:, to, :].rearrange("p t d -> p (t d)"), v_whole[:, n % 2, :],
                                             ACT.Copy).then_inc(v_hi_done, 1)
                    for i in range(tiles):
                        g, j = i // GT, i % GT
                        for half_tile in range(2):
                            use = turn_use(i, half_tile)
                            act.wait_ge(ring_full, half * uses + use + 1)
                            nc.scalar.activation(
                                probT[0][:, g % 2, half_tile * GT:(half_tile + 1) * GT, j * P:(j + 1) * P],
                                ring(use).rearrange("p (t n) -> p t n", n=P), ACT.Copy).then_inc(ring_hi, 1)
                        if i + 1 < tiles:
                            exp(half, i + 1)
                        if g >= 1 and j == GT - 1:
                            act.wait_ge(o_full, half * groups + g)
                            nc.scalar.activation(o[0][:], o_bank, ACT.Copy).then_inc(o_hi_done, 1)
                    act.wait_ge(o_full, (half + 1) * groups)
                    nc.scalar.activation(o[0][:], o_bank, ACT.Copy).then_inc(o_hi_done, 1)

        @block.vector
        def _(dve):
            for _ in range(2):
                dve.nop().then_inc(ring_free, 1)
            dve.nop().then_inc(o_done, 1)
            dve.nop().then_inc(out_done, 1)
            nc.vector.memset(k.acc[:], 0.0).then_inc(own, 1)
            dve.wait_ge(own, 1)

            def row_max(half, i):
                dve.wait_ge(score_full, half * tiles + i + 1)
                nc.vector.tensor_reduce(neg_max[:, i % 2:i % 2 + 1], scores(i), AX.XY, ALU.max,
                                        negate=True).then_inc(max_ready, 1)

            def o_lo(half, g):
                dve.wait_ge(o_hi_done, half * groups + g + 1)
                nc.vector.tensor_tensor(o[1][:], o_bank, f32(o[0][:]), ALU.subtract).then_inc(o_done, 1)

            def add_up(half, g, part):
                use = (half * groups + g) * 2 + part
                if part == 0:
                    nc.vector.reciprocal(over_total[:, g * GT:(g + 1) * GT], total[:, g * GT:(g + 1) * GT]).then_inc(own, 1)
                    dve.wait_ge(own, half * groups + g + 2)
                dve.wait_ge(out_full, use + 1)
                for j in range(2):
                    t = part * 2 + j
                    to = k.acc[:, (b_of[0] * ST) + g % QG * GT + t, :]
                    add = nc.vector.scalar_tensor_tensor(out=to, in0=out_bank[:, j * C:(j + 1) * C],
                                                         scalar=over_total[:, g * GT + t:g * GT + t + 1], in1=to,
                                                         op0=ALU.mult, op1=ALU.add)
                add.then_inc(out_done, 1)

            b_of = [0]
            with dve.Fori(0, passes) as m:
                for b in range(BATCH):
                    half = m * BATCH + b
                    hi_base = half * (qk_uses + 2 * tiles)
                    for n in range(qk_uses):
                        which, head, c = qk_chunk(n)
                        dve.wait_ge(ring_hi, hi_base + n + 1)
                        to = [h[:, head, c * NB:(c + 1) * NB] for h in (q, key)[which]]
                        nc.vector.scalar_tensor_tensor(
                            out=to[1], in0=ring(n), scalar=bias_qk[:, which * HP + head:which * HP + head + 1],
                            in1=f32(to[0]), op0=ALU.add, op1=ALU.subtract).then_inc(ring_free, 1)
                    if b:
                        b_of[0] = b - 1
                        for part in range(2):
                            add_up(half - 1, groups - 1, part)
                    b_of[0] = b
                    row_max(half, 0)
                    for n in range(v_uses):
                        dve.wait_ge(ring_full, half * uses + qk_uses + n + 1)
                        dve.wait_ge(v_done, half * v_uses + n + 1)
                        nc.vector.tensor_tensor(
                            v_whole[:, n % 2, :].rearrange("p (t d) -> p t d", t=2),
                            ring(n).rearrange("p (t d) -> p t d", t=2),
                            bias_v[:].unsqueeze(1).broadcast_to([P, 2, HP * D0]), ALU.add).then_inc(ring_free, 1)
                    for i in range(tiles):
                        g, j = i // GT, i % GT
                        if i + 1 < tiles:
                            row_max(half, i + 1)
                        for half_tile in range(2):
                            use = turn_use(i, half_tile)
                            dve.wait_ge(ring_hi, hi_base + qk_uses + 2 * i + half_tile + 1)
                            to = [h[:, g % 2, half_tile * GT:(half_tile + 1) * GT, j * P:(j + 1) * P] for h in probT]
                            nc.vector.tensor_tensor(to[1], ring(use).rearrange("p (t n) -> p t n", n=P), f32(to[0]),
                                                    ALU.subtract).then_inc(ring_free, 1)
                        if g >= 2 and j % 2:
                            add_up(half, g - 2, j // 2)
                        if g >= 1 and j == GT - 1:
                            o_lo(half, g - 1)
                    for part in range(2):
                        add_up(half, groups - 2, part)
                    o_lo(half, groups - 1)
                for part in range(2):
                    add_up(half, groups - 1, part)


def f32(ap):
    return ap.bitcast(F32)


def mlp_stage(nc, k, name, w_dram, n_chunks, *, hidden_scales=None, weigh=None):
    cols_up, cols_down = KC * IM, 2 * KC * IM
    cols = cols_down + C
    per_chunk = TOK // NB
    pair = 2 * per_chunk
    with ExitStack() as ctx:
        st = Stage(nc, ctx, name)
        staged = st.sb("staged", [P, 2, cols])
        w_hi, w_lo = st.halves("w", [P, 2, cols])
        gate_act = st.sb("gate_act", [P, 2, NB])
        hidden = st.sb("hidden", [P, 2, NB])
        hid_hi, hid_lo = st.halves("hid", [P, 2, NB])
        scales = st.sb("scales", [P, 2, n_chunks])
        gate_scale = st.sb("gate_scale", [P, 2])
        landed = [st.sem(f"landed{n}") for n in range(2)]
        scales_in, staged_free, hi_split, w_ready = (st.sem(n) for n in ("scales_in", "staged_free", "hi_split", "w_ready"))
        gate_full, up_full, silu_done, prod_done = (st.sem(n) for n in ("gate_full", "up_full", "silu_done", "prod_done"))
        hi_done, lo_done, down_full, acc_done = (st.sem(n) for n in ("hi_done", "lo_done", "down_full", "acc_done"))
        cleared, scale_set = st.sem("cleared"), st.sem("scale_set")
        block = ctx.enter_context(nc.Block())
        gate_bank = lambda q: k.psum[:, q % 2, :]
        up_bank = lambda q: k.psum[:, 2 + q % 2, :]
        down_tile = lambda q, j: k.psum[:, 4 + 2 * (q % 2) + j // 2, j % 2 * C:(j % 2 + 1) * C]

        @block.sync
        def _(sp):
            if hidden_scales is not None:
                sp.dma_start(scales[:], hidden_scales.rearrange("s p n -> p s n")).then_inc(scales_in, 16)
            with sp.Fori(0, n_chunks // 2) as m:
                for e in range(2):
                    sp.wait_ge(staged_free, m * 2 + e + 1)
                    sp.dma_start(staged[:, e, :], w_dram[bass.ds(m * 2 + e, 1)].squeeze(0)).then_inc(landed[e], 16)

        @block.tensor
        def _(pe):
            def gate_up(m, s, e_next=False):
                e, c = s // per_chunk % 2, s % per_chunk
                step = m * pair + s
                tokens = slice(c * NB, (c + 1) * NB)
                if c == 0:
                    pe.wait_ge(w_ready, m * 2 + s // per_chunk + 1)
                x = lambda kt: [h[:, kt, tokens] for h in k.xT]
                pe.wait_ge(silu_done, step + 1)
                project(nc, gate_bank(s), lambda kt: [w[:, e, kt * IM:(kt + 1) * IM] for w in (w_hi, w_lo)],
                        x).then_inc(gate_full, 1)
                pe.wait_ge(prod_done, step + 1)
                project(nc, up_bank(s), lambda kt: [w[:, e, cols_up + kt * IM:cols_up + (kt + 1) * IM]
                                                    for w in (w_hi, w_lo)], x).then_inc(up_full, 1)

            def down(m, s):
                e = s // per_chunk
                step = m * pair + s
                pe.wait_ge(lo_done, step + 3)
                for j in range(GT):
                    if j % 2 == 0:
                        pe.wait_ge(acc_done, step * 2 + j // 2 + 1)
                    ins = three_passes(nc, down_tile(s, j),
                                       [h[:, s % 2, j * P:(j + 1) * P] for h in (hid_hi, hid_lo)],
                                       [w[:, e, cols_down:cols] for w in (w_hi, w_lo)])
                    if j % 2:
                        ins.then_inc(down_full, 1)

            gate_up(0, 0)
            with pe.Fori(0, n_chunks // 2 - 1) as m:
                for s in range(pair):
                    gate_up(m, s + 1)
                    down(m, s)
            m = n_chunks // 2 - 1
            for s in range(pair):
                if s + 1 < pair:
                    gate_up(m, s + 1)
                down(m, s)

        @block.scalar
        def _(act):
            for _ in range(2):
                act.nop().then_inc(silu_done, 1)
            if hidden_scales is not None:
                act.wait_ge(scales_in, 16)
            with act.Fori(0, n_chunks // 2) as m:
                for s in range(pair):
                    step = m * pair + s
                    e = s // per_chunk
                    if hidden_scales is not None and s % per_chunk == 0:
                        nc.scalar.activation(gate_scale[:, e:e + 1], scales[:, 0, bass.ds(m * 2 + e, 1)],
                                             ACT.Copy).then_inc(scale_set, 1)
                        act.wait_ge(scale_set, m * 2 + e + 1)
                    act.wait_ge(gate_full, step + 1)
                    act.wait_ge(prod_done, step + 1)
                    by = 1.0 if hidden_scales is None else gate_scale[:, e:e + 1]
                    nc.scalar.activation(gate_act[:, s % 2, :], gate_bank(s), ACT.Silu, scale=by).then_inc(silu_done, 1)
                    act.wait_ge(prod_done, step + 3)
                    nc.scalar.activation(hid_hi[:, s % 2, :], hidden[:, s % 2, :], ACT.Copy).then_inc(hi_done, 1)

        @block.gpsimd
        def _(pool):
            for _ in range(2):
                pool.nop().then_inc(lo_done, 1)
            with pool.Fori(0, n_chunks // 2) as m:
                for s in range(pair):
                    pool.wait_ge(hi_done, m * pair + s + 1)
                    nc.gpsimd.tensor_tensor(hid_lo[:, s % 2, :], hidden[:, s % 2, :],
                                            hid_hi[:, s % 2, :].bitcast(F32), ALU.subtract).then_inc(lo_done, 1)

        @block.vector
        def _(dve):
            def split_weights(m, e):
                dve.wait_ge(landed[e % 2], m * 16 + (16 if e < 2 else 32))
                nc.vector.tensor_copy(w_hi[:, e % 2, :], staged[:, e % 2, :]).then_inc(hi_split, 1)
                dve.wait_ge(hi_split, m * 2 + e + 1)
                nc.vector.tensor_tensor(w_lo[:, e % 2, :], staged[:, e % 2, :], w_hi[:, e % 2, :].bitcast(F32),
                                        ALU.subtract).then_inc(w_ready, 1)
                dve.wait_ge(w_ready, m * 2 + e + 1)
                dve.nop().then_inc(staged_free, 1)

            def product(m, s):
                step = m * pair + s
                dve.wait_ge(silu_done, step + 3)
                dve.wait_ge(up_full, step + 1)
                dve.wait_ge(lo_done, step + 1)
                h, g = hidden[:, s % 2, :], gate_act[:, s % 2, :]
                if hidden_scales is None:
                    ins = nc.vector.tensor_tensor(h, up_bank(s), g, ALU.mult)
                else:
                    by = scales[:, 1, bass.ds(m * 2 + s // per_chunk, 1)]
                    ins = nc.vector.scalar_tensor_tensor(out=h, in0=up_bank(s), scalar=by, in1=g,
                                                         op0=ALU.mult, op1=ALU.mult)
                ins.then_inc(prod_done, 1)

            def add_up(m, s):
                step = m * pair + s
                for j in range(GT):
                    if j % 2 == 0:
                        dve.wait_ge(down_full, step * 2 + j // 2 + 1)
                    t = s % per_chunk * GT + j
                    by = 1.0 if weigh is None else weigh[:, bass.ds((m * 2 + s // per_chunk) * TT + t, 1)]
                    ins = nc.vector.scalar_tensor_tensor(out=k.acc[:, t, :], in0=down_tile(s, j), scalar=by,
                                                         in1=k.acc[:, t, :], op0=ALU.mult, op1=ALU.add)
                    if j % 2:
                        ins.then_inc(acc_done, 1)

            for _ in range(2):
                dve.nop().then_inc(prod_done, 1)
                dve.nop().then_inc(staged_free, 1)
            for _ in range(4):
                dve.nop().then_inc(acc_done, 1)
            nc.vector.memset(k.acc[:], 0.0).then_inc(cleared, 1)
            dve.wait_ge(cleared, 1)
            if hidden_scales is not None:
                dve.wait_ge(scales_in, 16)
            split_weights(0, 0)
            product(0, 0)
            with dve.Fori(0, n_chunks // 2 - 1) as m:
                for s in range(pair):
                    if s % per_chunk == 1:
                        split_weights(m, s // per_chunk + 1)
                    product(m, s + 1)
                    add_up(m, s)
            m = n_chunks // 2 - 1
            for s in range(pair):
                if s == 1:
                    split_weights(m, 1)
                if s + 1 < pair:
                    product(m, s + 1)
                add_up(m, s)


def route_stage(nc, k, name, router_dram, weigh):
    with ExitStack() as ctx:
        st = Stage(nc, ctx, name)
        router = st.sb("router", [P, KC, N_EXPERT])
        r_hi, r_lo = st.halves("r", [P, KC, N_EXPERT])
        score = st.sb("score", [P, TT, N_EXPERT])
        best = st.sb("best", [P, TT, N_TOP])
        rest = st.sb("rest", [P, TT, N_EXPERT])
        total = st.sb("total", [P, TT])
        factor = st.sb("factor", [P, TT])
        landed, own, r_ready, logits_full, score_ready = (
            st.sem(n) for n in ("landed", "own", "r_ready", "logits_full", "score_ready"))
        block = ctx.enter_context(nc.Block())

        @block.sync
        def _(sp):
            sp.dma_start(router[:], router_dram).then_inc(landed, 16)

        @block.tensor
        def _(pe):
            pe.wait_ge(r_ready, 1)
            for t in range(TT):
                ins = project(nc, k.psum[:, 0, t * N_EXPERT:(t + 1) * N_EXPERT],
                              lambda kt: [h[:, kt, t * P:(t + 1) * P] for h in k.xT],
                              lambda kt: [r[:, kt, :] for r in (r_hi, r_lo)])
            ins.then_inc(logits_full, 1)

        @block.scalar
        def _(act):
            act.wait_ge(logits_full, 1)
            nc.scalar.activation(score[:].rearrange("p t e -> p (t e)"), k.psum[:, 0, 0:TT * N_EXPERT],
                                 ACT.Sigmoid).then_inc(score_ready, 1)

        @block.vector
        def _(dve):
            link = Count(own)
            dve.wait_ge(landed, 16)
            link.step(dve, nc.vector.tensor_copy(r_hi[:], router[:]))
            nc.vector.tensor_tensor(r_lo[:], router[:], r_hi[:].bitcast(F32), ALU.subtract).then_inc(r_ready, 1)
            nc.vector.memset(weigh[:, N_EXPERT * TT:], 1.0)
            dve.wait_ge(score_ready, 1)
            for t in range(TT):
                link.inc(nc.vector.max(best[:, t, :], score[:, t, :]))
            link.wait(dve)
            for t in range(TT):
                link.inc(nc.vector.match_replace(rest[:, t, :], best[:, t, :], score[:, t, :], -1.0))
            link.step(dve, nc.vector.tensor_reduce(total[:], best[:], AX.X, ALU.add))
            link.step(dve, nc.vector.tensor_scalar(total[:], total[:], 1e-6, None, ALU.add))
            link.step(dve, nc.vector.reciprocal(factor[:], total[:]))
            link.step(dve, nc.vector.tensor_scalar(factor[:], factor[:], ROUTE_SCALE, None, ALU.mult))
            link.step(dve, nc.vector.tensor_scalar(rest[:], rest[:], 0.0, None, ALU.is_lt))
            link.step(dve, nc.vector.tensor_tensor(rest[:], rest[:], score[:], ALU.mult))
            nc.vector.tensor_tensor(weigh[:, 0:N_EXPERT * TT].rearrange("p (e t) -> p t e", t=TT), rest[:],
                                    factor[:].unsqueeze(2).broadcast_to([P, TT, N_EXPERT]), ALU.mult)


def projection_stage(nc, k, name, w_dram):
    with ExitStack() as ctx:
        st = Stage(nc, ctx, name)
        w = st.sb("w", [P, KC, C])
        w_hi, w_lo = st.halves("w", [P, KC, C])
        landed, own, w_ready, full, copied = (st.sem(n) for n in ("landed", "own", "w_ready", "full", "copied"))
        block = ctx.enter_context(nc.Block())

        @block.sync
        def _(sp):
            sp.dma_start(w[:], w_dram.rearrange("(k p) n -> p k n", p=P)).then_inc(landed, 16)

        @block.tensor
        def _(pe):
            pe.wait_ge(w_ready, 1)
            for t in range(TT):
                if t % 2 == 0 and t >= 16:
                    pe.wait_ge(copied, t // 2 - 7)
                ins = project(nc, k.psum[:, t // 2 % 8, t % 2 * C:(t % 2 + 1) * C],
                              lambda kt: [h[:, kt, t * P:(t + 1) * P] for h in k.xT],
                              lambda kt: [p[:, kt, :] for p in (w_hi, w_lo)])
                if t % 2:
                    ins.then_inc(full, 1)

        @block.vector
        def _(dve):
            dve.wait_ge(landed, 16)
            nc.vector.tensor_copy(w_hi[:], w[:]).then_inc(own, 1)
            dve.wait_ge(own, 1)
            nc.vector.tensor_tensor(w_lo[:], w[:], w_hi[:].bitcast(F32), ALU.subtract).then_inc(w_ready, 1)
            for b in range(TT // 2):
                dve.wait_ge(full, b + 1)
                nc.vector.tensor_copy(k.acc[:, 2 * b:2 * b + 2, :].rearrange("p t c -> p (t c)"),
                                      k.psum[:, b % 8, :]).then_inc(copied, 1)


HG = P // D1P
V_PARTS = 3
W1 = KC * (2 * P + HG * D1)


def attention1_stage(nc, k, name, ins):
    scale = float(D1) ** -0.5
    units = HG * BATCH
    tiles = units * ST
    groups = tiles // GT
    passes = H1 // HG
    cols_k, cols_v = KC * P, 2 * KC * P
    qk_chunks = TOK // NB
    v_tiles = NB // (HG * D1)
    v_uses = TT // v_tiles
    first_turn = 2 * qk_chunks + v_uses
    turns = lambda t: -(-(t + 1) // GT)
    unit_turns = sum(turns(t) for t in range(ST))
    uses = first_turn + units * unit_turns
    hi_uses = 2 * qk_chunks + units * unit_turns

    def turn_use(i, half_tile):
        return first_turn + i // ST * unit_turns + sum(turns(t) for t in range(i % ST)) + half_tile

    with ExitStack() as ctx:
        st = Stage(nc, ctx, name)
        staged = st.sb("staged", [P, W1])
        scale_row = st.sb("scale_row", [P, 1])
        one = st.sb("one", [P, 1])
        bias_in = st.sb("bias_in", [P, 2])
        bias_qk = st.sb("bias_qk", [P, 2])
        bias_v_in = st.sb("bias_v_in", [P, HG * D1])
        bias_v = st.sb("bias_v", [P, HG * D1])
        masked = st.sb("masked", [P, P])
        gather = st.sb("gather", [V_PARTS * D1, D1])
        w = st.halves("w", [P, W1])
        q = st.halves("q", [P, TOK])
        key = st.halves("key", [P, TOK])
        v_whole = st.sb("v_whole", [P, v_uses, NB])
        v = st.sb("v", [P, TT, HG, V_PARTS * D1], BF16)
        prob = st.sb("prob", [P, 2, SEQ])
        probT = [st.sb(f"probT_{h}", [P, 2, ST, NB], F16) for h in ("hi", "lo")]
        o = st.sb("o", [V_PARTS * D1, 2, NB])
        neg_max = st.sb("neg_max", [P, 2])
        total = st.sb("total", [P, tiles])
        over_total = st.sb("over_total", [P, tiles])
        landed, consts, staged_free, w_ready, split = (
            st.sem(n) for n in ("landed", "consts", "staged_free", "w_ready", "split"))
        ring_full, ring_hi, ring_free = (st.sem(n) for n in ("ring_full", "ring_hi", "ring_free"))
        v_part, v_rest = st.sem("v_part"), st.sem("v_rest")
        score_full, mask_done, max_ready, exp_done = (st.sem(n) for n in ("score_full", "mask_done", "max_ready", "exp_done"))
        scale_set = st.sem("scale_set")
        o_full, o_done, y_full, y_done, own = (st.sem(n) for n in ("o_full", "o_done", "y_full", "y_done", "own"))
        block = ctx.enter_context(nc.Block())

        ring = lambda n: k.psum[:, 4 + n % 2, :]
        scores = lambda i: k.psum[:, i % 2 * 2:i % 2 * 2 + 2, :].rearrange("p a b -> p (a b)")
        o_bank, y_bank = k.psum[0:V_PARTS * D1, 6, :], k.psum[:, 7, 0:GT * D1]

        def place(i):
            return i // (BATCH * ST), i // ST % BATCH, i % ST

        @block.sync
        def _(sp):
            sp.dma_start(masked[:], ins["masked"]).then_inc(consts, 16)
            sp.dma_start(gather[:], ins["gather"]).then_inc(consts, 16)
            with sp.Fori(0, passes) as m:
                sp.wait_ge(staged_free, m + 1)
                this = bass.ds(m, 1)
                sp.dma_start(staged[:], ins["w_attn"][this].squeeze(0)).then_inc(landed, 16)
                sp.dma_start(bias_in[:], ins["b_qk"][this].squeeze(0)).then_inc(landed, 16)
                sp.dma_start(bias_v_in[:], ins["b_v"][bass.ds(m * HG * D1, HG * D1)].partition_broadcast(P)).then_inc(landed, 16)

        @block.gpsimd
        def _(pool):
            pool.nop().then_inc(staged_free, 1)
            nc.gpsimd.memset(scale_row[:], scale).then_inc(scale_set, 1)
            nc.gpsimd.memset(one[:], 1.0).then_inc(scale_set, 1)
            pool.wait_ge(scale_set, 2)

            def split_weights(m, first=False):
                pool.wait_ge(landed, (m + 1) * 48)
                if not first:
                    pool.wait_ge(ring_full, (m - 1) * uses + first_turn)
                n = m * 3
                nc.gpsimd.tensor_tensor(staged[:, 0:cols_k], staged[:, 0:cols_k], scale_row[:].broadcast_to([P, cols_k]), ALU.mult).then_inc(split, 1)
                nc.gpsimd.tensor_scalar(bias_qk[:, 0:1], bias_in[:, 0:1], scale, 1.0, ALU.mult, ALU.mult)
                nc.gpsimd.tensor_scalar(bias_qk[:, 1:2], bias_in[:, 1:2], 1.0, 1.0, ALU.mult, ALU.mult)
                nc.gpsimd.tensor_scalar(bias_v[:], bias_v_in[:], 1.0, 1.0, ALU.mult, ALU.mult)
                pool.wait_ge(split, n + 1)
                nc.gpsimd.tensor_tensor(w[0][:], staged[:], one[:].broadcast_to([P, W1]), ALU.mult).then_inc(split, 1)
                pool.wait_ge(split, n + 2)
                nc.gpsimd.tensor_tensor(w[1][:], staged[:], f32(w[0][:]), ALU.subtract).then_inc(w_ready, 1)
                pool.wait_ge(w_ready, m + 1)
                pool.nop().then_inc(staged_free, 1)
                pool.nop().then_inc(split, 1)

            def split_v(m):
                for n in range(v_uses):
                    at = (m * v_uses + n) * 2
                    whole = v_whole[:, n, :].rearrange("p (t h d) -> p t h d", h=HG, d=D1)
                    part = lambda r: v[:, n * v_tiles:(n + 1) * v_tiles, :, r * D1:(r + 1) * D1]
                    pool.wait_ge(v_part, at + 1)
                    nc.gpsimd.tensor_tensor(whole, whole, part(0), ALU.subtract).then_inc(v_rest, 1)
                    pool.wait_ge(v_part, at + 2)
                    nc.gpsimd.tensor_tensor(part(2), whole, part(1), ALU.subtract).then_inc(v_rest, 1)

            split_weights(0, first=True)
            with pool.Fori(0, passes - 1) as m:
                split_v(m)
                split_weights(m + 1)
            split_v(passes - 1)

        @block.tensor
        def _(pe):
            def take_ring(m, n):
                pe.wait_ge(ring_free, m * uses + n + 1)

            def score(m, i):
                head, b, t = place(i)
                rows = slice(head * D1P, (head + 1) * D1P)
                pe.wait_ge(exp_done, m * tiles + i + 1)
                tokens = slice(b * SEQ + t * P, b * SEQ + (t + 1) * P)
                for c in range(turns(t)):
                    end = min((c + 1) * NB, (t + 1) * P)
                    mm = three_passes(nc, scores(i)[:, c * NB:end], [h[rows, tokens] for h in q],
                                      [h[rows, b * SEQ + c * NB:b * SEQ + end] for h in key])
                mm.then_inc(score_full, 1)

            def turn(m, i):
                t = i % ST
                pe.wait_ge(exp_done, m * tiles + i + 3)
                for half_tile in range(turns(t)):
                    use = turn_use(i, half_tile)
                    take_ring(m, use)
                    for kt in range(half_tile * GT, min((half_tile + 1) * GT, t + 1)):
                        mm = nc.tensor.transpose(ring(use)[:, kt % GT * P:(kt % GT + 1) * P],
                                                 prob[:, i % 2, kt * P:(kt + 1) * P], k.ident[:])
                    mm.then_inc(ring_full, 1)

            def weighted_v(m, g, part):
                head, b, t = place(g * GT)
                if part == 0:
                    pe.wait_ge(ring_free, m * uses + turn_use((g + 1) * GT - 1, turns(t + GT - 1) - 1) + 3)
                    pe.wait_ge(o_done, m * groups + g + 1)
                    if g == 0:
                        pe.wait_ge(v_rest, (m + 1) * v_uses * 2)
                keys = t + GT
                n = keys // GT
                for kt in range(part * n, (part + 1) * n):
                    q0 = max(0, kt - t) * P
                    for r in range(2):
                        mm = nc.tensor.matmul(o_bank[:, q0:], v[:, b * ST + kt, head, :], probT[r][:, g % 2, kt, q0:],
                                              start=kt == 0 and r == 0, stop=kt == keys - 1 and r == 1)
                if part == GT - 1:
                    mm.then_inc(o_full, 1)

            def turn_back(m, g):
                pe.wait_ge(o_done, m * groups + g + 2)
                pe.wait_ge(y_done, m * groups + g + 1)
                for j in range(GT):
                    mm = nc.tensor.matmul(y_bank[:, j * D1:(j + 1) * D1], o[:, g % 2, j * P:(j + 1) * P], gather[:],
                                          start=True, stop=True)
                mm.then_inc(y_full, 1)

            pe.wait_ge(consts, 32)
            with pe.Fori(0, passes) as m:
                pe.wait_ge(w_ready, m + 1)
                for n in range(2 * qk_chunks):
                    which, c = n // qk_chunks, n % qk_chunks
                    take_ring(m, n)
                    project(nc, ring(n), lambda kt: [h[:, which * cols_k + kt * P:which * cols_k + (kt + 1) * P] for h in w],
                            lambda kt: [h[:, kt, c * NB:(c + 1) * NB] for h in k.xT]).then_inc(ring_full, 1)
                pe.wait_ge(ring_free, m * uses + 2 * qk_chunks + 2)
                score(m, 0)
                for n in range(v_uses):
                    take_ring(m, 2 * qk_chunks + n)
                    for j in range(v_tiles):
                        t = n * v_tiles + j
                        mm = project(nc, ring(n)[:, j * HG * D1:(j + 1) * HG * D1],
                                     lambda kt: [h[:, kt, t * P:(t + 1) * P] for h in k.xT],
                                     lambda kt: [h[:, cols_v + kt * HG * D1:cols_v + (kt + 1) * HG * D1] for h in w])
                    mm.then_inc(ring_full, 1)
                for i in range(tiles):
                    g, j = i // GT, i % GT
                    if i + 1 < tiles:
                        score(m, i + 1)
                    turn(m, i)
                    if g >= 2 and j == 1:
                        turn_back(m, g - 2)
                    if g >= 1:
                        weighted_v(m, g - 1, j)
                turn_back(m, groups - 2)
                for part in range(GT):
                    weighted_v(m, groups - 1, part)
                turn_back(m, groups - 1)

        @block.scalar
        def _(act):
            for _ in range(2):
                act.nop().then_inc(exp_done, 1)
            act.nop().then_inc(o_done, 1)

            def exp(m, i):
                keys = (i % ST + 1) * P
                act.wait_ge(max_ready, m * tiles + i + 1)
                if i >= 2:
                    act.wait_ge(ring_full, m * uses + turn_use(i - 2, turns((i - 2) % ST) - 1) + 1)
                nc.scalar.activation(prob[:, i % 2, 0:keys], scores(i)[:, 0:keys], ACT.Exp, bias=neg_max[:, i % 2:i % 2 + 1],
                                     accum_out=total[:, i:i + 1]).then_inc(exp_done, 1)

            def copy_o(m, g):
                act.wait_ge(o_full, m * groups + g + 1)
                nc.scalar.activation(o[:, g % 2, :], o_bank, ACT.Copy).then_inc(o_done, 1)

            with act.Fori(0, passes) as m:
                for n in range(2 * qk_chunks):
                    which, c = n // qk_chunks, n % qk_chunks
                    act.wait_ge(ring_full, m * uses + n + 1)
                    nc.scalar.activation((q, key)[which][0][:, c * NB:(c + 1) * NB], ring(n), ACT.Identity,
                                         bias=bias_qk[:, which:which + 1]).then_inc(ring_hi, 1)
                exp(m, 0)
                for n in range(v_uses):
                    part = lambda r: v[:, n * v_tiles:(n + 1) * v_tiles, :, r * D1:(r + 1) * D1]
                    whole = v_whole[:, n, :].rearrange("p (t h d) -> p t h d", h=HG, d=D1)
                    act.wait_ge(ring_free, m * uses + 2 * qk_chunks + n + 3)
                    nc.scalar.activation(part(0), whole, ACT.Copy).then_inc(v_part, 1)
                    act.wait_ge(v_rest, (m * v_uses + n) * 2 + 1)
                    nc.scalar.activation(part(1), whole, ACT.Copy).then_inc(v_part, 1)
                for i in range(tiles):
                    g, j, t = i // GT, i % GT, i % ST
                    for half_tile in range(turns(t)):
                        use = turn_use(i, half_tile)
                        n = min(GT, t + 1 - half_tile * GT)
                        act.wait_ge(ring_full, m * uses + use + 1)
                        nc.scalar.activation(
                            probT[0][:, g % 2, half_tile * GT:half_tile * GT + n, j * P:(j + 1) * P],
                            ring(use)[:, 0:n * P].rearrange("p (t n) -> p t n", n=P), ACT.Copy).then_inc(ring_hi, 1)
                    if i + 1 < tiles:
                        exp(m, i + 1)
                    if g >= 1 and j == GT - 1:
                        copy_o(m, g - 1)
                copy_o(m, groups - 1)

        @block.vector
        def _(dve):
            for _ in range(2):
                dve.nop().then_inc(ring_free, 1)
            dve.nop().then_inc(y_done, 1)

            def row_max(m, i):
                t = i % ST
                at = m * tiles + i + 1
                dve.wait_ge(score_full, at)
                own_keys = scores(i)[:, t * P:(t + 1) * P]
                nc.vector.tensor_tensor(own_keys, own_keys, masked[:], ALU.add).then_inc(mask_done, 1)
                dve.wait_ge(mask_done, at)
                nc.vector.tensor_reduce(neg_max[:, i % 2:i % 2 + 1], scores(i)[:, 0:(t + 1) * P], AX.X, ALU.max,
                                        negate=True).then_inc(max_ready, 1)

            def rows(m, g):
                head, b, t = place(g * GT)
                part = slice(g * GT, (g + 1) * GT)
                nc.vector.reciprocal(over_total[:, part], total[:, part]).then_inc(own, 1)
                dve.wait_ge(own, m * groups + g + 1)
                dve.wait_ge(y_full, m * groups + g + 1)
                nc.vector.tensor_tensor(
                    k.acc[:, b * ST + t:b * ST + t + GT, bass.ds(m * HG * D1 + head * D1, D1)],
                    y_bank.rearrange("p (t d) -> p t d", d=D1),
                    over_total[:, part].unsqueeze(2).broadcast_to([P, GT, D1]), ALU.mult).then_inc(y_done, 1)

            dve.wait_ge(consts, 32)
            with dve.Fori(0, passes) as m:
                for n in range(2 * qk_chunks):
                    which, c = n // qk_chunks, n % qk_chunks
                    dve.wait_ge(ring_hi, m * hi_uses + n + 1)
                    to = [h[:, c * NB:(c + 1) * NB] for h in (q, key)[which]]
                    nc.vector.scalar_tensor_tensor(out=to[1], in0=ring(n), scalar=bias_qk[:, which:which + 1],
                                                   in1=f32(to[0]), op0=ALU.add, op1=ALU.subtract).then_inc(ring_free, 1)
                row_max(m, 0)
                for n in range(v_uses):
                    dve.wait_ge(ring_full, m * uses + 2 * qk_chunks + n + 1)
                    nc.vector.tensor_tensor(
                        v_whole[:, n, :].rearrange("p (t d) -> p t d", t=v_tiles),
                        ring(n).rearrange("p (t d) -> p t d", t=v_tiles),
                        bias_v[:].unsqueeze(1).broadcast_to([P, v_tiles, HG * D1]), ALU.add).then_inc(ring_free, 1)
                for i in range(tiles):
                    g, j, t = i // GT, i % GT, i % ST
                    if i + 1 < tiles:
                        row_max(m, i + 1)
                    for half_tile in range(turns(t)):
                        use = turn_use(i, half_tile)
                        n = min(GT, t + 1 - half_tile * GT)
                        dve.wait_ge(ring_hi, m * hi_uses + use - v_uses + 1)
                        to = [h[:, g % 2, half_tile * GT:half_tile * GT + n, j * P:(j + 1) * P] for h in probT]
                        nc.vector.tensor_tensor(to[1], ring(use)[:, 0:n * P].rearrange("p (t n) -> p t n", n=P), to[0],
                                                ALU.subtract).then_inc(ring_free, 1)
                    if g >= 2 and j == 1:
                        rows(m, g - 2)
                rows(m, groups - 2)
                rows(m, groups - 1)


def build(nc, ins, out):
    with ExitStack() as ctx:
        k = Core()
        def sb(n, s, d=F32):
            return ctx.enter_context(nc.sbuf_tensor(n, s, d))
        k.x_dram = ins["x"]
        k.acc = sb("acc_sb", [P, TT, C])
        k.xT = [sb(f"xT_{h}", [P, KC, TOK], F32R) for h in ("hi", "lo")]
        k.ident = sb("ident_sb", [P, P])
        k.psum = ctx.enter_context(nc.psum_tensor("psum", [P, 8, NB], F32))
        consts = ctx.enter_context(nc.semaphore("consts"))
        with nc.Block() as block:
            @block.sync
            def _(sp):
                sp.dma_start(k.ident[:], ins["ident"]).then_inc(consts, 16)
                sp.wait_ge(consts, 16)
        with nc.sbuf_tensor("x_first", [P, TT, C], F32) as k.x:
            norm_stage(nc, k, "norm0", sublayer=False, load=True)
        attention0_stage(nc, k, "attn0", ins)
        k.x = sb("x_sb", [P, TT, C])
        weigh = sb("weigh", [P, (N_EXPERT + N_SHARED) * TT])
        norm_stage(nc, k, "norm1", load=True, post=(ins["bo"], ALU.add))
        mlp_stage(nc, k, "mlp0", ins["ffn0_w"], N_FFN0, hidden_scales=ins["ffn0_scales"])
        norm_stage(nc, k, "norm2", post=(ins["down_s"], ALU.mult))
        attention1_stage(nc, k, "attn1", ins)
        norm_stage(nc, k, "turn", plain=True)
        projection_stage(nc, k, "proj", ins["w_proj"])
        norm_stage(nc, k, "norm3", post=(ins["b_proj"], ALU.add))
        route_stage(nc, k, "route", ins["router"], weigh)
        mlp_stage(nc, k, "moe", ins["moe_w"], N_EXPERT + N_SHARED, weigh=weigh)
        norm_stage(nc, k, "norm4", following=False, out=out)


def kernel(**inputs):
    import numpy as np
    import concourse.bacc as bacc
    from concourse.bass_utils import run_bass_kernel_spmd

    given = {n: np.asarray(a) for n, a in inputs.items()}
    l0 = {n[len("L0_attn_"):]: a for n, a in given.items() if n.startswith("L0_attn_")}

    def chunks(gate, up, down):
        cut = [a.reshape(KC, P, -1, IM).transpose(2, 1, 0, 3).reshape(-1, P, KC * IM) for a in (gate, up)]
        return np.concatenate([*cut, down.reshape(-1, IM, C)], axis=2)

    def pad_hidden(a):
        return np.pad(a, [(0, N_FFN0 * IM - INTER0)] + [(0, 0)] * (a.ndim - 1))

    def pad_heads(a):
        heads = np.pad(a.reshape(*a.shape[:-1], H1, D1), [(0, 0)] * a.ndim + [(0, D1P - D1)])
        return heads.reshape(*a.shape[:-1], H1 // HG, P)

    arrays = {"x": l0["x"].reshape(TOK, C)}
    for n in "qkvo":
        arrays[f"w{n}_codes"], arrays[f"w{n}_scales"] = l0[f"w{n}_codes"], l0[f"w{n}_scales"]
    for n in "qk":
        arrays[f"b{n}"] = l0[f"b{n}"].reshape(H0, D0).T
    arrays["bv"], arrays["bo"] = l0["bv"], l0["bo"]
    arrays["ffn0_w"] = chunks(*(pad_hidden(given[f"L0_ffn_{n}_w"]).T for n in ("gate", "up")),
                              pad_hidden(given["L0_ffn_down_w"].T))
    arrays["ffn0_scales"] = np.stack([pad_hidden(given[f"L0_ffn_{n}_s"]).reshape(N_FFN0, IM).T for n in ("gate", "up")])
    arrays["down_s"] = given["L0_ffn_down_s"]

    w_attn, b_attn = given["L1_attn_w_attn"], given["L1_attn_b_attn"]
    by_pass = [pad_heads(w_attn[:, 0:C]), pad_heads(w_attn[:, C:2 * C]), w_attn[:, 2 * C:].reshape(C, H1 // HG, HG * D1)]
    arrays["w_attn"] = np.concatenate([a.reshape(KC, P, H1 // HG, -1).transpose(2, 1, 0, 3).reshape(H1 // HG, P, -1)
                                       for a in by_pass], axis=2)
    arrays["b_qk"] = np.stack([pad_heads(b_attn[0:C]), pad_heads(b_attn[C:2 * C])], axis=-1)
    arrays["b_v"] = b_attn[2 * C:]
    arrays["w_proj"], arrays["b_proj"] = given["L1_attn_w_proj"], given["L1_attn_b_proj"]

    arrays["router"] = given["L1_ffn_gate_w"].T.reshape(KC, P, N_EXPERT).transpose(1, 0, 2)
    side_by_side = lambda a: a.transpose(1, 0, 2).reshape(C, N_EXPERT * IM)
    arrays["moe_w"] = np.concatenate([
        chunks(side_by_side(given["L1_ffn_Wg"]), side_by_side(given["L1_ffn_Wu"]),
               given["L1_ffn_Wd"].reshape(N_EXPERT * IM, C)),
        chunks(given["L1_ffn_sWg"], given["L1_ffn_sWu"], given["L1_ffn_sWd"])])

    arrays["ident"] = np.eye(P, dtype=np.float32)
    arrays["masked"] = np.triu(np.full((P, P), -1e30, np.float32), 1)
    arrays["gather"] = np.tile(np.eye(D1, dtype=np.float32), (V_PARTS, 1))

    nc = bacc.Bacc("TRN2", target_bir_lowering=False, num_devices=1)
    arrays = {f"in_{n}": np.ascontiguousarray(a) for n, a in arrays.items()}
    aps = {n[3:]: nc.dram_tensor(n, a.shape, mybir.dt.from_np(a.dtype), kind="ExternalInput").ap()
           for n, a in arrays.items()}
    out = nc.dram_tensor("out", (TOK, C), F32, kind="ExternalOutput").ap()
    build(nc, aps, out)
    result = run_bass_kernel_spmd(nc, [arrays], core_ids=[0])
    return result.results[0]["out"].reshape(BATCH, SEQ, C)
```

```python
from contextlib import ExitStack

import concourse.bass as bass
from concourse import mybir

F32 = mybir.dt.float32
F32R = mybir.dt.float32r
F16 = mybir.dt.float16
BF16 = mybir.dt.bfloat16
ALU = mybir.AluOpType
ACT = mybir.ActivationFunctionType
AX = mybir.AxisListType

P = 128
BATCH, SEQ, C = 2, 1024, 256
TOK = BATCH * SEQ
TT = TOK // P
KC = C // P
NB = 512
GT = NB // P
EPS = 1e-5

H0, D0 = 16, 128
FP4_BLOCK = 32
H1, D1 = 16, 16
D1P = 32
IM = 128
INTER0 = 704
N_FFN0 = -(-INTER0 // IM)
N_EXPERT, N_TOP, N_SHARED = 16, 8, 2
ROUTE_SCALE = 2.5

PASSES = ((0, 0), (0, 1), (1, 0))


class Count:

    def __init__(self, sem, base=0):
        self.sem, self.base, self.n = sem, base, 0

    def inc(self, ins):
        ins.then_inc(self.sem, 1)
        self.n += 1

    def wait(self, eng):
        eng.wait_ge(self.sem, self.base + self.n)

    def step(self, eng, ins):
        self.inc(ins)
        self.wait(eng)


class Core:
    pass


class Stage:

    def __init__(self, nc, ctx, name):
        self.nc, self.ctx, self.name = nc, ctx, name

    def sb(self, n, shape, dt=F32):
        return self.ctx.enter_context(self.nc.sbuf_tensor(f"{self.name}_{n}", shape, dt))

    def halves(self, n, shape):
        return [self.sb(f"{n}_{h}", shape, F32R) for h in ("hi", "lo")]

    def sem(self, n):
        return self.ctx.enter_context(self.nc.semaphore(f"{self.name}_{n}"))


def three_passes(nc, out, stationary, moving, start=True, stop=True):
    for n, (s, m) in enumerate(PASSES):
        ins = nc.tensor.matmul(out, stationary[s], moving[m], start=start and n == 0,
                               stop=stop and n == len(PASSES) - 1)
    return ins


def project(nc, out, stationary, moving):
    for kt in range(KC):
        ins = three_passes(nc, out, stationary(kt), moving(kt), start=kt == 0, stop=kt == KC - 1)
    return ins


def norm_stage(nc, k, name, *, sublayer=True, load=False, post=None, following=True, plain=False, out=None):
    groups = TT // GT
    with ExitStack() as ctx:
        st = Stage(nc, ctx, name)
        stats = st.sb("stats", [P, TT, 6])
        mean_var = st.sb("mean_var", [P, TT, 2])
        veps = st.sb("veps", [P, TT])
        rstd = st.sb("rstd", [P, TT])
        power = st.sb("power", [P, TT])
        normed = st.sb("normed", [P, TT, C])
        turned = st.sb("turned", [P, 2, KC, NB])
        row = st.sb("row", [P, C])
        loaded, row_loaded = st.sem("loaded"), st.sem("row_loaded")
        own, x_ready, stored = (st.sem(n) for n in ("own", "x_ready", "stored"))
        power_set, var_ready, rstd_ready = (st.sem(n) for n in ("power_set", "var_ready", "rstd_ready"))
        normed_ready, turned_ready = st.sem("normed_ready"), st.sem("turned_ready")
        copied, lo_done = st.sem("copied"), st.sem("lo_done")
        block = ctx.enter_context(nc.Block())
        rows_out = k.acc if plain else normed

        @block.sync
        def _(sp):
            if post:
                sp.dma_start(row[:], post[0].partition_broadcast(P)).then_inc(row_loaded, 16)
            if load:
                x_rows = k.x_dram.rearrange("(g t p) c -> g p t c", t=GT, p=P)
                for g in range(groups):
                    sp.dma_start(k.x[:, g * GT:(g + 1) * GT, :], x_rows[g]).then_inc(loaded, 16)
            if not following:
                out_rows = out.rearrange("(g t p) c -> g p t c", t=GT, p=P)
                for g in range(groups):
                    sp.wait_ge(x_ready, g + 1)
                    sp.dma_start(out_rows[g], k.x[:, g * GT:(g + 1) * GT, :]).then_inc(stored, 16)
                sp.wait_ge(stored, 16 * groups)

        @block.vector
        def _(dve):
            if plain:
                return
            link = Count(own)

            def statistics(src, g):
                for t in range(g * GT, (g + 1) * GT):
                    link.inc(nc.vector.bn_stats(stats[:, t, :], src[:, t, :]))
                link.wait(dve)
                for t in range(g * GT, (g + 1) * GT):
                    link.inc(nc.vector.bn_aggr(mean_var[:, t, :], stats[:, t, :]))

            def variances():
                link.wait(dve)
                nc.vector.tensor_scalar(veps[:], mean_var[:, :, 1], EPS, None, ALU.add).then_inc(var_ready, 1)

            def normalise(src, g):
                for t in range(g * GT, (g + 1) * GT):
                    ins = nc.vector.tensor_scalar(normed[:, t, :], src[:, t, :], mean_var[:, t, 0:1],
                                                  rstd[:, t:t + 1], ALU.subtract, ALU.mult)
                return ins

            nc.vector.memset(power[:], -0.5).then_inc(power_set, 1)
            if sublayer:
                if post:
                    dve.wait_ge(row_loaded, 16)
                for g in range(groups):
                    if post:
                        acc = k.acc[:, g * GT:(g + 1) * GT, :]
                        link.step(dve, nc.vector.tensor_tensor(
                            acc, acc, row[:].unsqueeze(1).broadcast_to([P, GT, C]), post[1]))
                    statistics(k.acc, g)
                variances()
                dve.wait_ge(rstd_ready, 1)
                if load:
                    dve.wait_ge(loaded, 16 * groups)
                for g in range(groups):
                    link.step(dve, normalise(k.acc, g))
                    x = k.x[:, g * GT:(g + 1) * GT, :]
                    ins = nc.vector.tensor_tensor(x, x, normed[:, g * GT:(g + 1) * GT, :], ALU.add)
                    if following:
                        link.step(dve, ins)
                        statistics(k.x, g)
                    else:
                        ins.then_inc(x_ready, 1)
            else:
                dve.wait_ge(loaded, 16 * groups)
                for g in range(groups):
                    statistics(k.x, g)
            if following:
                variances()
                dve.wait_ge(rstd_ready, 1 + int(sublayer))
                for g in range(groups):
                    normalise(k.x, g).then_inc(normed_ready, 1)

        @block.gpsimd
        def _(pool):
            if not plain:
                pool.wait_ge(power_set, 1)
                for n in range(int(sublayer) + int(following)):
                    pool.wait_ge(var_ready, n + 1)
                    nc.gpsimd.tensor_tensor(rstd[:], veps[:], power[:], ALU.pow).then_inc(rstd_ready, 1)
            if following:
                for g in range(groups):
                    pool.wait_ge(copied, g + 1)
                    for kt in range(KC):
                        part = slice(g * NB, (g + 1) * NB)
                        ins = nc.gpsimd.tensor_tensor(k.xT[1][:, kt, part], turned[:, g % 2, kt, :],
                                                      k.xT[0][:, kt, part].bitcast(F32), ALU.subtract)
                    ins.then_inc(lo_done, 1)

        @block.tensor
        def _(pe):
            if following:
                for g in range(groups):
                    if not plain:
                        pe.wait_ge(normed_ready, g + 1)
                    if g >= 2:
                        pe.wait_ge(copied, g - 1)
                    for kt in range(KC):
                        for j in range(GT):
                            ins = nc.tensor.transpose(k.psum[:, g % 2 * KC + kt, j * P:(j + 1) * P],
                                                      rows_out[:, g * GT + j, kt * P:(kt + 1) * P], k.ident[:])
                    ins.then_inc(turned_ready, 1)

        @block.scalar
        def _(act):
            if following:
                for g in range(groups):
                    act.wait_ge(turned_ready, g + 1)
                    bank = k.psum[:, g % 2 * KC:(g % 2 + 1) * KC, :]
                    nc.scalar.activation(k.xT[0][:, :, g * NB:(g + 1) * NB], bank, ACT.Copy)
                    if g >= 2:
                        act.wait_ge(lo_done, g - 1)
                    nc.scalar.activation(turned[:, g % 2], bank, ACT.Copy).then_inc(copied, 1)


HP = 2
WQKV = 3 * KC * HP * D0
WO = HP * C
ST = SEQ // P
QG = ST // GT


def attention0_stage(nc, k, name, ins):
    scale = float(D0) ** -0.5
    tiles = HP * ST
    groups = tiles // GT
    qk_uses, v_uses = HP * 2 * SEQ // NB, ST * HP * D0 // NB
    uses = qk_uses + v_uses + 2 * tiles
    passes = H0 // HP
    scale_rows = FP4_BLOCK
    with ExitStack() as ctx:
        st = Stage(nc, ctx, name)
        codes = st.sb("codes", [P, WQKV + WO])
        scales = st.sb("scales", [P, WQKV + WO])
        scale_row = st.sb("scale_row", [P, 1])
        bias_in = st.sb("bias_in", [P, 2 * HP])
        bias_qk = st.sb("bias_qk", [P, 2 * HP])
        bias_v_in = st.sb("bias_v_in", [P, HP * D0])
        bias_v = st.sb("bias_v", [P, HP * D0])
        w = st.halves("w", [P, 3, KC, HP * D0])
        wo = st.halves("wo", [P, HP, C])
        q = st.halves("q", [P, HP, SEQ])
        key = st.halves("key", [P, HP, SEQ])
        v = st.halves("v", [P, ST, HP * D0])
        prob = st.sb("prob", [P, 2, SEQ])
        v_whole = prob[:, 1, :].rearrange("p (a n) -> p a n", a=2)
        probT = st.halves("probT", [P, 2, ST, NB])
        o = st.halves("o", [P, NB])
        neg_max = st.sb("neg_max", [P, 2])
        total = st.sb("total", [P, tiles])
        over_total = st.sb("over_total", [P, tiles])
        landed, staged_free, w_ready, wo_ready = (st.sem(n) for n in ("landed", "staged_free", "w_ready", "wo_ready"))
        ring_full, ring_hi, ring_free = (st.sem(n) for n in ("ring_full", "ring_hi", "ring_free"))
        scale_set = st.sem("scale_set")
        v_hi_done, v_done = st.sem("v_hi_done"), st.sem("v_done")
        score_full, max_ready, exp_done = (st.sem(n) for n in ("score_full", "max_ready", "exp_done"))
        o_full, o_hi_done, o_done = (st.sem(n) for n in ("o_full", "o_hi_done", "o_done"))
        out_full, out_done, own, split = (st.sem(n) for n in ("out_full", "out_done", "own", "split"))
        block = ctx.enter_context(nc.Block())

        ring = lambda n: k.psum[:, 4 + n % 2, :]
        scores = lambda i: k.psum[:, i % 2 * 2:i % 2 * 2 + 2, :]
        o_bank, out_bank = k.psum[:, 6, :], k.psum[:, 7, :]
        turn_use = lambda i, half: qk_uses + v_uses + 2 * i + half

        def qk_chunk(n):
            return n // (SEQ // NB) % 2, n // (2 * SEQ // NB), n % (SEQ // NB)

        @block.sync
        def _(sp):
            def load(m):
                at = m * HP * D0
                part = bass.ds(at, HP * D0)
                n = 0
                for which, x in enumerate("qkv"):
                    to = slice(which * KC * HP * D0, (which + 1) * KC * HP * D0)
                    sp.dma_start(codes[:, to].rearrange("p (k n) -> p k n", k=KC),
                                 ins[f"w{x}_codes"].rearrange("(k p) n -> p k n", p=P)[:, :, part]).then_inc(landed, 16)
                    rows = ins[f"w{x}_scales"].rearrange("(k b) n -> b k n", k=KC)
                    for b in range(P // scale_rows):
                        sp.dma_start(scales[b * scale_rows:(b + 1) * scale_rows, to].rearrange("p (k n) -> p k n", k=KC),
                                     rows[b:b + 1, :, part].squeeze(0).partition_broadcast(scale_rows)).then_inc(landed, 16)
                        n += 1
                    n += 1
                sp.dma_start(codes[:, WQKV:].rearrange("p (h n) -> p h n", h=HP),
                             ins["wo_codes"].rearrange("(h p) n -> p h n", p=P)[:, bass.ds(m * HP, HP), :]).then_inc(landed, 16)
                rows = ins["wo_scales"].rearrange("(h b) n -> b h n", b=P // scale_rows)
                for b in range(P // scale_rows):
                    sp.dma_start(scales[b * scale_rows:(b + 1) * scale_rows, WQKV:].rearrange("p (h n) -> p h n", h=HP),
                                 rows[b:b + 1, bass.ds(m * HP, HP), :].squeeze(0).partition_broadcast(scale_rows)).then_inc(landed, 16)
                for which, x in enumerate("qk"):
                    sp.dma_start(bias_in[:, which * HP:(which + 1) * HP],
                                 ins[f"b{x}"][:, bass.ds(m * HP, HP)]).then_inc(landed, 16)
                sp.dma_start(bias_v_in[:], ins["bv"][part].partition_broadcast(P)).then_inc(landed, 16)

            with sp.Fori(0, passes) as m:
                sp.wait_ge(staged_free, m + 1)
                load(m)
        loads = 16 * (3 * (1 + P // scale_rows) + 1 + P // scale_rows + 2 + 1)

        @block.gpsimd
        def _(pool):
            pool.nop().then_inc(staged_free, 1)
            nc.gpsimd.memset(scale_row[:], scale).then_inc(scale_set, 1)
            pool.wait_ge(scale_set, 1)
            for _ in range(2):
                pool.nop().then_inc(v_done, 1)

            def split_weights(m, first=False):
                pool.wait_ge(landed, (m + 1) * loads)
                flat = lambda t: t[:].rearrange("p a b c -> p (a b c)")
                nq = KC * HP * D0
                n = m * 8
                nc.gpsimd.tensor_tensor(scales[:, 0:nq], scales[:, 0:nq], scale_row[:].broadcast_to([P, nq]), ALU.mult).then_inc(split, 1)
                nc.gpsimd.tensor_scalar(bias_in[:, 0:HP], bias_in[:, 0:HP], scale, 1.0, ALU.mult, ALU.mult).then_inc(split, 1)
                pool.wait_ge(split, n + 2)
                if not first:
                    pool.wait_ge(ring_full, (2 * (m - 1) + 1) * uses + qk_uses + v_uses)
                nc.gpsimd.tensor_tensor(flat(w[0]), codes[:, 0:WQKV], scales[:, 0:WQKV], ALU.mult).then_inc(split, 1)
                nc.gpsimd.tensor_scalar(bias_qk[:], bias_in[:], 1.0, 1.0, ALU.mult, ALU.mult)
                nc.gpsimd.tensor_scalar(bias_v[:], bias_v_in[:], 1.0, 1.0, ALU.mult, ALU.mult)
                if not first:
                    pool.wait_ge(out_full, 2 * groups * 2 * m)
                nc.gpsimd.tensor_tensor(wo[0][:].rearrange("p a b -> p (a b)"), codes[:, WQKV:], scales[:, WQKV:],
                                        ALU.mult).then_inc(split, 1)
                pool.wait_ge(split, n + 4)
                nc.gpsimd.tensor_tensor(codes[:], codes[:], scales[:], ALU.mult).then_inc(split, 1)
                pool.wait_ge(split, n + 5)
                nc.gpsimd.tensor_tensor(flat(w[1]), codes[:, 0:WQKV], flat(w[0]).bitcast(F32), ALU.subtract).then_inc(w_ready, 1)
                nc.gpsimd.tensor_tensor(wo[1][:].rearrange("p a b -> p (a b)"), codes[:, WQKV:],
                                        wo[0][:].rearrange("p a b -> p (a b)").bitcast(F32), ALU.subtract).then_inc(wo_ready, 1)
                pool.wait_ge(wo_ready, m + 1)
                pool.nop().then_inc(staged_free, 1)
                for _ in range(3):
                    pool.nop().then_inc(split, 1)

            def v_lo(m):
                for half in range(2):
                    for n in range(v_uses):
                        use = (m * 2 + half) * v_uses + n
                        pool.wait_ge(v_hi_done, use + 1)
                        to = slice(n * GT // HP, (n + 1) * GT // HP)
                        nc.gpsimd.tensor_tensor(v[1][:, to, :].rearrange("p t d -> p (t d)"), v_whole[:, n % 2, :],
                                                v[0][:, to, :].rearrange("p t d -> p (t d)").bitcast(F32),
                                                ALU.subtract).then_inc(v_done, 1)

            split_weights(0, first=True)
            with pool.Fori(0, passes - 1) as m:
                v_lo(m)
                split_weights(m + 1)
            v_lo(passes - 1)

        @block.tensor
        def _(pe):
            def take_ring(half, n):
                use = half * uses + n
                pe.wait_ge(ring_free, use + 1)

            def project_qk(half, b):
                for n in range(qk_uses):
                    which, head, c = qk_chunk(n)
                    cols = slice(head * D0, (head + 1) * D0)
                    tokens = slice(b * SEQ + c * NB, b * SEQ + (c + 1) * NB)
                    take_ring(half, n)
                    project(nc, ring(n), lambda kt: [h[:, which, kt, cols] for h in w],
                            lambda kt: [h[:, kt, tokens] for h in k.xT]).then_inc(ring_full, 1)

            def project_v(half, b):
                for n in range(v_uses):
                    take_ring(half, qk_uses + n)
                    for j in range(2):
                        t = b * ST + 2 * n + j
                        mm = project(nc, ring(n)[:, j * HP * D0:(j + 1) * HP * D0],
                                     lambda kt: [h[:, kt, t * P:(t + 1) * P] for h in k.xT],
                                     lambda kt: [h[:, 2, kt, :] for h in w])
                    mm.then_inc(ring_full, 1)

            def score(half, i):
                head, t = i // ST, i % ST
                pe.wait_ge(exp_done, half * tiles + i + 1)
                for c in range(SEQ // NB):
                    mm = three_passes(nc, scores(i)[:, c, :], [h[:, head, t * P:(t + 1) * P] for h in q],
                                      [h[:, head, c * NB:(c + 1) * NB] for h in key])
                mm.then_inc(score_full, 1)

            def turn(half, i):
                pe.wait_ge(exp_done, half * tiles + i + 3)
                for half_tile in range(2):
                    use = turn_use(i, half_tile)
                    take_ring(half, use)
                    for j in range(GT):
                        kt = half_tile * GT + j
                        mm = nc.tensor.transpose(ring(use)[:, j * P:(j + 1) * P], prob[:, i % 2, kt * P:(kt + 1) * P], k.ident[:])
                    mm.then_inc(ring_full, 1)

            def weighted_v(half, g, part):
                head = g // QG
                if part == 0:
                    pe.wait_ge(ring_free, half * uses + turn_use((g + 1) * GT - 1, 1) + 3)
                    pe.wait_ge(o_done, half * groups + g + 1)
                    if g == 0:
                        pe.wait_ge(v_done, (half + 1) * v_uses + 2)
                n = ST // GT
                for kt in range(part * n, (part + 1) * n):
                    mm = three_passes(nc, o_bank, [h[:, kt, head * D0:(head + 1) * D0] for h in v],
                                      [h[:, g % 2, kt, :] for h in probT], start=kt == 0, stop=kt == ST - 1)
                if part == GT - 1:
                    mm.then_inc(o_full, 1)

            def output(half, g, part):
                use = (half * groups + g) * 2 + part
                if part == 0:
                    pe.wait_ge(o_done, half * groups + g + 2)
                pe.wait_ge(out_done, use + 1)
                for j in range(2):
                    t = part * 2 + j
                    mm = three_passes(nc, out_bank[:, j * C:(j + 1) * C], [h[:, t * P:(t + 1) * P] for h in o],
                                      [h[:, g // QG, :] for h in wo])
                mm.then_inc(out_full, 1)

            with pe.Fori(0, passes) as m:
                for b in range(BATCH):
                    half = m * BATCH + b
                    if b == 0:
                        pe.wait_ge(w_ready, m + 1)
                    project_qk(half, b)
                    if b == 0:
                        pe.wait_ge(wo_ready, m + 1)
                    else:
                        for part in range(2):
                            output(half - 1, groups - 1, part)
                    pe.wait_ge(ring_free, half * uses + qk_uses + 2)
                    score(half, 0)
                    project_v(half, b)
                    for i in range(tiles):
                        g, j = i // GT, i % GT
                        if i + 1 < tiles:
                            score(half, i + 1)
                        turn(half, i)
                        if g >= 2 and j % 2:
                            output(half, g - 2, j // 2)
                        if g >= 1:
                            weighted_v(half, g - 1, j)
                    for part in range(GT):
                        if part % 2 == 0:
                            output(half, groups - 2, part // 2)
                        weighted_v(half, groups - 1, part)
                for part in range(2):
                    output(half, groups - 1, part)

        @block.scalar
        def _(act):
            for _ in range(2):
                act.nop().then_inc(exp_done, 1)

            def exp(half, i):
                act.wait_ge(max_ready, half * tiles + i + 1)
                if i >= 2:
                    act.wait_ge(ring_full, half * uses + turn_use(i - 2, 1) + 1)
                if i == 1:
                    act.wait_ge(v_done, (half + 1) * v_uses + 2)
                nc.scalar.activation(prob[:, i % 2, :], scores(i).rearrange("p a b -> p (a b)"), ACT.Exp,
                                     bias=neg_max[:, i % 2:i % 2 + 1],
                                     accum_out=total[:, i:i + 1]).then_inc(exp_done, 1)

            with act.Fori(0, passes) as m:
                for b in range(BATCH):
                    half = m * BATCH + b
                    hi_base = half * (qk_uses + 2 * tiles)
                    for n in range(qk_uses):
                        which, head, c = qk_chunk(n)
                        act.wait_ge(ring_full, half * uses + n + 1)
                        nc.scalar.activation((q, key)[which][0][:, head, c * NB:(c + 1) * NB], ring(n), ACT.Identity,
                                             bias=bias_qk[:, which * HP + head:which * HP + head + 1]).then_inc(ring_hi, 1)
                    exp(half, 0)
                    for n in range(v_uses):
                        act.wait_ge(ring_free, half * uses + qk_uses + n + 3)
                        to = slice(n * GT // HP, (n + 1) * GT // HP)
                        nc.scalar.activation(v[0][:, to, :].rearrange("p t d -> p (t d)"), v_whole[:, n % 2, :],
                                             ACT.Copy).then_inc(v_hi_done, 1)
                    for i in range(tiles):
                        g, j = i // GT, i % GT
                        for half_tile in range(2):
                            use = turn_use(i, half_tile)
                            act.wait_ge(ring_full, half * uses + use + 1)
                            nc.scalar.activation(
                                probT[0][:, g % 2, half_tile * GT:(half_tile + 1) * GT, j * P:(j + 1) * P],
                                ring(use).rearrange("p (t n) -> p t n", n=P), ACT.Copy).then_inc(ring_hi, 1)
                        if i + 1 < tiles:
                            exp(half, i + 1)
                        if g >= 1 and j == GT - 1:
                            act.wait_ge(o_full, half * groups + g)
                            nc.scalar.activation(o[0][:], o_bank, ACT.Copy).then_inc(o_hi_done, 1)
                    act.wait_ge(o_full, (half + 1) * groups)
                    nc.scalar.activation(o[0][:], o_bank, ACT.Copy).then_inc(o_hi_done, 1)

        @block.vector
        def _(dve):
            for _ in range(2):
                dve.nop().then_inc(ring_free, 1)
            dve.nop().then_inc(o_done, 1)
            dve.nop().then_inc(out_done, 1)
            nc.vector.memset(k.acc[:], 0.0).then_inc(own, 1)
            dve.wait_ge(own, 1)

            def row_max(half, i):
                dve.wait_ge(score_full, half * tiles + i + 1)
                nc.vector.tensor_reduce(neg_max[:, i % 2:i % 2 + 1], scores(i), AX.XY, ALU.max,
                                        negate=True).then_inc(max_ready, 1)

            def o_lo(half, g):
                dve.wait_ge(o_hi_done, half * groups + g + 1)
                nc.vector.tensor_tensor(o[1][:], o_bank, f32(o[0][:]), ALU.subtract).then_inc(o_done, 1)

            def add_up(half, g, part):
                use = (half * groups + g) * 2 + part
                if part == 0:
                    nc.vector.reciprocal(over_total[:, g * GT:(g + 1) * GT], total[:, g * GT:(g + 1) * GT]).then_inc(own, 1)
                    dve.wait_ge(own, half * groups + g + 2)
                dve.wait_ge(out_full, use + 1)
                for j in range(2):
                    t = part * 2 + j
                    to = k.acc[:, (b_of[0] * ST) + g % QG * GT + t, :]
                    add = nc.vector.scalar_tensor_tensor(out=to, in0=out_bank[:, j * C:(j + 1) * C],
                                                         scalar=over_total[:, g * GT + t:g * GT + t + 1], in1=to,
                                                         op0=ALU.mult, op1=ALU.add)
                add.then_inc(out_done, 1)

            b_of = [0]
            with dve.Fori(0, passes) as m:
                for b in range(BATCH):
                    half = m * BATCH + b
                    hi_base = half * (qk_uses + 2 * tiles)
                    for n in range(qk_uses):
                        which, head, c = qk_chunk(n)
                        dve.wait_ge(ring_hi, hi_base + n + 1)
                        to = [h[:, head, c * NB:(c + 1) * NB] for h in (q, key)[which]]
                        nc.vector.scalar_tensor_tensor(
                            out=to[1], in0=ring(n), scalar=bias_qk[:, which * HP + head:which * HP + head + 1],
                            in1=f32(to[0]), op0=ALU.add, op1=ALU.subtract).then_inc(ring_free, 1)
                    if b:
                        b_of[0] = b - 1
                        for part in range(2):
                            add_up(half - 1, groups - 1, part)
                    b_of[0] = b
                    row_max(half, 0)
                    for n in range(v_uses):
                        dve.wait_ge(ring_full, half * uses + qk_uses + n + 1)
                        dve.wait_ge(v_done, half * v_uses + n + 1)
                        nc.vector.tensor_tensor(
                            v_whole[:, n % 2, :].rearrange("p (t d) -> p t d", t=2),
                            ring(n).rearrange("p (t d) -> p t d", t=2),
                            bias_v[:].unsqueeze(1).broadcast_to([P, 2, HP * D0]), ALU.add).then_inc(ring_free, 1)
                    for i in range(tiles):
                        g, j = i // GT, i % GT
                        if i + 1 < tiles:
                            row_max(half, i + 1)
                        for half_tile in range(2):
                            use = turn_use(i, half_tile)
                            dve.wait_ge(ring_hi, hi_base + qk_uses + 2 * i + half_tile + 1)
                            to = [h[:, g % 2, half_tile * GT:(half_tile + 1) * GT, j * P:(j + 1) * P] for h in probT]
                            nc.vector.tensor_tensor(to[1], ring(use).rearrange("p (t n) -> p t n", n=P), f32(to[0]),
                                                    ALU.subtract).then_inc(ring_free, 1)
                        if g >= 2 and j % 2:
                            add_up(half, g - 2, j // 2)
                        if g >= 1 and j == GT - 1:
                            o_lo(half, g - 1)
                    for part in range(2):
                        add_up(half, groups - 2, part)
                    o_lo(half, groups - 1)
                for part in range(2):
                    add_up(half, groups - 1, part)


def f32(ap):
    return ap.bitcast(F32)


def mlp_stage(nc, k, name, w_dram, n_chunks, *, hidden_scales=None, weigh=None):
    cols_up, cols_down = KC * IM, 2 * KC * IM
    cols = cols_down + C
    per_chunk = TOK // NB
    pair = 2 * per_chunk
    with ExitStack() as ctx:
        st = Stage(nc, ctx, name)
        staged = st.sb("staged", [P, 2, cols])
        w_hi, w_lo = st.halves("w", [P, 2, cols])
        gate_act = st.sb("gate_act", [P, 2, NB])
        hidden = st.sb("hidden", [P, 2, NB])
        hid_hi, hid_lo = st.halves("hid", [P, 2, NB])
        scales = st.sb("scales", [P, 2, n_chunks])
        gate_scale = st.sb("gate_scale", [P, 2])
        landed = [st.sem(f"landed{n}") for n in range(2)]
        scales_in, staged_free, hi_split, w_ready = (st.sem(n) for n in ("scales_in", "staged_free", "hi_split", "w_ready"))
        gate_full, up_full, silu_done, prod_done = (st.sem(n) for n in ("gate_full", "up_full", "silu_done", "prod_done"))
        hi_done, lo_done, down_full, acc_done = (st.sem(n) for n in ("hi_done", "lo_done", "down_full", "acc_done"))
        cleared, scale_set = st.sem("cleared"), st.sem("scale_set")
        block = ctx.enter_context(nc.Block())
        gate_bank = lambda q: k.psum[:, q % 2, :]
        up_bank = lambda q: k.psum[:, 2 + q % 2, :]
        down_tile = lambda q, j: k.psum[:, 4 + 2 * (q % 2) + j // 2, j % 2 * C:(j % 2 + 1) * C]

        @block.sync
        def _(sp):
            if hidden_scales is not None:
                sp.dma_start(scales[:], hidden_scales.rearrange("s p n -> p s n")).then_inc(scales_in, 16)
            with sp.Fori(0, n_chunks // 2) as m:
                for e in range(2):
                    sp.wait_ge(staged_free, m * 2 + e + 1)
                    sp.dma_start(staged[:, e, :], w_dram[bass.ds(m * 2 + e, 1)].squeeze(0)).then_inc(landed[e], 16)

        @block.tensor
        def _(pe):
            def gate_up(m, s, e_next=False):
                e, c = s // per_chunk % 2, s % per_chunk
                step = m * pair + s
                tokens = slice(c * NB, (c + 1) * NB)
                if c == 0:
                    pe.wait_ge(w_ready, m * 2 + s // per_chunk + 1)
                x = lambda kt: [h[:, kt, tokens] for h in k.xT]
                pe.wait_ge(silu_done, step + 1)
                project(nc, gate_bank(s), lambda kt: [w[:, e, kt * IM:(kt + 1) * IM] for w in (w_hi, w_lo)],
                        x).then_inc(gate_full, 1)
                pe.wait_ge(prod_done, step + 1)
                project(nc, up_bank(s), lambda kt: [w[:, e, cols_up + kt * IM:cols_up + (kt + 1) * IM]
                                                    for w in (w_hi, w_lo)], x).then_inc(up_full, 1)

            def down(m, s):
                e = s // per_chunk
                step = m * pair + s
                pe.wait_ge(lo_done, step + 3)
                for j in range(GT):
                    if j % 2 == 0:
                        pe.wait_ge(acc_done, step * 2 + j // 2 + 1)
                    ins = three_passes(nc, down_tile(s, j),
                                       [h[:, s % 2, j * P:(j + 1) * P] for h in (hid_hi, hid_lo)],
                                       [w[:, e, cols_down:cols] for w in (w_hi, w_lo)])
                    if j % 2:
                        ins.then_inc(down_full, 1)

            gate_up(0, 0)
            with pe.Fori(0, n_chunks // 2 - 1) as m:
                for s in range(pair):
                    gate_up(m, s + 1)
                    down(m, s)
            m = n_chunks // 2 - 1
            for s in range(pair):
                if s + 1 < pair:
                    gate_up(m, s + 1)
                down(m, s)

        @block.scalar
        def _(act):
            for _ in range(2):
                act.nop().then_inc(silu_done, 1)
            if hidden_scales is not None:
                act.wait_ge(scales_in, 16)
            with act.Fori(0, n_chunks // 2) as m:
                for s in range(pair):
                    step = m * pair + s
                    e = s // per_chunk
                    if hidden_scales is not None and s % per_chunk == 0:
                        nc.scalar.activation(gate_scale[:, e:e + 1], scales[:, 0, bass.ds(m * 2 + e, 1)],
                                             ACT.Copy).then_inc(scale_set, 1)
                        act.wait_ge(scale_set, m * 2 + e + 1)
                    act.wait_ge(gate_full, step + 1)
                    act.wait_ge(prod_done, step + 1)
                    by = 1.0 if hidden_scales is None else gate_scale[:, e:e + 1]
                    nc.scalar.activation(gate_act[:, s % 2, :], gate_bank(s), ACT.Silu, scale=by).then_inc(silu_done, 1)
                    act.wait_ge(prod_done, step + 3)
                    nc.scalar.activation(hid_hi[:, s % 2, :], hidden[:, s % 2, :], ACT.Copy).then_inc(hi_done, 1)

        @block.gpsimd
        def _(pool):
            for _ in range(2):
                pool.nop().then_inc(lo_done, 1)
            with pool.Fori(0, n_chunks // 2) as m:
                for s in range(pair):
                    pool.wait_ge(hi_done, m * pair + s + 1)
                    nc.gpsimd.tensor_tensor(hid_lo[:, s % 2, :], hidden[:, s % 2, :],
                                            hid_hi[:, s % 2, :].bitcast(F32), ALU.subtract).then_inc(lo_done, 1)

        @block.vector
        def _(dve):
            def split_weights(m, e):
                dve.wait_ge(landed[e % 2], m * 16 + (16 if e < 2 else 32))
                nc.vector.tensor_copy(w_hi[:, e % 2, :], staged[:, e % 2, :]).then_inc(hi_split, 1)
                dve.wait_ge(hi_split, m * 2 + e + 1)
                nc.vector.tensor_tensor(w_lo[:, e % 2, :], staged[:, e % 2, :], w_hi[:, e % 2, :].bitcast(F32),
                                        ALU.subtract).then_inc(w_ready, 1)
                dve.wait_ge(w_ready, m * 2 + e + 1)
                dve.nop().then_inc(staged_free, 1)

            def product(m, s):
                step = m * pair + s
                dve.wait_ge(silu_done, step + 3)
                dve.wait_ge(up_full, step + 1)
                dve.wait_ge(lo_done, step + 1)
                h, g = hidden[:, s % 2, :], gate_act[:, s % 2, :]
                if hidden_scales is None:
                    ins = nc.vector.tensor_tensor(h, up_bank(s), g, ALU.mult)
                else:
                    by = scales[:, 1, bass.ds(m * 2 + s // per_chunk, 1)]
                    ins = nc.vector.scalar_tensor_tensor(out=h, in0=up_bank(s), scalar=by, in1=g,
                                                         op0=ALU.mult, op1=ALU.mult)
                ins.then_inc(prod_done, 1)

            def add_up(m, s):
                step = m * pair + s
                for j in range(GT):
                    if j % 2 == 0:
                        dve.wait_ge(down_full, step * 2 + j // 2 + 1)
                    t = s % per_chunk * GT + j
                    by = 1.0 if weigh is None else weigh[:, bass.ds((m * 2 + s // per_chunk) * TT + t, 1)]
                    ins = nc.vector.scalar_tensor_tensor(out=k.acc[:, t, :], in0=down_tile(s, j), scalar=by,
                                                         in1=k.acc[:, t, :], op0=ALU.mult, op1=ALU.add)
                    if j % 2:
                        ins.then_inc(acc_done, 1)

            for _ in range(2):
                dve.nop().then_inc(prod_done, 1)
                dve.nop().then_inc(staged_free, 1)
            for _ in range(4):
                dve.nop().then_inc(acc_done, 1)
            nc.vector.memset(k.acc[:], 0.0).then_inc(cleared, 1)
            dve.wait_ge(cleared, 1)
            if hidden_scales is not None:
                dve.wait_ge(scales_in, 16)
            split_weights(0, 0)
            product(0, 0)
            with dve.Fori(0, n_chunks // 2 - 1) as m:
                for s in range(pair):
                    if s % per_chunk == 1:
                        split_weights(m, s // per_chunk + 1)
                    product(m, s + 1)
                    add_up(m, s)
            m = n_chunks // 2 - 1
            for s in range(pair):
                if s == 1:
                    split_weights(m, 1)
                if s + 1 < pair:
                    product(m, s + 1)
                add_up(m, s)


def route_stage(nc, k, name, router_dram, weigh):
    with ExitStack() as ctx:
        st = Stage(nc, ctx, name)
        router = st.sb("router", [P, KC, N_EXPERT])
        r_hi, r_lo = st.halves("r", [P, KC, N_EXPERT])
        score = st.sb("score", [P, TT, N_EXPERT])
        best = st.sb("best", [P, TT, N_TOP])
        rest = st.sb("rest", [P, TT, N_EXPERT])
        total = st.sb("total", [P, TT])
        factor = st.sb("factor", [P, TT])
        landed, own, r_ready, logits_full, score_ready = (
            st.sem(n) for n in ("landed", "own", "r_ready", "logits_full", "score_ready"))
        block = ctx.enter_context(nc.Block())

        @block.sync
        def _(sp):
            sp.dma_start(router[:], router_dram).then_inc(landed, 16)

        @block.tensor
        def _(pe):
            pe.wait_ge(r_ready, 1)
            for t in range(TT):
                ins = project(nc, k.psum[:, 0, t * N_EXPERT:(t + 1) * N_EXPERT],
                              lambda kt: [h[:, kt, t * P:(t + 1) * P] for h in k.xT],
                              lambda kt: [r[:, kt, :] for r in (r_hi, r_lo)])
            ins.then_inc(logits_full, 1)

        @block.scalar
        def _(act):
            act.wait_ge(logits_full, 1)
            nc.scalar.activation(score[:].rearrange("p t e -> p (t e)"), k.psum[:, 0, 0:TT * N_EXPERT],
                                 ACT.Sigmoid).then_inc(score_ready, 1)

        @block.vector
        def _(dve):
            link = Count(own)
            dve.wait_ge(landed, 16)
            link.step(dve, nc.vector.tensor_copy(r_hi[:], router[:]))
            nc.vector.tensor_tensor(r_lo[:], router[:], r_hi[:].bitcast(F32), ALU.subtract).then_inc(r_ready, 1)
            nc.vector.memset(weigh[:, N_EXPERT * TT:], 1.0)
            dve.wait_ge(score_ready, 1)
            for t in range(TT):
                link.inc(nc.vector.max(best[:, t, :], score[:, t, :]))
            link.wait(dve)
            for t in range(TT):
                link.inc(nc.vector.match_replace(rest[:, t, :], best[:, t, :], score[:, t, :], -1.0))
            link.step(dve, nc.vector.tensor_reduce(total[:], best[:], AX.X, ALU.add))
            link.step(dve, nc.vector.tensor_scalar(total[:], total[:], 1e-6, None, ALU.add))
            link.step(dve, nc.vector.reciprocal(factor[:], total[:]))
            link.step(dve, nc.vector.tensor_scalar(factor[:], factor[:], ROUTE_SCALE, None, ALU.mult))
            link.step(dve, nc.vector.tensor_scalar(rest[:], rest[:], 0.0, None, ALU.is_lt))
            link.step(dve, nc.vector.tensor_tensor(rest[:], rest[:], score[:], ALU.mult))
            nc.vector.tensor_tensor(weigh[:, 0:N_EXPERT * TT].rearrange("p (e t) -> p t e", t=TT), rest[:],
                                    factor[:].unsqueeze(2).broadcast_to([P, TT, N_EXPERT]), ALU.mult)


def projection_stage(nc, k, name, w_dram):
    with ExitStack() as ctx:
        st = Stage(nc, ctx, name)
        w = st.sb("w", [P, KC, C])
        w_hi, w_lo = st.halves("w", [P, KC, C])
        landed, own, w_ready, full, copied = (st.sem(n) for n in ("landed", "own", "w_ready", "full", "copied"))
        block = ctx.enter_context(nc.Block())

        @block.sync
        def _(sp):
            sp.dma_start(w[:], w_dram.rearrange("(k p) n -> p k n", p=P)).then_inc(landed, 16)

        @block.tensor
        def _(pe):
            pe.wait_ge(w_ready, 1)
            for t in range(TT):
                if t % 2 == 0 and t >= 16:
                    pe.wait_ge(copied, t // 2 - 7)
                ins = project(nc, k.psum[:, t // 2 % 8, t % 2 * C:(t % 2 + 1) * C],
                              lambda kt: [h[:, kt, t * P:(t + 1) * P] for h in k.xT],
                              lambda kt: [p[:, kt, :] for p in (w_hi, w_lo)])
                if t % 2:
                    ins.then_inc(full, 1)

        @block.vector
        def _(dve):
            dve.wait_ge(landed, 16)
            nc.vector.tensor_copy(w_hi[:], w[:]).then_inc(own, 1)
            dve.wait_ge(own, 1)
            nc.vector.tensor_tensor(w_lo[:], w[:], w_hi[:].bitcast(F32), ALU.subtract).then_inc(w_ready, 1)
            for b in range(TT // 2):
                dve.wait_ge(full, b + 1)
                nc.vector.tensor_copy(k.acc[:, 2 * b:2 * b + 2, :].rearrange("p t c -> p (t c)"),
                                      k.psum[:, b % 8, :]).then_inc(copied, 1)


HG = 4
HEAD_ROWS = P // HG
STACK = 64
N_SHIFT = 2 * GT
f32 = lambda ap: ap.bitcast(F32)


def attention1_stage(nc, k, name, ins):
    passes = H1 // HG
    chunks = SEQ // NB
    unit_steps = [(c, kt) for c in range(chunks) for kt in range((c + 1) * GT)]
    UNIT, HALF = len(unit_steps), HG * len(unit_steps)
    PASS = BATCH * HALF
    STEPS = passes * PASS
    LEAD_SCORES, LEAD_MAX, FIRST = 2, 14, 12
    pieces = [(t, part) for t in range(ST) for part in range(t // GT + 1)]
    last_piece = [max(n for n, (t, _) in enumerate(pieces) if t // GT == c) for c in range(chunks)]
    pairs = HG // 2
    proj_jobs = [(pair, c, which) for pair in range(pairs) for c in range(chunks) for which in range(2)]
    N_PROJ = len(proj_jobs)
    PROJ_STEPS = (5, 8, 13, 17, 20, 25, 29, 32)
    TURN_STEPS = (3, 11)
    TURN_LEAD = (9, 1)
    V_USES = TT * C // NB
    PROLOGUE_USES = V_USES + N_PROJ
    SCORE_BANKS = 3

    def place(u):
        return u // HG % BATCH, u % HG

    def misc_jobs(g):
        half, r, s = g // HALF, g % HALF, g % UNIT
        jobs = []
        for c in range(chunks):
            if s == TURN_STEPS[c] and 0 <= (g + TURN_LEAD[c]) // UNIT < STEPS // UNIT:
                jobs.append(("maxima", (g + TURN_LEAD[c]) // UNIT, c))
        if g >= 0 and r in PROJ_STEPS and half + 1 < STEPS // HALF:
            jobs.append(("project", half + 1, PROJ_STEPS.index(r)))
        for at, kind, back, c in ((41, "sums", 0, 0), (44, "spread", 0, 0), (1, "out0", 1, 0), (4, "out1", 1, 0),
                                  (2, "sums", 1, 1), (6, "spread", 1, 1), (10, "out0", 1, 1), (11, "out1", 1, 1)):
            if r == at and 0 <= half - back < STEPS // HALF:
                jobs.append((kind, half - back, c))
        return jobs

    first_use, uses = {}, PROLOGUE_USES
    for g in range(-LEAD_MAX, STEPS + FIRST):
        first_use[g] = uses
        uses += len(misc_jobs(g))
    USES = first_use[FIRST + PASS] - first_use[FIRST]

    def timeline(eng, step):
        for g in range(-LEAD_MAX, FIRST):
            step(0, g)
        with eng.Fori(0, passes - 1) as m:
            for g in range(FIRST, FIRST + PASS):
                step(m, g)
        for g in range(STEPS - PASS + FIRST, STEPS + FIRST):
            step(0, g)

    with ExitStack() as ctx:
        st = Stage(nc, ctx, name)
        w = st.halves("w", [P, KC, 2 * pairs, P])
        wv = st.halves("wv", [P, KC, C])
        wp = st.halves("wp", [P, passes, C])
        bias_in = st.sb("bias_in", [P, 2 * pairs])
        bias = st.sb("bias", [P, 2 * pairs])
        bias_lo = st.sb("bias_lo", [P, 2 * pairs])
        lo_rows = st.sb("lo_rows", [P, 2])
        bias_v = st.sb("bias_v", [P, C])
        one = st.sb("one", [P, 1])
        masks = st.sb("masks", [P, 2, P], BF16)
        ident_b = st.sb("ident_b", [P, P], BF16)
        tile_rows = st.sb("tile_rows", [P, GT, P])
        sum_rows = st.sb("sum_rows", [P, HG])
        q = [[st.sb(f"q_{b}{h}", [P, SEQ], F32R) for h in range(HG)] for b in range(BATCH)]
        key = [[st.sb(f"key_{b}{h}", [P, SEQ], F32R) for h in range(HG)] for b in range(BATCH)]
        projected = st.sb("projected", [P, 2, NB])
        only_hi = st.sb("only_hi", [P, 2, NB], F32R)
        v_all = st.sb("v_all", [P, TT, C])
        v = [st.sb(f"v_{b}", [P, ST, HG, 2 * D1]) for b in range(BATCH)]
        peaks = st.sb("peaks", [P, 2, UNIT])
        peak = st.sb("peak", [P, GT])
        shift = st.sb("shift", [P, 2, STACK + N_SHIFT])
        probT = st.sb("probT", [P, SCORE_BANKS, NB])
        o = st.sb("o", [P, chunks, NB])
        over_sum = st.sb("over_sum", [P, GT * HG])
        wide = st.sb("wide", [P, GT * HG, HEAD_ROWS])
        factor = st.sb("factor", [P, NB])
        y_whole = st.sb("y_whole", [P, NB])
        y = st.halves("y", [P, NB])
        wv_in = wide[:].rearrange("p a b -> p (a b)")
        wp_in = probT[:].rearrange("p a b -> p (a b)")[:, 0:passes * C]
        w_in = o[:].rearrange("p a b -> p (a b)")
        masks_in = y_whole[:, 0:2 * P].rearrange("p (a b) -> p a b", b=P)
        consts, landed, w_free, w_ready, split = (
            st.sem(n) for n in ("consts", "landed", "w_free", "w_ready", "split"))
        prepared, zeroed, ones_set, wv_ready, wp_ready = (st.sem(n) for n in ("prepared", "zeroed", "ones_set", "wv_ready", "wp_ready"))
        max_full, max_free, peak_done, shift_ready, shifted = (
            st.sem(n) for n in ("max_full", "max_free", "peak_done", "shift_ready", "shifted"))
        misc_full, misc_free, stacked = (st.sem(n) for n in ("misc_full", "misc_free", "stacked"))
        scores_full, exp_done, weighed = (st.sem(n) for n in ("scores_full", "exp_done", "weighed"))
        v_ready, inverted, widened = (st.sem(n) for n in ("v_ready", "inverted", "widened"))
        o_done, y_split, y_ready = (st.sem(n) for n in ("o_done", "y_split", "y_ready"))
        block = ctx.enter_context(nc.Block())

        max_bank = lambda n: k.psum[:, n % 2, :]
        score_bank = lambda g: k.psum[:, 2 + g % SCORE_BANKS, :]
        o_bank = lambda c: k.psum[:, 5 + c, :]
        misc = k.psum[:, 7, :]
        prologue_bank = lambda n: k.psum[:, 4 + n % 4, :]
        stack_rows = lambda h: slice(h % 2 * STACK, (h % 2 + 1) * STACK)
        shift_rows = lambda h: slice(0, N_SHIFT) if h % 2 else slice(STACK, STACK + N_SHIFT)
        other_rows = lambda h: slice(0, STACK) if h % 2 else slice(STACK, P)
        chunk = lambda c: slice(c * NB, (c + 1) * NB)

        def stack(eng, m, half, j):
            pair, c, which = proj_jobs[j]
            for i in range(2):
                h = 2 * pair + i
                rows = stack_rows(h)
                eng.tensor_tensor((q, key)[which][half % BATCH][h][rows, chunk(c)], projected[rows, j % 2, :],
                                  f32(only_hi[rows, j % 2, :]), ALU.subtract).then_inc(stacked, 1)
                eng.wait_ge(stacked, m * BATCH * N_PROJ * 2 + (half * N_PROJ + j) * 2 + i + 1)

        @block.sync
        def _(sp):
            for to, n in ((wv_in, "w_v"), (masks_in, "masks"), (lo_rows[:], "lo_rows"),
                          (tile_rows[:], "tile_rows"), (sum_rows[:], "sum_rows"), (wp_in, "w_proj")):
                sp.dma_start(to, ins[n]).then_inc(consts, 16)
            sp.dma_start(bias_v[:], ins["b_v"].partition_broadcast(P)).then_inc(consts, 16)
            with sp.Fori(0, passes) as m:
                sp.wait_ge(w_free, m + 1)
                sp.dma_start(w_in, ins["w_attn"][bass.ds(m, 1)].squeeze(0)).then_inc(landed, 16)
                sp.dma_start(bias_in[:], ins["b_qk"][bass.ds(m, 1)].squeeze(0)).then_inc(landed, 16)

        @block.gpsimd
        def _(pool):
            for _ in range(chunks):
                pool.nop().then_inc(y_ready, 1)
            pool.nop().then_inc(w_free, 1)
            nc.gpsimd.memset(one[:], 1.0).then_inc(ones_set, 1)
            pool.wait_ge(ones_set, 1)
            flat = lambda a: a.rearrange("p a b -> p (a b)")

            def halve(whole, parts, ready, n):
                width = whole.shape[1]
                nc.gpsimd.tensor_tensor(parts[0], whole, one[:].broadcast_to([P, width]), ALU.mult).then_inc(split, 1)
                pool.wait_ge(split, n)
                nc.gpsimd.tensor_tensor(parts[1], whole, f32(parts[0]), ALU.subtract).then_inc(ready, 1)

            def split_weights(m, at):
                cols = 2 * pairs * P * KC
                pool.wait_ge(landed, (m + at + 1) * 32)
                if at:
                    pool.wait_ge(stacked, (m + at) * BATCH * N_PROJ * 2)
                nc.gpsimd.tensor_tensor(bias[:], bias_in[:], one[:].broadcast_to([P, 2 * pairs]), ALU.mult)
                lo = lo_rows[:].unsqueeze(2).broadcast_to([P, 2, pairs])
                by_which = lambda a: a[:].rearrange("p (w n) -> p w n", w=2)
                nc.gpsimd.tensor_tensor(by_which(bias_lo), by_which(bias_in), lo, ALU.mult)
                halve(w_in, [h[:].rearrange("p a n b -> p (a n b)") for h in w], w_ready, m + at + (3 if at else 2))
                pool.wait_ge(w_ready, m + at + 1)

            def out_operand(m, half, c, use):
                at = m * BATCH * chunks * 2 + (chunks * half + c) * 2
                pool.wait_ge(misc_free, m * USES + use + 2)
                nc.gpsimd.tensor_tensor(y_whole[:], o[:, c, :], factor[:], ALU.mult).then_inc(y_split, 1)
                pool.wait_ge(y_split, at + 1)
                nc.gpsimd.tensor_tensor(y[0][:], y_whole[:], one[:].broadcast_to([P, NB]), ALU.mult).then_inc(y_split, 1)
                pool.wait_ge(y_split, at + 2)
                nc.gpsimd.tensor_tensor(y[1][:], y_whole[:], f32(y[0][:]), ALU.subtract).then_inc(y_ready, 1)
                pool.wait_ge(y_ready, m * BATCH * chunks + chunks * half + c + 1 + chunks)

            def take_v(m, half):
                b = half % BATCH
                if half > 1:
                    pool.wait_ge(weighed, m * PASS + (half - 1) * HALF + SCORE_BANKS)
                nc.gpsimd.tensor_tensor(
                    v[b][:, :, :, 0:D1],
                    v_all[:, b * ST:(b + 1) * ST, bass.ds((m + half // BATCH) * HG * D1, HG * D1)].rearrange("p t (h d) -> p t h d", d=D1),
                    one[:].unsqueeze(2).unsqueeze(3).broadcast_to([P, ST, HG, D1]), ALU.mult).then_inc(v_ready, 1)
                pool.wait_ge(v_ready, m * BATCH + half + 1)

            def step(m, g):
                half, r = g // HALF, g % HALF
                if g >= 0 and r == 20 and half + 1 < STEPS // HALF:
                    take_v(m, half + 1)
                if g >= 0 and half % BATCH == 0 and half // BATCH + 1 < passes:
                    if r == 12:
                        pool.nop().then_inc(w_free, 1)
                    if r == 34:
                        split_weights(m, half // BATCH + 1)
                for n, (kind, half, c) in enumerate(misc_jobs(g)):
                    if kind == "sums":
                        pool.wait_ge(inverted, m * BATCH * chunks + half * chunks + c + 1)
                        nc.gpsimd.tensor_tensor(wide[:], over_sum[:].unsqueeze(2).broadcast_to([P, GT * HG, HEAD_ROWS]),
                                                one[:].unsqueeze(2).broadcast_to([P, GT * HG, HEAD_ROWS]), ALU.mult).then_inc(widened, 1)
                        pool.wait_ge(widened, m * BATCH * chunks + half * chunks + c + 1)
                    if kind == "project":
                        pool.wait_ge(misc_free, m * USES + first_use[g] + n + 2)
                        stack(pool, m, half, c)
                    if kind == "spread":
                        out_operand(m, half, c, first_use[g] + n)

            pool.wait_ge(consts, 112)
            halve(wv_in, [flat(h[:]) for h in wv], wv_ready, 1)
            split_weights(0, 0)
            halve(wp_in, [flat(h[:]) for h in wp], wp_ready, 3)
            pool.wait_ge(misc_free, V_USES + 1)
            take_v(0, 0)
            timeline(pool, step)

        @block.tensor
        def _(pe):
            def maxima_scores(m, n):
                u, (t, part) = n // UNIT, pieces[n % UNIT]
                b, h = place(u)
                rows = stack_rows(h)
                keys = slice(part * NB, min((part + 1) * NB, (t + 1) * P))
                bank = max_bank(n)[:, 0:keys.stop - keys.start]
                if part == 0 and t % GT == 0:
                    pe.wait_ge(stacked, m * BATCH * N_PROJ * 2 + (u // HG * N_PROJ + proj_jobs.index((h // 2, t // GT, 1)) + 1) * 2)
                pe.wait_ge(max_free, m * PASS + n + 1)
                own = keys.stop == (t + 1) * P
                mm = nc.tensor.matmul(bank, q[b][h][rows, t * P:(t + 1) * P], key[b][h][rows, keys], start=True, stop=not own)
                if own:
                    mm = nc.tensor.matmul(bank[:, -P:], ident_b[:], masks[:, 0, :], start=False, stop=True)
                mm.then_inc(max_full, 1)

            def scores(m, g):
                u, (c, kt) = g // UNIT, unit_steps[g % UNIT]
                b, h = place(u)
                q0 = max(0, kt - c * GT) * P
                if kt == 0:
                    pe.wait_ge(shifted, m * (PASS // UNIT * chunks) + u * chunks + c + 1)
                pe.wait_ge(exp_done, m * PASS + g + 1)
                mm = nc.tensor.matmul(score_bank(g)[:, q0:], key[b][h][:, kt * P:(kt + 1) * P],
                                      q[b][h][:, c * NB + q0:(c + 1) * NB], start=True, stop=kt < c * GT)
                if kt >= c * GT:
                    mm = nc.tensor.matmul(score_bank(g)[:, q0:q0 + P], ident_b[:], masks[:, 1, :], start=False, stop=True)
                mm.then_inc(scores_full, 1)

            def weigh_v(m, g):
                u, (c, kt) = g // UNIT, unit_steps[g % UNIT]
                b, h = place(u)
                q0 = max(0, kt - c * GT) * P
                if h == 0 and kt == 0:
                    pe.wait_ge(o_done, m * BATCH * chunks + u // HG * chunks + c + 1)
                    pe.wait_ge(v_ready, m * BATCH + u // HG + 1)
                pe.wait_ge(exp_done, m * PASS + g + 1 + SCORE_BANKS)
                nc.tensor.matmul(o_bank(c)[h * HEAD_ROWS:(h + 1) * HEAD_ROWS, q0:],
                                 v[b][:, kt, h, :], probT[:, g % SCORE_BANKS, q0:], start=kt == 0, stop=kt == (c + 1) * GT - 1).then_inc(weighed, 1)

            def project_qk(m, half, j, bank):
                pair, c, which = proj_jobs[j]
                at = half // BATCH
                pe.wait_ge(w_ready, m + at + 1)
                tokens = slice(half % BATCH * SEQ + c * NB, half % BATCH * SEQ + (c + 1) * NB)
                return project(nc, bank, lambda kt: [x[:, kt, which * pairs + pair, :] for x in w],
                               lambda kt: [x[:, kt, tokens] for x in k.xT])

            def shared(m, g):
                for n, (kind, at, c) in enumerate(misc_jobs(g)):
                    pe.wait_ge(misc_free, m * USES + first_use[g] + n + 1)
                    if kind == "project":
                        mm = project_qk(m, at, c, misc)
                    elif kind == "maxima":
                        _, h = place(at)
                        rows = shift_rows(h)
                        pe.wait_ge(shift_ready, m * (PASS // UNIT * chunks) + at * chunks + c + 1)
                        mm = nc.tensor.transpose(misc[0:rows.stop, 0:P], shift[:, h % 2, 0:rows.stop], k.ident[:])
                    elif kind == "sums":
                        pe.wait_ge(o_done, m * BATCH * chunks + at * chunks + c + 1 + chunks)
                        for t in range(GT):
                            mm = nc.tensor.matmul(misc[:, t * HG:(t + 1) * HG], o[:, c, t * P:(t + 1) * P], sum_rows[:],
                                                  start=True, stop=True)
                    elif kind == "spread":
                        pe.wait_ge(widened, m * BATCH * chunks + at * chunks + c + 1)
                        for t in range(GT):
                            mm = nc.tensor.matmul(
                                misc[:, t * P:(t + 1) * P],
                                wide[:, t * HG:(t + 1) * HG, :].rearrange("p h n -> p (h n)"), k.ident[:],
                                start=True, stop=True)
                    else:
                        pe.wait_ge(y_ready, m * BATCH * chunks + at * chunks + c + 1 + chunks)
                        for j in range(2):
                            t = 2 * int(kind == "out1") + j
                            mm = three_passes(nc, misc[:, j * C:(j + 1) * C], [x[:, t * P:(t + 1) * P] for x in y],
                                              [x[:, bass.ds(m + at // BATCH, 1), :].squeeze(1) for x in wp])
                    mm.then_inc(misc_full, 1)

            def step(m, g):
                if 0 <= g + LEAD_SCORES < STEPS:
                    scores(m, g + LEAD_SCORES)
                if g + LEAD_MAX < STEPS:
                    maxima_scores(m, g + LEAD_MAX)
                shared(m, g)
                if 0 <= g < STEPS:
                    weigh_v(m, g)

            pe.wait_ge(wv_ready, 1)
            for n in range(PROLOGUE_USES):
                if n >= 4:
                    pe.wait_ge(misc_free, n - 2)
                if n < V_USES:
                    for j in range(2):
                        t = 2 * n + j
                        mm = project(nc, prologue_bank(n)[:, j * C:(j + 1) * C], lambda kt: [x[:, kt, t * P:(t + 1) * P] for x in k.xT],
                                     lambda kt: [x[:, kt, :] for x in wv])
                else:
                    mm = project_qk(0, 0, n - V_USES, prologue_bank(n))
                mm.then_inc(misc_full, 1)
            pe.wait_ge(prepared, 1)
            pe.wait_ge(wp_ready, 1)
            timeline(pe, step)

        @block.scalar
        def _(act):
            for _ in range(SCORE_BANKS):
                act.nop().then_inc(exp_done, 1)
            for _ in range(chunks):
                act.nop().then_inc(o_done, 1)

            def take_projection(m, half, j, bank, full):
                pair, c, which = proj_jobs[j]
                n = which * pairs + pair
                if half or j >= 2:
                    act.wait_ge(stacked, m * BATCH * N_PROJ * 2 + (half * N_PROJ + j - 1) * 2)
                act.wait_ge(misc_full, full)
                nc.scalar.activation(only_hi[:, j % 2, :], bank, ACT.Identity, bias=bias_lo[:, n:n + 1],
                                     scale=lo_rows[:, which:which + 1])
                nc.scalar.activation(projected[:, j % 2, :], bank, ACT.Identity, bias=bias[:, n:n + 1]).then_inc(misc_free, 1)

            def exp(m, g):
                c, kt = unit_steps[g % UNIT]
                q0 = max(0, kt - c * GT) * P
                act.wait_ge(weighed, m * PASS + g + 1)
                act.wait_ge(scores_full, m * PASS + g + 1)
                nc.scalar.activation(probT[:, g % SCORE_BANKS, q0:], score_bank(g)[:, q0:], ACT.Exp,
                                     scale=float(D1) ** -0.5).then_inc(exp_done, 1)

            def copy_o(m, half, c):
                act.wait_ge(y_ready, m * BATCH * chunks + half * chunks + c + 1)
                if c == 0:
                    act.wait_ge(w_ready, m + min(half // BATCH + 2, passes))
                last = half * HALF + (HG - 1) * UNIT + unit_steps.index((c, (c + 1) * GT - 1))
                act.wait_ge(weighed, m * PASS + last + 1 + SCORE_BANKS)
                nc.scalar.activation(o[:, c, :], o_bank(c), ACT.Copy).then_inc(o_done, 1)

            def step(m, g):
                half, r = g // HALF, g % HALF
                if 0 <= g + LEAD_SCORES < STEPS:
                    exp(m, g + LEAD_SCORES)
                if 0 <= g < STEPS and r == HALF - GT * chunks:
                    copy_o(m, half, 0)
                if g > 0 and r == 0:
                    copy_o(m, half - 1, 1)
                for n, (kind, at, j) in enumerate(misc_jobs(g)):
                    if kind == "project":
                        take_projection(m, at, j, misc, m * USES + first_use[g] + n + 1)
                    if kind == "spread":
                        act.wait_ge(misc_full, m * USES + first_use[g] + n + 1)
                        nc.scalar.activation(factor[:], misc, ACT.Copy).then_inc(misc_free, 1)

            for _ in range(SCORE_BANKS):
                act.nop().then_inc(weighed, 1)
            act.wait_ge(consts, 112)
            act.wait_ge(w_ready, 1)
            act.wait_ge(misc_free, V_USES + 1)
            for j in range(N_PROJ):
                take_projection(0, 0, j, prologue_bank(V_USES + j), V_USES + j + 1)
            timeline(act, step)

        @block.vector
        def _(dve):
            for _ in range(2):
                dve.nop().then_inc(max_free, 1)
            dve.nop().then_inc(misc_free, 1)

            def take_max(m, n):
                u, (t, part) = n // UNIT, pieces[n % UNIT]
                width = min(NB, (t + 1) * P - part * NB)
                dve.wait_ge(max_full, m * PASS + n + 1)
                nc.vector.tensor_reduce(peaks[:, u % 2, n % UNIT:n % UNIT + 1], max_bank(n)[:, 0:width], AX.X, ALU.max,
                                        negate=True).then_inc(max_free, 1)
                if n % UNIT in last_piece:
                    c = last_piece.index(n % UNIT)
                    _, h = place(u)
                    rows = shift_rows(h)
                    hi, lo = (shift[:, h % 2, rows.start + i * GT:rows.start + (i + 1) * GT] for i in range(2))
                    dve.wait_ge(max_free, m * PASS + n + 3)
                    least = peaks[:, u % 2, 0:GT]
                    if c == 1:
                        first, second = (peaks[:, u % 2, GT + i:UNIT:2] for i in range(2))
                        least = peak[:]
                        nc.vector.tensor_tensor(least, first, second, ALU.min).then_inc(peak_done, 1)
                        dve.wait_ge(peak_done, m * (PASS // UNIT * 3) + u * 3 + 2)
                    nc.vector.tensor_copy(hi.bitcast(F32R), least).then_inc(peak_done, 1)
                    dve.wait_ge(peak_done, m * (PASS // UNIT * 3) + u * 3 + 2 * c + 1)
                    nc.vector.tensor_tensor(lo, least, hi, ALU.subtract).then_inc(shift_ready, 1)

            def shared(m, g):
                for n, (kind, at, c) in enumerate(misc_jobs(g)):
                    if kind in ("spread", "project"):
                        continue
                    dve.wait_ge(misc_full, m * USES + first_use[g] + n + 1)
                    if kind == "maxima":
                        b, h = place(at)
                        rows = shift_rows(h)
                        nc.vector.tensor_tensor(
                            q[b][h][rows, chunk(c)].rearrange("p (t n) -> p t n", n=P),
                            misc[rows, 0:P].unsqueeze(1).broadcast_to([N_SHIFT, GT, P]), tile_rows[rows], ALU.mult).then_inc(shifted, 1)
                        dve.wait_ge(shifted, m * (PASS // UNIT * chunks) + at * chunks + c + 1)
                        dve.nop().then_inc(misc_free, 1)
                    elif kind == "sums":
                        nc.vector.reciprocal(over_sum[:], misc[:, 0:GT * HG]).then_inc(inverted, 1)
                        dve.wait_ge(inverted, m * BATCH * chunks + at * chunks + c + 1)
                        dve.nop().then_inc(misc_free, 1)
                    else:
                        t = at % BATCH * ST + c * GT + 2 * int(kind == "out1")
                        nc.vector.tensor_tensor(k.acc[:, t:t + 2, :], k.acc[:, t:t + 2, :],
                                                misc.rearrange("p (t n) -> p t n", n=C), ALU.add).then_inc(misc_free, 1)

            def step(m, g):
                if g + LEAD_MAX < STEPS:
                    take_max(m, g + LEAD_MAX)
                shared(m, g)

            nc.vector.memset(k.acc[:], 0.0)
            for b in range(BATCH):
                nc.vector.memset(v[b][:, :, :, D1:], 1.0)
            nc.vector.memset(shift[:], 0.0)
            for b in range(BATCH):
                for h in range(HG):
                    nc.vector.memset(f32(q[b][h][other_rows(h)]), 0.0)
                    done = nc.vector.memset(f32(key[b][h][other_rows(h)]), 0.0)
            done.then_inc(zeroed, 1)
            dve.wait_ge(zeroed, 1)
            for b in range(BATCH):
                for h in range(HG):
                    nc.vector.memset(f32(key[b][h][shift_rows(h)]), 1.0)
            dve.wait_ge(consts, 112)
            nc.vector.tensor_copy(masks[:], masks_in)
            nc.vector.tensor_copy(ident_b[:], k.ident[:]).then_inc(prepared, 1)
            for n in range(PROLOGUE_USES):
                if n < V_USES:
                    dve.wait_ge(misc_full, n + 1)
                    nc.vector.tensor_tensor(
                        v_all[:, 2 * n:2 * n + 2, :], prologue_bank(n).rearrange("p (t n) -> p t n", t=2),
                        bias_v[:].unsqueeze(1).broadcast_to([P, 2, C]),
                        ALU.add).then_inc(misc_free, 1)
                else:
                    dve.wait_ge(misc_free, n + 2)
                    stack(dve, 0, 0, n - V_USES)
            timeline(dve, step)


def build(nc, ins, out):
    with ExitStack() as ctx:
        k = Core()
        def sb(n, s, d=F32):
            return ctx.enter_context(nc.sbuf_tensor(n, s, d))
        k.x_dram = ins["x"]
        k.acc = sb("acc_sb", [P, TT, C])
        k.xT = [sb(f"xT_{h}", [P, KC, TOK], F32R) for h in ("hi", "lo")]
        k.ident = sb("ident_sb", [P, P])
        k.psum = ctx.enter_context(nc.psum_tensor("psum", [P, 8, NB], F32))
        consts = ctx.enter_context(nc.semaphore("consts"))
        with nc.Block() as block:
            @block.sync
            def _(sp):
                sp.dma_start(k.ident[:], ins["ident"]).then_inc(consts, 16)
                sp.wait_ge(consts, 16)
        with nc.sbuf_tensor("x_first", [P, TT, C], F32) as k.x:
            norm_stage(nc, k, "norm0", sublayer=False, load=True)
        attention0_stage(nc, k, "attn0", ins)
        k.x = sb("x_sb", [P, TT, C])
        norm_stage(nc, k, "norm1", load=True, post=(ins["bo"], ALU.add))
        mlp_stage(nc, k, "mlp0", ins["ffn0_w"], N_FFN0, hidden_scales=ins["ffn0_scales"])
        norm_stage(nc, k, "norm2", post=(ins["down_s"], ALU.mult))
        attention1_stage(nc, k, "attn1", ins)
        weigh = sb("weigh", [P, (N_EXPERT + N_SHARED) * TT])
        norm_stage(nc, k, "norm3", post=(ins["b_proj"], ALU.add))
        route_stage(nc, k, "route", ins["router"], weigh)
        mlp_stage(nc, k, "moe", ins["moe_w"], N_EXPERT + N_SHARED, weigh=weigh)
        norm_stage(nc, k, "norm4", following=False, out=out)


def kernel(**inputs):
    import numpy as np
    import concourse.bacc as bacc
    from concourse.bass_utils import run_bass_kernel_spmd

    given = {n: np.asarray(a) for n, a in inputs.items()}
    l0 = {n[len("L0_attn_"):]: a for n, a in given.items() if n.startswith("L0_attn_")}

    def chunks(gate, up, down):
        cut = [a.reshape(KC, P, -1, IM).transpose(2, 1, 0, 3).reshape(-1, P, KC * IM) for a in (gate, up)]
        return np.concatenate([*cut, down.reshape(-1, IM, C)], axis=2)

    def pad_hidden(a):
        return np.pad(a, [(0, N_FFN0 * IM - INTER0)] + [(0, 0)] * (a.ndim - 1))

    def stacked(a):
        heads = a.reshape(*a.shape[:-1], H1, D1)
        rows = np.concatenate([heads] * 3 + [np.zeros_like(heads)], axis=-1)
        return rows.reshape(*a.shape[:-1], H1 // HG, HG // 2, P)

    arrays = {"x": l0["x"].reshape(TOK, C)}
    for n in "qkvo":
        arrays[f"w{n}_codes"], arrays[f"w{n}_scales"] = l0[f"w{n}_codes"], l0[f"w{n}_scales"]
    for n in "qk":
        arrays[f"b{n}"] = l0[f"b{n}"].reshape(H0, D0).T
    arrays["bv"], arrays["bo"] = l0["bv"], l0["bo"]
    arrays["ffn0_w"] = chunks(*(pad_hidden(given[f"L0_ffn_{n}_w"]).T for n in ("gate", "up")),
                              pad_hidden(given["L0_ffn_down_w"].T))
    arrays["ffn0_scales"] = np.stack([pad_hidden(given[f"L0_ffn_{n}_s"]).reshape(N_FFN0, IM).T for n in ("gate", "up")])
    arrays["down_s"] = given["L0_ffn_down_s"]

    w_attn, b_attn = given["L1_attn_w_attn"], given["L1_attn_b_attn"]
    qk = np.stack([stacked(w_attn[:, i * C:(i + 1) * C]) for i in range(2)], axis=2)
    arrays["w_attn"] = qk.reshape(KC, P, H1 // HG, HG, P).transpose(2, 1, 0, 3, 4).reshape(H1 // HG, P, -1)
    b_qk = np.stack([stacked(b_attn[i * C:(i + 1) * C]) for i in range(2)], axis=1)
    arrays["b_qk"] = b_qk.reshape(H1 // HG, HG, P).transpose(0, 2, 1)
    arrays["w_v"] = w_attn[:, 2 * C:].reshape(KC, P, C).transpose(1, 0, 2).reshape(P, KC * C)
    arrays["b_v"] = b_attn[2 * C:]
    w_proj = given["L1_attn_w_proj"].reshape(H1 // HG, HG, D1, C)
    w_proj = np.pad(w_proj, [(0, 0), (0, 0), (0, HEAD_ROWS - D1), (0, 0)])
    arrays["w_proj"] = w_proj.reshape(H1 // HG, P, C).transpose(1, 0, 2).reshape(P, -1)
    arrays["b_proj"] = given["L1_attn_b_proj"]

    arrays["router"] = given["L1_ffn_gate_w"].T.reshape(KC, P, N_EXPERT).transpose(1, 0, 2)
    side_by_side = lambda a: a.transpose(1, 0, 2).reshape(C, N_EXPERT * IM)
    arrays["moe_w"] = np.concatenate([
        chunks(side_by_side(given["L1_ffn_Wg"]), side_by_side(given["L1_ffn_Wu"]),
               given["L1_ffn_Wd"].reshape(N_EXPERT * IM, C)),
        chunks(given["L1_ffn_sWg"], given["L1_ffn_sWu"], given["L1_ffn_sWd"])])

    arrays["ident"] = np.eye(P, dtype=np.float32)
    later = np.full((P, P), -1e30, np.float32)
    arrays["masks"] = np.stack([np.triu(later, 1), np.tril(later, -1)], axis=1)
    part = np.arange(P) % STACK // D1
    arrays["lo_rows"] = np.stack([part == 1, part == 2], axis=-1).astype(np.float32)
    own_tile = np.tile(np.repeat(np.eye(GT, dtype=np.float32), P, axis=1), (2, 1)).reshape(2 * GT, GT, P)
    arrays["tile_rows"] = np.zeros((P, GT, P), np.float32)
    for start in (0, STACK):
        arrays["tile_rows"][start:start + 2 * GT] = own_tile
    sum_row = np.arange(HG) * HEAD_ROWS + D1
    arrays["sum_rows"] = (np.arange(P)[:, None] == sum_row).astype(np.float32)

    nc = bacc.Bacc("TRN2", target_bir_lowering=False, num_devices=1)
    arrays = {f"in_{n}": np.ascontiguousarray(a) for n, a in arrays.items()}
    aps = {n[3:]: nc.dram_tensor(n, a.shape, mybir.dt.from_np(a.dtype), kind="ExternalInput").ap()
           for n, a in arrays.items()}
    out = nc.dram_tensor("out", (TOK, C), F32, kind="ExternalOutput").ap()
    build(nc, aps, out)
    result = run_bass_kernel_spmd(nc, [arrays], core_ids=[0])
    return result.results[0]["out"].reshape(BATCH, SEQ, C)
```

```python
from contextlib import ExitStack

import concourse.bass as bass
from concourse import mybir

F32 = mybir.dt.float32
F32R = mybir.dt.float32r
F16 = mybir.dt.float16
BF16 = mybir.dt.bfloat16
ALU = mybir.AluOpType
ACT = mybir.ActivationFunctionType
AX = mybir.AxisListType

P = 128
BATCH, SEQ, C = 2, 1024, 256
TOK = BATCH * SEQ
TT = TOK // P
KC = C // P
NB = 512
GT = NB // P
EPS = 1e-5

H0, D0 = 16, 128
FP4_BLOCK = 32
H1, D1 = 16, 16
D1P = 32
IM = 128
INTER0 = 704
N_FFN0 = -(-INTER0 // IM)
N_EXPERT, N_TOP, N_SHARED = 16, 8, 2
ROUTE_SCALE = 2.5

PASSES = ((0, 0), (0, 1), (1, 0))


class Count:

    def __init__(self, sem, base=0):
        self.sem, self.base, self.n = sem, base, 0

    def inc(self, ins):
        ins.then_inc(self.sem, 1)
        self.n += 1

    def wait(self, eng):
        eng.wait_ge(self.sem, self.base + self.n)

    def step(self, eng, ins):
        self.inc(ins)
        self.wait(eng)


class Core:
    pass


class Stage:

    def __init__(self, nc, ctx, name):
        self.nc, self.ctx, self.name = nc, ctx, name

    def sb(self, n, shape, dt=F32):
        return self.ctx.enter_context(self.nc.sbuf_tensor(f"{self.name}_{n}", shape, dt))

    def halves(self, n, shape):
        return [self.sb(f"{n}_{h}", shape, F32R) for h in ("hi", "lo")]

    def sem(self, n):
        return self.ctx.enter_context(self.nc.semaphore(f"{self.name}_{n}"))


def three_passes(nc, out, stationary, moving, start=True, stop=True):
    for n, (s, m) in enumerate(PASSES):
        ins = nc.tensor.matmul(out, stationary[s], moving[m], start=start and n == 0,
                               stop=stop and n == len(PASSES) - 1)
    return ins


def project(nc, out, stationary, moving):
    for kt in range(KC):
        ins = three_passes(nc, out, stationary(kt), moving(kt), start=kt == 0, stop=kt == KC - 1)
    return ins


class Program:

    def __init__(self, sync, tensor, scalar, vector, gpsimd):
        self.sync, self.tensor, self.scalar, self.vector, self.gpsimd = sync, tensor, scalar, vector, gpsimd


def nothing(eng):
    pass


def run_block(nc, *programs):
    with nc.Block() as block:
        @block.sync
        def _(sp):
            for p in programs:
                p.sync(sp)

        @block.gpsimd
        def _(pool):
            for p in programs:
                p.gpsimd(pool)

        @block.tensor
        def _(pe):
            for p in programs:
                p.tensor(pe)

        @block.scalar
        def _(act):
            for p in programs:
                p.scalar(act)

        @block.vector
        def _(dve):
            for p in programs:
                p.vector(dve)


class Norm:

    groups = TT // GT
    sizes = dict(stats=TT * 6, mean_var=TT * 2, power=GT, veps=TT, neg_mean=TT, rstd=TT, offset=TT)

    def __init__(self, nc, ctx, k, name, *, x=None, load=False, out=None, bank=0, room, ahead=0):
        self.nc, self.k, self.x, self.load, self.out, self.bank = nc, k, x, load or x is None, out, bank
        self.ahead, self.meanwhile = ahead, nothing
        self.done = dict(gpsimd=ahead, scalar=ahead, vector=ahead)
        self.scalings = 0
        self.lag = 0 if x is None else 2
        st = Stage(nc, ctx, name)
        small, at = {}, 0
        for n, size in self.sizes.items():
            small[n] = room[:, at:at + size]
            at += size
        self.stats = small["stats"].rearrange("p (t n) -> p t n", t=TT)
        self.mean_var = small["mean_var"].rearrange("p (t n) -> p t n", t=TT)
        self.power, self.veps, self.neg_mean, self.rstd = (small[n] for n in ("power", "veps", "neg_mean", "rstd"))
        self.offset = small["offset"]
        self.loaded = [st.sem(f"loaded{g}") for g in range(self.groups if self.load else 0)]
        self.own, self.power_set, self.pool_own = (st.sem(n) for n in ("own", "power_set", "pool_own"))
        if x is not None:
            self.acc_stats, self.acc_ready, self.acc_normed = (st.sem(n) for n in ("acc_stats", "acc_ready", "acc_normed"))
        if out is None:
            self.x_stats, self.x_ready, self.x_normed = (st.sem(n) for n in ("x_stats", "x_ready", "x_normed"))
            self.turned, self.hi_done, self.lo_done = (st.sem(n) for n in ("turned", "hi_done", "lo_done"))
        else:
            self.x_final, self.stored = st.sem("x_final"), st.sem("stored")
        self.link = Count(self.own)

    def tiles(self, g):
        return range(g * GT, (g + 1) * GT)

    def part(self, a, g):
        return a[:, g * GT:(g + 1) * GT, :]

    def load_x(self, sp, g):
        rows = self.k.x_dram.rearrange("(g t p) c -> g p t c", t=GT, p=P)
        sp.dma_start(self.part(self.k.acc if self.x is None else self.x, g), rows[g]).then_inc(self.loaded[g], 16)

    def sync(self, sp):
        if self.load:
            for g in range(self.ahead, self.groups):
                self.load_x(sp, g)
        if self.out is not None:
            rows = self.out.rearrange("(g t p) c -> g p t c", t=GT, p=P)
            for g in range(self.groups):
                sp.wait_ge(self.x_final, g + 1)
                sp.dma_start(rows[g], self.part(self.x, g)).then_inc(self.stored, 16)
            sp.wait_ge(self.stored, 16 * self.groups)

    def last_groups(self):
        return range(max(self.ahead, self.groups - self.lag), self.groups)

    def scale_and_offset(self, pool, g, stats, ready):
        n = self.scalings
        self.scalings += 1
        cols = slice(g * GT, (g + 1) * GT)
        pool.wait_ge(stats, g + 1)
        self.nc.gpsimd.tensor_tensor(self.rstd[:, cols], self.veps[:, cols], self.power, ALU.pow).then_inc(self.pool_own, 1)
        pool.wait_ge(self.pool_own, n + 1)
        self.nc.gpsimd.tensor_tensor(self.offset[:, cols], self.neg_mean[:, cols], self.rstd[:, cols], ALU.mult).then_inc(ready, 1)

    def early_gpsimd(self, pool, g):
        if self.x is not None:
            self.scale_and_offset(pool, g, self.acc_stats, self.acc_ready)
        if g >= self.ahead + self.lag:
            self.scale_x(pool, g - self.lag)

    def scale_x(self, pool, g):
        if self.out is None:
            self.scale_and_offset(pool, g, self.x_stats, self.x_ready)

    def prepare(self, pool):
        self.nc.gpsimd.memset(self.power, -0.5).then_inc(self.power_set, 1)
        pool.wait_ge(self.power_set, 1)

    def gpsimd(self, pool):
        if not self.done["gpsimd"]:
            self.prepare(pool)
        for g in range(self.done["gpsimd"], self.groups):
            self.early_gpsimd(pool, g)
        for g in self.last_groups():
            self.scale_x(pool, g)

    def statistics(self, dve, src, g, ready):
        nc, link = self.nc, self.link
        for t in self.tiles(g):
            link.inc(nc.vector.bn_stats(self.stats[:, t, :], src[:, t, :]))
        link.wait(dve)
        for t in self.tiles(g):
            link.inc(nc.vector.bn_aggr(self.mean_var[:, t, :], self.stats[:, t, :]))
        link.wait(dve)
        cols = slice(g * GT, (g + 1) * GT)
        nc.vector.tensor_scalar(self.neg_mean[:, cols], self.mean_var[:, cols, 0], -1.0, None, ALU.mult)
        nc.vector.tensor_scalar(self.veps[:, cols], self.mean_var[:, cols, 1], EPS, None, ALU.add).then_inc(ready, 1)

    def normalise(self, src, g, done):
        for t in self.tiles(g):
            ins = self.nc.scalar.activation(self.k.acc[:, t, :], src[:, t, :], ACT.Identity, bias=self.offset[:, t:t + 1],
                                            scale=self.rstd[:, t:t + 1])
        ins.then_inc(done, 1)

    def add_up(self, dve, g):
        if self.load:
            dve.wait_ge(self.loaded[g], 16)
        if self.x is None:
            self.statistics(dve, self.k.acc, g, self.x_stats)
            return
        dve.wait_ge(self.acc_normed, g + 1)
        x = self.part(self.x, g)
        ins = self.nc.vector.tensor_tensor(x, x, self.part(self.k.acc, g), ALU.add)
        if self.out is not None:
            ins.then_inc(self.x_final, 1)
        else:
            self.link.step(dve, ins)
            self.statistics(dve, self.x, g, self.x_stats)

    def early_vector(self, dve, g):
        if self.x is not None:
            self.statistics(dve, self.k.acc, g, self.acc_stats)
        if g >= self.ahead + self.lag:
            self.add_up(dve, g - self.lag)

    def early_scalar(self, act, g):
        if self.x is not None:
            act.wait_ge(self.acc_ready, g + 1)
            self.normalise(self.k.acc, g, self.acc_normed)
        if g >= self.ahead + self.lag:
            self.normalise_x(act, g - self.lag)

    def normalise_x(self, act, g):
        if self.out is None:
            act.wait_ge(self.x_ready, g + 1)
            self.normalise(self.k.acc if self.x is None else self.x, g, self.x_normed)

    def banks(self, g):
        return self.k.psum[:, self.bank + g % 2 * KC:self.bank + (g % 2 + 1) * KC, :]

    def take_hi(self, act, g):
        if self.out is None:
            act.wait_ge(self.turned, g + 1)
            self.nc.scalar.activation(self.k.xT[0][:, :, g * NB:(g + 1) * NB], self.banks(g), ACT.Copy).then_inc(self.hi_done, 1)

    def take_lo(self, dve, g):
        if self.out is None:
            dve.wait_ge(self.hi_done, g + 1)
            hi, lo = (h[:, :, g * NB:(g + 1) * NB] for h in self.k.xT)
            self.nc.vector.tensor_tensor(lo, self.banks(g), hi.bitcast(F32), ALU.subtract).then_inc(self.lo_done, 1)

    def turn(self, pe, g):
        pe.wait_ge(self.x_normed, g + 1)
        if g >= 2:
            pe.wait_ge(self.lo_done, g - 1)
        for kt in range(KC):
            for j, t in enumerate(self.tiles(g)):
                ins = self.nc.tensor.transpose(self.banks(g)[:, kt, j * P:(j + 1) * P],
                                               self.k.acc[:, t, kt * P:(kt + 1) * P], self.k.ident[:])
        ins.then_inc(self.turned, 1)

    def tensor(self, pe):
        if self.out is None:
            for g in range(self.groups):
                if g and g == self.ahead:
                    self.meanwhile(pe)
                self.turn(pe, g)

    def rest_of_acc(self, dve):
        for g in range(self.done["vector"], self.groups):
            self.early_vector(dve, g)
        self.done["vector"] = self.groups

    def rest(self):
        return Program(nothing, nothing, nothing, self.rest_of_acc, nothing)

    def scalar(self, act):
        for g in range(self.ahead):
            self.take_hi(act, g)
        for g in range(self.done["scalar"], self.groups):
            self.early_scalar(act, g)
        for g in self.last_groups():
            self.normalise_x(act, g)
        for g in range(self.ahead, self.groups):
            self.take_hi(act, g)

    def vector(self, dve):
        for g in range(self.ahead):
            self.take_lo(dve, g)
        for g in range(self.done["vector"], self.groups):
            self.early_vector(dve, g)
        for g in self.last_groups():
            self.add_up(dve, g)
        for g in range(self.ahead, self.groups):
            self.take_lo(dve, g)


HP = 2
WQKV = 3 * KC * HP * D0
WO = HP * C
ST = SEQ // P
QG = ST // GT


def attention0_stage(nc, k, name, ins, after):
    scale = float(D0) ** -0.5
    tiles = HP * ST
    groups = tiles // GT
    qk_uses, v_uses = HP * 2 * SEQ // NB, ST * HP * D0 // NB
    uses = qk_uses + 2 * tiles
    passes = H0 // HP
    scale_rows = FP4_BLOCK
    with ExitStack() as ctx:
        st = Stage(nc, ctx, name)
        staged = k.x[:].rearrange("p t c -> p (t c)")
        codes, scales = staged[:, 0:WQKV + WO], staged[:, WQKV + WO:]
        scale_row, one = st.sb("scale_row", [P, 1]), st.sb("one", [P, 1])
        bias_in = st.sb("bias_in", [P, 2 * HP])
        bias_qk = st.sb("bias_qk", [P, 2 * HP])
        bias_v_in = st.sb("bias_v_in", [P, HP * D0])
        bias_v = st.sb("bias_v", [P, HP * D0])
        bias_o_in, ident_in = st.sem("bias_o_in"), st.sem("ident_in")
        w = st.halves("w", [P, 3, KC, HP * D0])
        wo = st.halves("wo", [P, HP, C])
        q = st.halves("q", [P, HP, SEQ])
        key = st.halves("key", [P, HP, SEQ])
        v = st.halves("v", [P, ST, HP * D0])
        prob = st.sb("prob", [P, 2, SEQ])
        v_whole = scales[:, 0:2 * NB].rearrange("p (a n) -> p a n", a=2)
        norm = Norm(nc, ctx, k, "norm0", room=prob[:, 0, :])
        bias_o = prob[:, 1, 0:C]
        probT = st.halves("probT", [P, 2, ST, NB])
        o = st.halves("o", [P, NB])
        neg_max = st.sb("neg_max", [P, 2])
        total = st.sb("total", [P, tiles])
        over_total = st.sb("over_total", [P, tiles])
        landed, staged_free, w_ready, wo_ready = (st.sem(n) for n in ("landed", "staged_free", "w_ready", "wo_ready"))
        ring_full, ring_hi, ring_free = (st.sem(n) for n in ("ring_full", "ring_hi", "ring_free"))
        scale_set = st.sem("scale_set")
        v_full, v_taken, v_hi_done, v_done = (st.sem(n) for n in ("v_full", "v_taken", "v_hi_done", "v_done"))
        score_full, max_ready, exp_done = (st.sem(n) for n in ("score_full", "max_ready", "exp_done"))
        o_full, o_hi_done, o_done = (st.sem(n) for n in ("o_full", "o_hi_done", "o_done"))
        out_full, out_done, own, split = (st.sem(n) for n in ("out_full", "out_done", "own", "split"))
        block = ctx.enter_context(nc.Block())

        ring = lambda n: k.psum[:, 4 + n % 2, :]
        scores = lambda i: k.psum[:, i % 2 * 2:i % 2 * 2 + 2, :]
        o_bank = lambda g: k.psum[:, 0 if g == groups - 1 else 6, :]
        out_bank = k.psum[:, 7, :]
        v_bank = lambda n: k.psum[:, 6 + n % 2, :]
        qk_bank = lambda n: k.psum[:, 4 + n % 3, :]
        turn_use = lambda i, half: qk_uses + 2 * i + half

        def qk_chunk(n):
            return n // (SEQ // NB) % 2, n // (2 * SEQ // NB), n % (SEQ // NB)

        OUT_AT = (2, 4)
        NORM_ACC_DVE, NORM_ACC_ACT, NORM_X_DVE, NORM_X_ACT = (2, 4), (9, 10), (11, 12), (13, 14)

        def halves(eng, projections, attend, begin_norm=None):
            projections(0, 0, first=True)
            with eng.Fori(0, passes - 1) as m:
                for b in range(BATCH):
                    attend(m, b)
                    projections(m, b + 1)
            attend(passes - 1, 0)
            projections(passes - 1, 1)
            attend(passes - 1, 1, begin_norm)

        @block.sync
        def _(sp):
            def load(m):
                at = m * HP * D0
                part = bass.ds(at, HP * D0)
                n = 0
                for which, x in enumerate("qkv"):
                    to = slice(which * KC * HP * D0, (which + 1) * KC * HP * D0)
                    sp.dma_start(codes[:, to].rearrange("p (k n) -> p k n", k=KC),
                                 ins[f"w{x}_codes"].rearrange("(k p) n -> p k n", p=P)[:, :, part]).then_inc(landed, 16)
                    rows = ins[f"w{x}_scales"].rearrange("(k b) n -> b k n", k=KC)
                    for b in range(P // scale_rows):
                        sp.dma_start(scales[b * scale_rows:(b + 1) * scale_rows, to].rearrange("p (k n) -> p k n", k=KC),
                                     rows[b:b + 1, :, part].squeeze(0).partition_broadcast(scale_rows)).then_inc(landed, 16)
                        n += 1
                    n += 1
                sp.dma_start(codes[:, WQKV:].rearrange("p (h n) -> p h n", h=HP),
                             ins["wo_codes"].rearrange("(h p) n -> p h n", p=P)[:, bass.ds(m * HP, HP), :]).then_inc(landed, 16)
                rows = ins["wo_scales"].rearrange("(h b) n -> b h n", b=P // scale_rows)
                for b in range(P // scale_rows):
                    sp.dma_start(scales[b * scale_rows:(b + 1) * scale_rows, WQKV:].rearrange("p (h n) -> p h n", h=HP),
                                 rows[b:b + 1, bass.ds(m * HP, HP), :].squeeze(0).partition_broadcast(scale_rows)).then_inc(landed, 16)
                for which, x in enumerate("qk"):
                    sp.dma_start(bias_in[:, which * HP:(which + 1) * HP],
                                 ins[f"b{x}"][:, bass.ds(m * HP, HP)]).then_inc(landed, 16)
                sp.dma_start(bias_v_in[:], ins["bv"][part].partition_broadcast(P)).then_inc(landed, 16)

            norm.sync(sp)
            sp.dma_start(k.ident[:], ins["ident"]).then_inc(ident_in, 16)
            sp.dma_start(bias_o, ins["bo"].partition_broadcast(P)).then_inc(bias_o_in, 16)
            with sp.Fori(0, passes) as m:
                sp.wait_ge(staged_free, m + 1)
                load(m)
            sp.wait_ge(staged_free, passes + 1)
            for g in range(after.ahead):
                after.load_x(sp, g)
        loads = 16 * (3 * (1 + P // scale_rows) + 1 + P // scale_rows + 2 + 1)

        @block.gpsimd
        def _(pool):
            pool.nop().then_inc(staged_free, 1)
            norm.gpsimd(pool)
            nc.gpsimd.memset(scale_row[:], scale).then_inc(scale_set, 1)
            nc.gpsimd.memset(one[:], 1.0).then_inc(scale_set, 1)
            pool.wait_ge(scale_set, 2)
            for _ in range(2):
                pool.nop().then_inc(v_done, 1)

            def split_weights(m, first=False):
                pool.wait_ge(landed, (m + 1) * loads)
                flat = lambda t: t[:].rearrange("p a b c -> p (a b c)")
                nq = KC * HP * D0
                n = m * 5
                nc.gpsimd.tensor_tensor(scales[:, 0:nq], scales[:, 0:nq], scale_row[:].broadcast_to([P, nq]), ALU.mult).then_inc(split, 1)
                nc.gpsimd.tensor_scalar(bias_in[:, 0:HP], bias_in[:, 0:HP], scale, 1.0, ALU.mult, ALU.mult).then_inc(split, 1)
                pool.wait_ge(split, n + 2)
                if not first:
                    pool.wait_ge(v_full, 2 * m * v_uses)
                nc.gpsimd.tensor_tensor(flat(w[0]), codes[:, 0:WQKV], scales[:, 0:WQKV], ALU.mult).then_inc(split, 1)
                nc.gpsimd.tensor_scalar(bias_qk[:], bias_in[:], 1.0, 1.0, ALU.mult, ALU.mult)
                nc.gpsimd.tensor_scalar(bias_v[:], bias_v_in[:], 1.0, 1.0, ALU.mult, ALU.mult)
                pool.wait_ge(split, n + 3)
                nc.gpsimd.tensor_tensor(codes, codes, scales, ALU.mult).then_inc(split, 1)
                pool.wait_ge(split, n + 4)
                nc.gpsimd.tensor_tensor(flat(w[1]), codes[:, 0:WQKV], flat(w[0]).bitcast(F32), ALU.subtract).then_inc(w_ready, 1)
                if not first:
                    pool.wait_ge(out_full, 2 * groups * 2 * m)
                wo_hi, wo_lo = (h[:].rearrange("p a b -> p (a b)") for h in wo)
                nc.gpsimd.tensor_tensor(wo_hi, codes[:, WQKV:], one[:].broadcast_to([P, WO]), ALU.mult).then_inc(split, 1)
                pool.wait_ge(split, n + 5)
                nc.gpsimd.tensor_tensor(wo_lo, codes[:, WQKV:], f32(wo_hi), ALU.subtract).then_inc(wo_ready, 1)

            def v_lo(m):
                for half in range(2):
                    for n in range(v_uses):
                        use = (m * 2 + half) * v_uses + n
                        pool.wait_ge(v_hi_done, use + 1)
                        to = slice(n * GT // HP, (n + 1) * GT // HP)
                        nc.gpsimd.tensor_tensor(v[1][:, to, :].rearrange("p t d -> p (t d)"), v_whole[:, n % 2, :],
                                                v[0][:, to, :].rearrange("p t d -> p (t d)").bitcast(F32),
                                                ALU.subtract).then_inc(v_done, 1)

            split_weights(0, first=True)
            with pool.Fori(0, passes - 1) as m:
                v_lo(m)
                pool.wait_ge(wo_ready, m + 1)
                pool.wait_ge(v_done, (m + 1) * 2 * v_uses + 2)
                pool.nop().then_inc(staged_free, 1)
                split_weights(m + 1)
            pool.wait_ge(wo_ready, passes)
            pool.nop().then_inc(staged_free, 1)
            v_lo(passes - 1)
            after.prepare(pool)
            for g in range(after.ahead):
                after.early_gpsimd(pool, g)
            for g in range(after.ahead):
                after.scale_x(pool, g)
            after.early_gpsimd(pool, after.ahead)
            after.done["gpsimd"] = after.ahead + 1

        @block.tensor
        def _(pe):
            def take_ring(half, n):
                use = half * uses + n
                pe.wait_ge(ring_free, use + 1)

            def project_qk(half, b, some):
                for n in some:
                    which, head, c = qk_chunk(n)
                    cols = slice(head * D0, (head + 1) * D0)
                    tokens = slice(b * SEQ + c * NB, b * SEQ + (c + 1) * NB)
                    if n < 2:
                        take_ring(half, n)
                    elif n > 2:
                        pe.wait_ge(ring_free, half * uses + n)
                    project(nc, qk_bank(n), lambda kt: [h[:, which, kt, cols] for h in w],
                            lambda kt: [h[:, kt, tokens] for h in k.xT]).then_inc(ring_full, 1)

            def project_v(half, b, n):
                if n == 1:
                    pe.wait_ge(out_done, half * groups * 2 + 1)
                elif n > 1:
                    pe.wait_ge(v_taken, half * v_uses + n - 1)
                for j in range(2):
                    t = b * ST + 2 * n + j
                    mm = project(nc, v_bank(n)[:, j * HP * D0:(j + 1) * HP * D0],
                                 lambda kt: [h[:, kt, t * P:(t + 1) * P] for h in k.xT],
                                 lambda kt: [h[:, 2, kt, :] for h in w])
                mm.then_inc(v_full, 1)

            def score(half, i):
                head, t = i // ST, i % ST
                pe.wait_ge(exp_done, half * tiles + i + 1)
                for c in range(SEQ // NB):
                    mm = three_passes(nc, scores(i)[:, c, :], [h[:, head, t * P:(t + 1) * P] for h in q],
                                      [h[:, head, c * NB:(c + 1) * NB] for h in key])
                mm.then_inc(score_full, 1)

            def turn(half, i):
                pe.wait_ge(exp_done, half * tiles + i + 3)
                for half_tile in range(2):
                    use = turn_use(i, half_tile)
                    take_ring(half, use)
                    for j in range(GT):
                        kt = half_tile * GT + j
                        mm = nc.tensor.transpose(ring(use)[:, j * P:(j + 1) * P], prob[:, i % 2, kt * P:(kt + 1) * P], k.ident[:])
                    mm.then_inc(ring_full, 1)

            def weighted_v(half, g, part):
                head = g // QG
                if part == 0:
                    pe.wait_ge(ring_free, half * uses + turn_use((g + 1) * GT - 1, 1) + 3)
                    if g == groups - 1:
                        pe.wait_ge(exp_done, half * tiles + tiles - 1 + 2)
                    elif g:
                        pe.wait_ge(o_done, half * groups + g + 1)
                if g == 0:
                    pe.wait_ge(v_done, half * v_uses + part + 3)
                n = ST // GT
                for kt in range(part * n, (part + 1) * n):
                    mm = three_passes(nc, o_bank(g), [h[:, kt, head * D0:(head + 1) * D0] for h in v],
                                      [h[:, g % 2, kt, :] for h in probT], start=kt == 0, stop=kt == ST - 1)
                if part == GT - 1:
                    mm.then_inc(o_full, 1)

            def output(half, g, part):
                use = (half * groups + g) * 2 + part
                if part == 0:
                    pe.wait_ge(o_done, half * groups + g + 2)
                pe.wait_ge(out_done, use + 1)
                for j in range(2):
                    t = part * 2 + j
                    mm = three_passes(nc, out_bank[:, j * C:(j + 1) * C], [h[:, t * P:(t + 1) * P] for h in o],
                                      [h[:, g // QG, :] for h in wo])
                mm.then_inc(out_full, 1)

            pe.wait_ge(ident_in, 16)
            norm.tensor(pe)
            pe.wait_ge(norm.lo_done, norm.groups)
            head_uses = qk_uses // HP

            def projections(m, b, first=False):
                half = m * BATCH + b
                if b % BATCH == 0:
                    pe.wait_ge(w_ready, m + b // BATCH + 1)
                project_qk(half, b % BATCH, range(OUT_AT[0]))
                if not first:
                    output(half - 1, groups - 1, 0)
                project_qk(half, b % BATCH, range(*OUT_AT))
                if not first:
                    output(half - 1, groups - 1, 1)
                project_qk(half, b % BATCH, range(OUT_AT[1], head_uses + 1))
                pe.wait_ge(ring_free, half * uses + head_uses + 2)
                pe.wait_ge(o_done, half * groups + 1)
                score(half, 0)
                project_qk(half, b % BATCH, range(head_uses + 1, qk_uses))

            def attend(m, b, beside=None):
                half = m * BATCH + b
                for i in range(tiles):
                    g, j = i // GT, i % GT
                    if i + 1 < tiles:
                        if i + 1 == ST:
                            pe.wait_ge(ring_free, half * uses + qk_uses + 2)
                        score(half, i + 1)
                    turn(half, i)
                    if i < v_uses:
                        project_v(half, b, i)
                    if g >= 2 and j % 2:
                        if b == 0 and i == 2 * GT + 1:
                            pe.wait_ge(wo_ready, m + 1)
                        output(half, g - 2, j // 2)
                    if g >= 1:
                        weighted_v(half, g - 1, j)
                for part in range(GT):
                    weighted_v(half, groups - 1, part)
                    if 1 <= part <= 2:
                        output(half, groups - 2, part - 1)

            halves(pe, projections, attend)
            for part in range(2):
                output(passes * BATCH - 1, groups - 1, part)

        @block.scalar
        def _(act):
            for _ in range(2):
                act.nop().then_inc(exp_done, 1)
            norm.scalar(act)

            def exp(half, i):
                act.wait_ge(max_ready, half * tiles + i + 1)
                if i >= 2:
                    act.wait_ge(ring_full, half * uses + turn_use(i - 2, 1) + 1)
                nc.scalar.activation(prob[:, i % 2, :], scores(i).rearrange("p a b -> p (a b)"), ACT.Exp,
                                     bias=neg_max[:, i % 2:i % 2 + 1],
                                     accum_out=total[:, i:i + 1]).then_inc(exp_done, 1)

            def projections(m, b, first=False):
                half = m * BATCH + b
                for n in range(qk_uses):
                    which, head, c = qk_chunk(n)
                    act.wait_ge(ring_full, half * uses + n + 1)
                    nc.scalar.activation((q, key)[which][0][:, head, c * NB:(c + 1) * NB], qk_bank(n), ACT.Identity,
                                         bias=bias_qk[:, which * HP + head:which * HP + head + 1]).then_inc(ring_hi, 1)
                    if n == qk_uses // HP + 1:
                        exp(half, 0)

            def attend(m, b, beside=None):
                half = m * BATCH + b
                for i in range(tiles):
                    g, j = i // GT, i % GT
                    for half_tile in range(2):
                        use = turn_use(i, half_tile)
                        act.wait_ge(ring_full, half * uses + use + 1)
                        nc.scalar.activation(
                            probT[0][:, g % 2, half_tile * GT:(half_tile + 1) * GT, j * P:(j + 1) * P],
                            ring(use).rearrange("p (t n) -> p t n", n=P), ACT.Copy).then_inc(ring_hi, 1)
                    if i + 1 < tiles:
                        exp(half, i + 1)
                    if i < v_uses:
                        act.wait_ge(v_taken, half * v_uses + i + 1)
                        to = slice(i * GT // HP, (i + 1) * GT // HP)
                        nc.scalar.activation(v[0][:, to, :].rearrange("p t d -> p (t d)"), v_whole[:, i % 2, :],
                                             ACT.Copy).then_inc(v_hi_done, 1)
                    if beside:
                        beside(i)
                    if g >= 1 and j == GT - 1:
                        act.wait_ge(o_full, half * groups + g)
                        nc.scalar.activation(o[0][:], o_bank(g - 1), ACT.Copy).then_inc(o_hi_done, 1)
                act.wait_ge(o_full, half * groups + groups)
                nc.scalar.activation(o[0][:], o_bank(groups - 1), ACT.Copy).then_inc(o_hi_done, 1)

            def begin_norm(i):
                if i in NORM_ACC_ACT:
                    after.early_scalar(act, NORM_ACC_ACT.index(i))
                if i in NORM_X_ACT:
                    after.normalise_x(act, NORM_X_ACT.index(i))

            halves(act, projections, attend, begin_norm)
            after.early_scalar(act, after.ahead)
            after.done["scalar"] = after.ahead + 1

        @block.vector
        def _(dve):
            for _ in range(2):
                dve.nop().then_inc(ring_free, 1)
            dve.nop().then_inc(o_done, 1)
            dve.nop().then_inc(out_done, 1)
            norm.vector(dve)
            dve.wait_ge(bias_o_in, 16)
            nc.vector.tensor_copy(k.acc[:], bias_o.unsqueeze(1).broadcast_to([P, TT, C])).then_inc(own, 1)
            dve.wait_ge(own, 1)

            def row_max(half, i):
                dve.wait_ge(score_full, half * tiles + i + 1)
                nc.vector.tensor_reduce(neg_max[:, i % 2:i % 2 + 1], scores(i), AX.XY, ALU.max,
                                        negate=True).then_inc(max_ready, 1)

            def o_lo(half, g):
                dve.wait_ge(o_hi_done, half * groups + g + 1)
                nc.vector.tensor_tensor(o[1][:], o_bank(g), f32(o[0][:]), ALU.subtract).then_inc(o_done, 1)

            def add_up(half, b, g, part):
                use = (half * groups + g) * 2 + part
                if part == 0:
                    nc.vector.reciprocal(over_total[:, g * GT:(g + 1) * GT], total[:, g * GT:(g + 1) * GT]).then_inc(own, 1)
                    dve.wait_ge(own, half * groups + g + 2)
                dve.wait_ge(out_full, use + 1)
                for j in range(2):
                    t = part * 2 + j
                    to = k.acc[:, b * ST + g % QG * GT + t, :]
                    add = nc.vector.scalar_tensor_tensor(out=to, in0=out_bank[:, j * C:(j + 1) * C],
                                                         scalar=over_total[:, g * GT + t:g * GT + t + 1], in1=to,
                                                         op0=ALU.mult, op1=ALU.add)
                add.then_inc(out_done, 1)

            def projections(m, b, first=False):
                half = m * BATCH + b
                for n in range(qk_uses):
                    if not first and n in OUT_AT:
                        add_up(half - 1, (b - 1) % BATCH, groups - 1, OUT_AT.index(n))
                    if n == qk_uses // HP + 1:
                        row_max(half, 0)
                    which, head, c = qk_chunk(n)
                    dve.wait_ge(ring_hi, half * uses + n + 1)
                    to = [h[:, head, c * NB:(c + 1) * NB] for h in (q, key)[which]]
                    nc.vector.scalar_tensor_tensor(
                        out=to[1], in0=qk_bank(n), scalar=bias_qk[:, which * HP + head:which * HP + head + 1],
                        in1=f32(to[0]), op0=ALU.add, op1=ALU.subtract).then_inc(ring_free, 1)

            def attend(m, b, beside=None):
                half = m * BATCH + b
                for i in range(tiles):
                    g, j = i // GT, i % GT
                    if i + 1 < tiles:
                        row_max(half, i + 1)
                    for half_tile in range(2):
                        use = turn_use(i, half_tile)
                        dve.wait_ge(ring_hi, half * uses + use + 1)
                        to = [h[:, g % 2, half_tile * GT:(half_tile + 1) * GT, j * P:(j + 1) * P] for h in probT]
                        nc.vector.tensor_tensor(to[1], ring(use).rearrange("p (t n) -> p t n", n=P), f32(to[0]),
                                                ALU.subtract).then_inc(ring_free, 1)
                    if i < v_uses:
                        dve.wait_ge(v_full, half * v_uses + i + 1)
                        dve.wait_ge(v_done, half * v_uses + i + 1)
                        nc.vector.tensor_tensor(
                            v_whole[:, i % 2, :].rearrange("p (t d) -> p t d", t=2),
                            v_bank(i).rearrange("p (t d) -> p t d", t=2),
                            bias_v[:].unsqueeze(1).broadcast_to([P, 2, HP * D0]), ALU.add).then_inc(v_taken, 1)
                    if g >= 2 and j % 2:
                        add_up(half, b, g - 2, j // 2)
                    if g >= 1 and j == GT - 1:
                        o_lo(half, g - 1)
                    if beside:
                        beside(i)
                for part in range(2):
                    add_up(half, b, groups - 2, part)
                o_lo(half, groups - 1)

            def begin_norm(i):
                if i in NORM_ACC_DVE:
                    dve.wait_ge(out_done, (passes * BATCH - 1) * groups * 2 + 1)
                    after.early_vector(dve, NORM_ACC_DVE.index(i))
                if i in NORM_X_DVE:
                    after.add_up(dve, NORM_X_DVE.index(i))

            halves(dve, projections, attend, begin_norm)
            dve.wait_ge(out_done, passes * BATCH * groups * 2 - 1)
            after.early_vector(dve, after.ahead)
            after.done["vector"] = after.ahead + 1
            for part in range(2):
                add_up(passes * BATCH - 1, BATCH - 1, groups - 1, part)


def f32(ap):
    return ap.bitcast(F32)


def mlp_stage(nc, ctx, k, name, w_dram, n_chunks, before, after, *, hidden_scales=None, out_scale=None, weigh=None,
              weigh_vector=(), early_steps=False):
    cols_up, cols_down = KC * IM, 2 * KC * IM
    cols = cols_down + C
    per_chunk = TOK // NB
    pair = 2 * per_chunk
    last = n_chunks // 2 - 1
    st = Stage(nc, ctx, name)
    staged = st.sb("staged", [P, 2, cols])
    w_hi, w_lo = st.halves("w", [P, 2, cols])
    gate_act = st.sb("gate_act", [P, 2, NB])
    hidden = st.sb("hidden", [P, 2, NB])
    hid_hi, hid_lo = st.halves("hid", [P, 2, NB])
    landed = [st.sem(f"landed{n}") for n in range(2)]
    staged_free, hi_split, w_ready = (st.sem(n) for n in ("staged_free", "hi_split", "w_ready"))
    gate_full, up_full, silu_done, prod_done = (st.sem(n) for n in ("gate_full", "up_full", "silu_done", "prod_done"))
    hi_done, lo_done, down_full, acc_done = (st.sem(n) for n in ("hi_done", "lo_done", "down_full", "acc_done"))
    if hidden_scales is not None:
        scales = st.sb("scales", [P, 2, n_chunks])
        gate_scale = st.sb("gate_scale", [P, 2])
        scales_in, scale_set = st.sem("scales_in"), st.sem("scale_set")
    if out_scale is not None:
        row = st.sb("row", [P, C])
        row_in, scaled = st.sem("row_in"), st.sem("scaled")
    gate_bank = lambda q: k.psum[:, q % 2, :]
    up_bank = lambda q: k.psum[:, 2 + q % 2, :]
    down_tile = lambda q, j: k.psum[:, 4 + 2 * (q % 2) + j // 2, j % 2 * C:(j % 2 + 1) * C]

    def first_loads(sp):
        if out_scale is not None:
            sp.dma_start(row[:], out_scale.partition_broadcast(P)).then_inc(row_in, 16)
        if hidden_scales is not None:
            sp.dma_start(scales[:], hidden_scales.rearrange("s p n -> p s n")).then_inc(scales_in, 16)
        for e in range(2):
            sp.dma_start(staged[:, e, :], w_dram[e]).then_inc(landed[e], 16)

    def sync(sp):
        with sp.Fori(1, n_chunks // 2) as m:
            for e in range(2):
                sp.wait_ge(staged_free, m * 2 + e - 1)
                sp.dma_start(staged[:, e, :], w_dram[bass.ds(m * 2 + e, 1)].squeeze(0)).then_inc(landed[e], 16)

    def gate_up(pe, m, s):
        e, c = s // per_chunk % 2, s % per_chunk
        step = m * pair + s
        tokens = slice(c * NB, (c + 1) * NB)
        if c == 0:
            pe.wait_ge(w_ready, m * 2 + s // per_chunk + 1)
        x = lambda kt: [h[:, kt, tokens] for h in k.xT]
        pe.wait_ge(before.lo_done, c + 1)
        pe.wait_ge(silu_done, step + 1)
        project(nc, gate_bank(s), lambda kt: [w[:, e, kt * IM:(kt + 1) * IM] for w in (w_hi, w_lo)],
                x).then_inc(gate_full, 1)
        pe.wait_ge(prod_done, step + 1)
        project(nc, up_bank(s), lambda kt: [w[:, e, cols_up + kt * IM:cols_up + (kt + 1) * IM]
                                            for w in (w_hi, w_lo)], x).then_inc(up_full, 1)

    def first_steps(pe):
        for s in range(2):
            gate_up(pe, 0, s)

    def tensor(pe):
        def down(m, s):
            e = s // per_chunk
            step = m * pair + s
            pe.wait_ge(lo_done, step + 3)
            for j in range(GT):
                if j % 2 == 0:
                    pe.wait_ge(acc_done, step * 2 + j // 2 + 1)
                ins = three_passes(nc, down_tile(s, j),
                                   [h[:, s % 2, j * P:(j + 1) * P] for h in (hid_hi, hid_lo)],
                                   [w[:, e, cols_down:cols] for w in (w_hi, w_lo)])
                if j % 2:
                    ins.then_inc(down_full, 1)

        if not early_steps:
            first_steps(pe)
        for s in range(pair):
            if s > 0:
                gate_up(pe, 0, s + 1)
            down(0, s)
        with pe.Fori(1, last) as m:
            for s in range(pair):
                gate_up(pe, m, s + 1)
                down(m, s)
        for s in range(pair):
            if s + 1 < pair:
                gate_up(pe, last, s + 1)
            down(last, s)

    def first_banks(act):
        for _ in range(2):
            act.nop().then_inc(silu_done, 1)

    def scalar(act):
        if hidden_scales is not None:
            act.wait_ge(scales_in, 16)

        def step(m, s):
            n = m * pair + s
            e = s // per_chunk
            if hidden_scales is not None and s % per_chunk == 0:
                nc.scalar.activation(gate_scale[:, e:e + 1], scales[:, 0, bass.ds(m * 2 + e, 1)],
                                     ACT.Copy).then_inc(scale_set, 1)
                act.wait_ge(scale_set, m * 2 + e + 1)
            act.wait_ge(gate_full, n + 1)
            act.wait_ge(prod_done, n + 1)
            by = 1.0 if hidden_scales is None else gate_scale[:, e:e + 1]
            nc.scalar.activation(gate_act[:, s % 2, :], gate_bank(s), ACT.Silu, scale=by).then_inc(silu_done, 1)
            act.wait_ge(prod_done, n + 3)
            nc.scalar.activation(hid_hi[:, s % 2, :], hidden[:, s % 2, :], ACT.Copy).then_inc(hi_done, 1)

        with act.Fori(0, last) as m:
            for s in range(pair):
                step(m, s)
        for s in range(pair):
            step(last, s)
            if s > per_chunk:
                after.early_scalar(act, s - per_chunk - 1)
        after.done["scalar"] = per_chunk - 1

    def gpsimd(pool):
        for _ in range(2):
            pool.nop().then_inc(lo_done, 1)
        after.prepare(pool)

        def step(m, s):
            pool.wait_ge(hi_done, m * pair + s + 1)
            nc.gpsimd.tensor_tensor(hid_lo[:, s % 2, :], hidden[:, s % 2, :],
                                    hid_hi[:, s % 2, :].bitcast(F32), ALU.subtract).then_inc(lo_done, 1)

        with pool.Fori(0, last) as m:
            for s in range(pair):
                step(m, s)
        for s in range(pair):
            step(last, s)
            if s > per_chunk:
                after.early_gpsimd(pool, s - per_chunk - 1)
        after.done["gpsimd"] = per_chunk - 1

    def split_weights(dve, m, e):
        dve.wait_ge(landed[e % 2], m * 16 + (16 if e < 2 else 32))
        if out_scale is not None:
            down_in = staged[:, e % 2, cols_down:cols]
            nc.vector.tensor_tensor(down_in, down_in, row[:], ALU.mult).then_inc(scaled, 1)
            dve.wait_ge(scaled, m * 2 + e + 1)
        nc.vector.tensor_copy(w_hi[:, e % 2, :], staged[:, e % 2, :]).then_inc(hi_split, 1)
        dve.wait_ge(hi_split, m * 2 + e + 1)
        nc.vector.tensor_tensor(w_lo[:, e % 2, :], staged[:, e % 2, :], w_hi[:, e % 2, :].bitcast(F32),
                                ALU.subtract).then_inc(w_ready, 1)
        dve.wait_ge(w_ready, m * 2 + e + 1)
        dve.nop().then_inc(staged_free, 1)

    def first_weights(dve):
        for _ in range(2):
            dve.nop().then_inc(prod_done, 1)
        for _ in range(4):
            dve.nop().then_inc(acc_done, 1)
        if out_scale is not None:
            dve.wait_ge(row_in, 16)
        split_weights(dve, 0, 0)

    def vector(dve):
        def product(m, s):
            step = m * pair + s
            dve.wait_ge(silu_done, step + 3)
            dve.wait_ge(up_full, step + 1)
            dve.wait_ge(lo_done, step + 1)
            h, g = hidden[:, s % 2, :], gate_act[:, s % 2, :]
            if hidden_scales is None:
                ins = nc.vector.tensor_tensor(h, up_bank(s), g, ALU.mult)
            else:
                by = scales[:, 1, bass.ds(m * 2 + s // per_chunk, 1)]
                ins = nc.vector.scalar_tensor_tensor(out=h, in0=up_bank(s), scalar=by, in1=g,
                                                     op0=ALU.mult, op1=ALU.mult)
            ins.then_inc(prod_done, 1)

        def add_up(m, s, first=False):
            step = m * pair + s
            for j in range(GT):
                if j % 2 == 0:
                    dve.wait_ge(down_full, step * 2 + j // 2 + 1)
                t = s % per_chunk * GT + j
                by = 1.0 if weigh is None else weigh[:, bass.ds((m * 2 + s // per_chunk) * TT + t, 1)]
                if first:
                    ins = nc.vector.tensor_scalar(k.acc[:, t, :], down_tile(s, j), by, None, ALU.mult)
                else:
                    ins = nc.vector.scalar_tensor_tensor(out=k.acc[:, t, :], in0=down_tile(s, j), scalar=by,
                                                         in1=k.acc[:, t, :], op0=ALU.mult, op1=ALU.add)
                if j % 2:
                    ins.then_inc(acc_done, 1)

        def step(m, s, first=False, final=False):
            if s % per_chunk == 1 and not (final and s > 1):
                split_weights(dve, m, s // per_chunk + 1)
            if not (final and s + 1 == pair):
                product(m, s + 1)
            add_up(m, s, first)

        if hidden_scales is not None:
            dve.wait_ge(scales_in, 16)
        product(0, 0)
        for s in range(pair):
            step(0, s, first=s < per_chunk)
            if s < len(weigh_vector):
                weigh_vector[s](dve)
        with dve.Fori(1, last) as m:
            for s in range(pair):
                step(m, s)
        for s in range(pair):
            step(last, s, final=True)
            if s >= per_chunk:
                dve.wait_ge(acc_done, (last * pair + s) * 2 + 6)
                after.early_vector(dve, s - per_chunk)
        after.done["vector"] = per_chunk

    if early_steps:
        before.meanwhile = first_steps
    return Program(first_loads, nothing, first_banks, first_weights, nothing), Program(sync, tensor, scalar, vector, gpsimd)


def route_stage(nc, ctx, k, name, router_dram, weigh, before):
    st = Stage(nc, ctx, name)
    router = st.sb("router", [P, KC, N_EXPERT])
    r_hi, r_lo = st.halves("r", [P, KC, N_EXPERT])
    score = st.sb("score", [P, TT, N_EXPERT])
    best = st.sb("best", [P, TT, N_TOP])
    rest = st.sb("rest", [P, TT, N_EXPERT])
    total = st.sb("total", [P, TT])
    factor = st.sb("factor", [P, TT])
    landed, own, r_ready, logits_full, score_ready = (
        st.sem(n) for n in ("landed", "own", "r_ready", "logits_full", "score_ready"))

    def sync(sp):
        sp.dma_start(router[:], router_dram).then_inc(landed, 16)

    def logits(pe, tiles):
        for t in tiles:
            if t % GT == 0:
                pe.wait_ge(before.lo_done, t // GT + 1)
            ins = project(nc, k.psum[:, 0, t * N_EXPERT:(t + 1) * N_EXPERT],
                          lambda kt: [h[:, kt, t * P:(t + 1) * P] for h in k.xT],
                          lambda kt: [r[:, kt, :] for r in (r_hi, r_lo)])
        return ins

    ahead = before.ahead * GT

    def first_logits(pe):
        pe.wait_ge(r_ready, 1)
        logits(pe, range(ahead))

    before.meanwhile = first_logits

    def tensor(pe):
        logits(pe, range(ahead, TT)).then_inc(logits_full, 1)
        pe.wait_ge(score_ready, 1)

    def scalar(act):
        act.wait_ge(logits_full, 1)
        nc.scalar.activation(score[:].rearrange("p t e -> p (t e)"), k.psum[:, 0, 0:TT * N_EXPERT],
                             ACT.Sigmoid).then_inc(score_ready, 1)

    link = Count(own)

    def vector(dve):
        dve.wait_ge(landed, 16)
        link.step(dve, nc.vector.tensor_copy(r_hi[:], router[:]))
        nc.vector.tensor_tensor(r_lo[:], router[:], r_hi[:].bitcast(F32), ALU.subtract).then_inc(r_ready, 1)
        link.inc(nc.vector.memset(weigh[:, 0:N_SHARED * TT], 1.0))

    def find_best(dve):
        dve.wait_ge(score_ready, 1)
        for t in range(TT):
            link.inc(nc.vector.max(best[:, t, :], score[:, t, :]))

    def take_best(dve):
        link.wait(dve)
        for t in range(TT):
            link.inc(nc.vector.match_replace(rest[:, t, :], best[:, t, :], score[:, t, :], -1.0))

    def sum_best(dve):
        link.step(dve, nc.vector.tensor_reduce(total[:], best[:], AX.X, ALU.add))
        link.step(dve, nc.vector.tensor_scalar(total[:], total[:], 1e-6, None, ALU.add))
        link.step(dve, nc.vector.reciprocal(factor[:], total[:]))
        link.step(dve, nc.vector.tensor_scalar(factor[:], factor[:], ROUTE_SCALE, None, ALU.mult))

    def weigh_best(dve):
        link.step(dve, nc.vector.tensor_scalar(rest[:], rest[:], 0.0, None, ALU.is_lt))
        link.step(dve, nc.vector.tensor_tensor(rest[:], rest[:], score[:], ALU.mult))
        link.step(dve, nc.vector.tensor_tensor(weigh[:, N_SHARED * TT:].rearrange("p (e t) -> p t e", t=TT), rest[:],
                                               factor[:].unsqueeze(2).broadcast_to([P, TT, N_EXPERT]), ALU.mult))

    return (Program(sync, nothing, nothing, vector, nothing), Program(nothing, tensor, scalar, nothing, nothing),
            (find_best, take_best, sum_best, weigh_best))


HG = 4
HEAD_ROWS = P // HG
STACK = 64
N_SHIFT = 2 * GT
f32 = lambda ap: ap.bitcast(F32)


def attention1_stage(nc, k, name, ins, before, after):
    passes = H1 // HG
    chunks = SEQ // NB
    pairs = HG // 2
    half_steps = [(c, kt, h) for c in range(chunks) for kt in range((c + 1) * GT) for h in range(HG)]
    half_pieces = [(c, t, part, 2 * pair + i) for c in range(chunks) for pair in range(pairs)
                   for t in range(c * GT, (c + 1) * GT) for part in range(c + 1) for i in range(2)]
    assert len(half_steps) == len(half_pieces)
    HALF = len(half_steps)
    PASS = BATCH * HALF
    STEPS, HALVES = passes * PASS, passes * BATCH
    LEAD_SCORES, LEAD_MAX, FIRST = 3, 40, 16
    chunk_start = [half_steps.index((c, 0, 0)) for c in range(chunks)] + [HALF]
    stack_jobs = [(c, pair, which) for c in range(chunks) for pair in range(pairs) for which in range(2)]
    N_STACK = len(stack_jobs)
    PROJ_STEPS, STACK_STEPS = (0, 16), (3, 4, 7, 8, 20, 21, 35, 37)
    PROLOGUE_USES = chunks + N_STACK
    V_USES = TT * C // NB
    V_STEPS = range(2 - LEAD_MAX, 2 - LEAD_MAX + 4 * V_USES, 4)
    SCORE_BANKS, PROBS = 3, 6

    def misc_jobs(g):
        half, r = g // HALF, g % HALF
        jobs = []
        for c in range(chunks):
            of = (g + LEAD_MAX - 2) // HALF
            if (g + LEAD_MAX - 2) % HALF == chunk_start[c + 1] % HALF:
                of -= int(c == chunks - 1)
                if 0 <= of < HALVES:
                    jobs.append(("maxima", of, c))
        if g in V_STEPS:
            jobs.append(("v", 0, V_STEPS.index(g)))
        if g >= 0 and r in PROJ_STEPS and half + 1 < HALVES:
            jobs.append(("project", half + 1, PROJ_STEPS.index(r)))
        if g >= 0 and r in STACK_STEPS and half + 1 < HALVES:
            jobs.append(("stack", half + 1, STACK_STEPS.index(r)))
        for at, kind, back, c in ((18, "sums", 0, 0), (23, "spread", 0, 0), (31, "out0", 0, 0), (33, "out1", 0, 0),
                                  (2, "sums", 1, 1), (5, "spread", 1, 1), (14, "out0", 1, 1), (15, "out1", 1, 1)):
            if r == at and 0 <= half - back < HALVES:
                jobs.append((kind, half - back, c))
        return jobs

    first_use, uses = {}, PROLOGUE_USES
    for g in range(-LEAD_MAX, STEPS + FIRST):
        first_use[g] = uses
        uses += len(misc_jobs(g))
    v_use = [first_use[g] + misc_jobs(g).index(("v", 0, n)) for n, g in enumerate(V_STEPS)]
    USES = first_use[FIRST + PASS] - first_use[FIRST]
    assert USES % 2 == 0

    LAST = STEPS - HALF
    NORM_ACC_DVE, NORM_X_DVE = (LAST + 17, LAST + 19), (LAST + 27, LAST + 29)
    NORM_ACC_POOL, NORM_X_POOL = (LAST + 19, LAST + 21), (LAST + 29, LAST + 31)
    NORM_ACC_ACT, NORM_X_ACT = (LAST + 21, LAST + 24), (LAST + 49, LAST + 51)

    def timeline(eng, step):
        for g in range(-LEAD_MAX, FIRST):
            step(0, g)
        with eng.Fori(0, passes - 1) as m:
            for g in range(FIRST, FIRST + PASS):
                step(m, g)
        for g in range(STEPS - PASS + FIRST, STEPS + FIRST):
            step(0, g)

    with ExitStack() as ctx:
        st = Stage(nc, ctx, name)
        w_in = st.sb("w_in", [P, KC * P])
        w = st.halves("w", [P, KC, P])
        wv = st.halves("wv", [P, KC, C])
        wp = st.halves("wp", [P, passes, C])
        bias_in, bias = st.sb("bias_in", [P, 1]), st.sb("bias", [P, 1])
        to_stack = st.sb("to_stack", [P, 2 * 2 * pairs, P], F32R)
        one = st.sb("one", [P, 1])
        masks = st.sb("masks", [P, 2, P], BF16)
        ident_b = st.sb("ident_b", [P, P], BF16)
        tile_rows = st.sb("tile_rows", [P, GT, P])
        sum_rows = st.sb("sum_rows", [P, HG])
        q = [[st.sb(f"q_{b}{h}", [P, SEQ], F32R) for h in range(HG)] for b in range(BATCH)]
        key = [[st.sb(f"key_{b}{h}", [P, SEQ], F32R) for h in range(HG)] for b in range(BATCH)]
        qk = st.halves("qk", [P, chunks, NB])
        v_all = st.sb("v_all", [P, TT, C])
        v = [st.sb(f"v_{b}", [P, ST, HG, 2 * D1]) for b in range(BATCH)]
        peaks = st.sb("peaks", [P, 2, HALF])
        peak = st.sb("peak", [P, HG, GT])
        shift = st.sb("shift", [P, HG, STACK + N_SHIFT])
        probT = st.sb("probT", [P, PROBS, NB])
        o = st.sb("o", [P, chunks, NB])
        over_sum = st.sb("over_sum", [P, GT * HG])
        wide = st.sb("wide", [P, GT * HG, HEAD_ROWS])
        factor = wide[:].rearrange("p a b -> p (a b)")
        y = st.halves("y", [P, NB])
        wv_in, early = factor, probT[:].rearrange("p a b -> p (a b)")
        wp_in = early[:, 0:passes * C]
        bias_v = early[:, passes * C:(passes + 1) * C]
        bias_y = early[:, (passes + 2) * C:(passes + 3) * C]
        masks_in = early[:, (passes + 1) * C:(passes + 2) * C].rearrange("p (a b) -> p a b", b=P)
        to_stack_in = early[:, (passes + 3) * C:(passes + 3) * C + 4 * pairs * P]
        consts, landed, w_free, w_ready, split = (
            st.sem(n) for n in ("consts", "landed", "w_free", "w_ready", "split"))
        to_stack_ready = st.sem("to_stack_ready")
        prepared, zeroed, ones_set, wv_ready, wp_ready = (st.sem(n) for n in ("prepared", "zeroed", "ones_set", "wv_ready", "wp_ready"))
        max_full, max_free, peak_done, shift_ready, shifted = (
            st.sem(n) for n in ("max_full", "max_free", "peak_done", "shift_ready", "shifted"))
        misc_full, qk_hi, qk_lo, stacked = (st.sem(n) for n in ("misc_full", "qk_hi", "qk_lo", "stacked"))
        misc_free = [st.sem(f"misc_free{n}") for n in range(2)]
        scores_full, exp_done, weighed = (st.sem(n) for n in ("scores_full", "exp_done", "weighed"))
        v_ready, inverted, widened = (st.sem(n) for n in ("v_ready", "inverted", "widened"))
        o_done, y_split, y_ready = (st.sem(n) for n in ("o_done", "y_split", "y_ready"))
        block = ctx.enter_context(nc.Block())

        max_bank = lambda n: k.psum[:, n % 2, :]
        score_bank = lambda g: k.psum[:, 2 + g % SCORE_BANKS, :]
        o_bank = k.psum[:, 5, :]
        misc_bank = lambda n: k.psum[:, 6 + n % 2, :]
        stack_rows = lambda h: slice(h % 2 * STACK, (h % 2 + 1) * STACK)
        shift_rows = lambda h: slice(0, N_SHIFT) if h % 2 else slice(STACK, STACK + N_SHIFT)
        other_rows = lambda h: slice(0, STACK) if h % 2 else slice(STACK, P)
        shift_cols = lambda h: slice(STACK, STACK + N_SHIFT) if h % 2 else slice(0, STACK + N_SHIFT)
        chunk = lambda c: slice(c * NB, (c + 1) * NB)

        def wait_misc(eng, m, use):
            eng.wait_ge(misc_free[use % 2], m * (USES // 2) + use // 2 + 1)

        def wait_read(eng, m, use):
            eng.wait_ge(misc_free[use % 2], m * (USES // 2) + use // 2 + 2)

        @block.sync
        def _(sp):
            before.sync(sp)
            for to, n in ((to_stack_in, "to_stack"), (wv_in, "w_v"), (masks_in, "masks"),
                          (tile_rows[:], "tile_rows"), (sum_rows[:], "sum_rows"), (wp_in, "w_proj")):
                sp.dma_start(to, ins[n]).then_inc(consts, 16)
            sp.dma_start(bias_v, ins["b_v"].partition_broadcast(P)).then_inc(consts, 16)
            sp.dma_start(bias_y, ins["b_proj"].partition_broadcast(P)).then_inc(consts, 16)
            with sp.Fori(0, passes) as m:
                sp.wait_ge(w_free, m + 1)
                sp.dma_start(w_in[:], ins["w_attn"][bass.ds(m, 1)].squeeze(0)).then_inc(landed, 16)
                sp.dma_start(bias_in[:], ins["b_qk"][bass.ds(m, 1)].squeeze(0)).then_inc(landed, 16)

        @block.gpsimd
        def _(pool):
            for _ in range(chunks):
                pool.nop().then_inc(y_ready, 1)
            pool.nop().then_inc(w_free, 1)
            nc.gpsimd.memset(one[:], 1.0).then_inc(ones_set, 1)
            pool.wait_ge(ones_set, 1)
            flat = lambda a: a.rearrange("p a b -> p (a b)")

            def halve(whole, parts, ready, n):
                width = whole.shape[1]
                nc.gpsimd.tensor_tensor(parts[0], whole, one[:].broadcast_to([P, width]), ALU.mult).then_inc(split, 1)
                pool.wait_ge(split, n)
                nc.gpsimd.tensor_tensor(parts[1], whole, f32(parts[0]), ALU.subtract).then_inc(ready, 1)

            def split_weights(m, at):
                pool.wait_ge(landed, (m + at + 1) * 32)
                if at:
                    pool.wait_ge(qk_lo, (m + at) * BATCH * chunks)
                nc.gpsimd.tensor_tensor(bias[:], bias_in[:], one[:], ALU.mult)
                halve(w_in[:], [flat(h[:]) for h in w], w_ready, m + at + (3 if at else 1))
                pool.wait_ge(w_ready, m + at + 1)
                pool.nop().then_inc(w_free, 1)

            def out_operand(m, half, c, use):
                at = m * BATCH * chunks * 2 + (chunks * half + c) * 2
                wait_read(pool, m, use)
                nc.gpsimd.tensor_tensor(factor, o[:, c, :], factor, ALU.mult).then_inc(y_split, 1)
                pool.wait_ge(y_split, at + 1)
                nc.gpsimd.tensor_tensor(y[0][:], factor, one[:].broadcast_to([P, NB]), ALU.mult).then_inc(y_split, 1)
                pool.wait_ge(y_split, at + 2)
                nc.gpsimd.tensor_tensor(y[1][:], factor, f32(y[0][:]), ALU.subtract).then_inc(y_ready, 1)
                pool.wait_ge(y_ready, m * BATCH * chunks + chunks * half + c + 1 + chunks)

            def take_v(m, half):
                b = half % BATCH
                if half > 1:
                    pool.wait_ge(weighed, m * PASS + (half - 1) * HALF + SCORE_BANKS)
                nc.gpsimd.tensor_tensor(
                    v[b][:, :, :, 0:D1],
                    v_all[:, b * ST:(b + 1) * ST, bass.ds((m + half // BATCH) * HG * D1, HG * D1)].rearrange("p t (h d) -> p t h d", d=D1),
                    one[:].unsqueeze(2).unsqueeze(3).broadcast_to([P, ST, HG, D1]), ALU.mult).then_inc(v_ready, 1)
                pool.wait_ge(v_ready, m * BATCH + half + 1)

            def step(m, g):
                half, r = g // HALF, g % HALF
                if g >= 0 and r == 8 and half + 1 < HALVES:
                    take_v(m, half + 1)
                if g >= 0 and half % BATCH == 0 and r == 30 and half // BATCH + 1 < passes:
                    split_weights(m, half // BATCH + 1)
                for n, (kind, half, c) in enumerate(misc_jobs(g)):
                    if kind == "sums":
                        pool.wait_ge(inverted, m * BATCH * chunks + half * chunks + c + 1)
                        nc.gpsimd.tensor_tensor(wide[:], over_sum[:].unsqueeze(2).broadcast_to([P, GT * HG, HEAD_ROWS]),
                                                one[:].unsqueeze(2).broadcast_to([P, GT * HG, HEAD_ROWS]), ALU.mult).then_inc(widened, 1)
                        pool.wait_ge(widened, m * BATCH * chunks + half * chunks + c + 1)
                    if kind == "spread":
                        out_operand(m, half, c, first_use[g] + n)
                if g in NORM_ACC_POOL:
                    after.early_gpsimd(pool, NORM_ACC_POOL.index(g))
                if g in NORM_X_POOL:
                    after.scale_x(pool, NORM_X_POOL.index(g))

            before.gpsimd(pool)
            split_weights(0, 0)
            pool.wait_ge(consts, 128)
            halve(wv_in, [flat(h[:]) for h in wv], wv_ready, 2)
            halve(wp_in, [flat(h[:]) for h in wp], wp_ready, 3)
            pool.wait_ge(wp_ready, 1)
            pads = [(key[0][h], rows(h), value) for h in range(HG) for rows, value in ((other_rows, 0.0), (shift_rows, 1.0))]
            for h in range(HG):
                pads += [(q[1][h], other_rows(h), 0.0), (key[1][h], other_rows(h), 0.0), (key[1][h], shift_rows(h), 1.0)]
            for n, (x, rows, value) in enumerate(pads):
                nc.gpsimd.memset(f32(x[rows]), value).then_inc(ones_set, 1)
                pool.wait_ge(ones_set, n + 2)
            for n in (V_USES - 2, V_USES - 1):
                wait_read(pool, 0, v_use[n])
            take_v(0, 0)
            after.prepare(pool)
            timeline(pool, step)

        @block.tensor
        def _(pe):
            def maxima_scores(m, n):
                half, (c, t, part, h) = n // HALF, half_pieces[n % HALF]
                b = half % BATCH
                rows = stack_rows(h)
                keys = slice(part * NB, min((part + 1) * NB, (t + 1) * P))
                bank = max_bank(n)[:, 0:keys.stop - keys.start]
                if part == 0 and t % GT == 0 and h % 2 == 0:
                    pe.wait_ge(stacked, m * BATCH * N_STACK * 2 + (half * N_STACK + stack_jobs.index((c, h // 2, 1)) + 1) * 2)
                pe.wait_ge(max_free, m * PASS + n + 1)
                own = keys.stop == (t + 1) * P
                mm = nc.tensor.matmul(bank, q[b][h][rows, t * P:(t + 1) * P], key[b][h][rows, keys], start=True, stop=not own)
                if own:
                    mm = nc.tensor.matmul(bank[:, -P:], ident_b[:], masks[:, 0, :], start=False, stop=True)
                mm.then_inc(max_full, 1)

            def scores(m, g):
                half, (c, kt, h) = g // HALF, half_steps[g % HALF]
                b = half % BATCH
                q0 = max(0, kt - c * GT) * P
                if g == 0:
                    pe.wait_ge(ones_set, 1 + 2 * HG)
                if kt == 0:
                    pe.wait_ge(shifted, m * BATCH * chunks * HG + (half * chunks + c) * HG + h + 1)
                pe.wait_ge(exp_done, m * PASS + g + 1)
                mm = nc.tensor.matmul(score_bank(g)[:, q0:], key[b][h][:, kt * P:(kt + 1) * P],
                                      q[b][h][:, c * NB + q0:(c + 1) * NB], start=True, stop=kt < c * GT)
                if kt >= c * GT:
                    mm = nc.tensor.matmul(score_bank(g)[:, q0:q0 + P], ident_b[:], masks[:, 1, :], start=False, stop=True)
                mm.then_inc(scores_full, 1)

            def weigh_v(m, g):
                half, (c, kt, _) = g // HALF, half_steps[g % HALF]
                q0 = max(0, kt - c * GT) * P
                if kt == 0:
                    pe.wait_ge(o_done, m * BATCH * chunks + half * chunks + c + 1)
                    pe.wait_ge(v_ready, m * BATCH + half + 1)
                pe.wait_ge(exp_done, m * PASS + g + 1 + SCORE_BANKS)
                for h in range(HG):
                    nc.tensor.matmul(o_bank[h * HEAD_ROWS:(h + 1) * HEAD_ROWS, q0:], v[half % BATCH][:, kt, h, :],
                                     probT[:, (g - HG + 1 + h) % PROBS, q0:], start=kt == 0,
                                     stop=kt == (c + 1) * GT - 1).then_inc(weighed, 1)

            def project_qk(m, half, c, bank):
                pe.wait_ge(w_ready, m + half // BATCH + 1)
                tokens = slice(half % BATCH * SEQ + c * NB, half % BATCH * SEQ + (c + 1) * NB)
                return project(nc, bank, lambda kt: [x[:, kt, :] for x in w], lambda kt: [x[:, kt, tokens] for x in k.xT])

            def stack(m, half, j, bank):
                c, pair, which = stack_jobs[j]
                pe.wait_ge(qk_lo, m * BATCH * chunks + half * chunks + c + 1)
                for part in range(2):
                    mm = nc.tensor.matmul(bank, to_stack[:, (which * pairs + pair) * 2 + part, :], qk[part][:, c, :],
                                          start=part == 0, stop=part == 1)
                return mm

            def shared(m, g):
                for n, (kind, half, c) in enumerate(misc_jobs(g)):
                    use = first_use[g] + n
                    misc = misc_bank(use)
                    wait_misc(pe, m, use)
                    at = half * chunks + c
                    if kind == "project":
                        mm = project_qk(m, half, c, misc)
                    elif kind == "stack":
                        mm = stack(m, half, c, misc)
                    elif kind == "v":
                        pe.wait_ge(wv_ready, 1)
                        for j in range(2):
                            t = 2 * c + j
                            mm = project(nc, misc[:, j * C:(j + 1) * C], lambda kt: [x[:, kt, t * P:(t + 1) * P] for x in k.xT],
                                         lambda kt: [x[:, kt, :] for x in wv])
                    elif kind == "maxima":
                        pe.wait_ge(shift_ready, m * BATCH * chunks + at + 1)
                        for h in range(HG):
                            cols = shift_cols(h)
                            mm = nc.tensor.transpose(misc[0:cols.stop - cols.start, h * P:(h + 1) * P], shift[:, h, cols], k.ident[:])
                    elif kind == "sums":
                        pe.wait_ge(o_done, m * BATCH * chunks + at + 2)
                        for t in range(GT):
                            mm = nc.tensor.matmul(misc[:, t * HG:(t + 1) * HG], o[:, c, t * P:(t + 1) * P], sum_rows[:],
                                                  start=True, stop=True)
                    elif kind == "spread":
                        pe.wait_ge(widened, m * BATCH * chunks + at + 1)
                        for t in range(GT):
                            mm = nc.tensor.matmul(
                                misc[:, t * P:(t + 1) * P],
                                wide[:, t * HG:(t + 1) * HG, :].rearrange("p h n -> p (h n)"), k.ident[:],
                                start=True, stop=True)
                    else:
                        pe.wait_ge(y_ready, m * BATCH * chunks + at + 1 + chunks)
                        for j in range(2):
                            t = 2 * int(kind == "out1") + j
                            mm = three_passes(nc, misc[:, j * C:(j + 1) * C], [x[:, t * P:(t + 1) * P] for x in y],
                                              [x[:, bass.ds(m + half // BATCH, 1), :].squeeze(1) for x in wp])
                    mm.then_inc(misc_full, 1)

            def step(m, g):
                if 0 <= g + LEAD_SCORES < STEPS:
                    scores(m, g + LEAD_SCORES)
                if g + LEAD_MAX < STEPS:
                    maxima_scores(m, g + LEAD_MAX)
                shared(m, g)
                if 0 <= g < STEPS and g % HG == HG - 1:
                    weigh_v(m, g)

            before.tensor(pe)
            pe.wait_ge(before.lo_done, before.groups)
            pe.wait_ge(to_stack_ready, 1)
            for use in range(PROLOGUE_USES):
                wait_misc(pe, 0, use)
                if use < chunks:
                    project_qk(0, 0, use, misc_bank(use)).then_inc(misc_full, 1)
                else:
                    stack(0, 0, use - chunks, misc_bank(use)).then_inc(misc_full, 1)
            pe.wait_ge(prepared, 1)
            pe.wait_ge(wp_ready, 1)
            timeline(pe, step)

        @block.scalar
        def _(act):
            for _ in range(SCORE_BANKS):
                act.nop().then_inc(exp_done, 1)
            act.nop().then_inc(o_done, 1)

            def take_projection(m, half, c, use):
                act.wait_ge(misc_full, m * USES + use + 1)
                nc.scalar.activation(qk[0][:, c, :], misc_bank(use), ACT.Identity, bias=bias[:, 0:1]).then_inc(qk_hi, 1)

            def take_stack(m, half, j, use):
                c, pair, which = stack_jobs[j]
                act.wait_ge(misc_full, m * USES + use + 1)
                for i in range(2):
                    h = 2 * pair + i
                    nc.scalar.activation((q, key)[which][half % BATCH][h][stack_rows(h), chunk(c)], misc_bank(use)[stack_rows(h)],
                                         ACT.Copy).then_inc(stacked, 1)
                act.wait_ge(stacked, m * BATCH * N_STACK * 2 + (half * N_STACK + j + 1) * 2)
                act.nop().then_inc(misc_free[use % 2], 1)

            def exp(m, g):
                c, kt, _ = half_steps[g % HALF]
                q0 = max(0, kt - c * GT) * P
                act.wait_ge(weighed, m * PASS + g + 1)
                act.wait_ge(scores_full, m * PASS + g + 1)
                nc.scalar.activation(probT[:, g % PROBS, q0:], score_bank(g)[:, q0:], ACT.Exp,
                                     scale=float(D1) ** -0.5).then_inc(exp_done, 1)

            def copy_o(m, half, c):
                act.wait_ge(y_ready, m * BATCH * chunks + half * chunks + c + 1)
                act.wait_ge(weighed, m * PASS + half * HALF + chunk_start[c + 1] + PROBS)
                nc.scalar.activation(o[:, c, :], o_bank, ACT.Copy).then_inc(o_done, 1)

            def step(m, g):
                half, r = g // HALF, g % HALF
                if 0 <= g + LEAD_SCORES < STEPS:
                    exp(m, g + LEAD_SCORES)
                if 0 <= g < STEPS and r == chunk_start[1]:
                    copy_o(m, half, 0)
                if g > 0 and r == 0:
                    copy_o(m, half - 1, 1)
                for n, (kind, of, j) in enumerate(misc_jobs(g)):
                    use = first_use[g] + n
                    if kind == "project":
                        take_projection(m, of, j, use)
                    if kind == "stack":
                        take_stack(m, of, j, use)
                    if kind == "spread":
                        act.wait_ge(misc_full, m * USES + use + 1)
                        nc.scalar.activation(factor, misc_bank(use), ACT.Copy).then_inc(misc_free[use % 2], 1)
                if g in NORM_ACC_ACT:
                    after.early_scalar(act, NORM_ACC_ACT.index(g))
                if g in NORM_X_ACT:
                    after.normalise_x(act, NORM_X_ACT.index(g))

            for _ in range(PROBS):
                act.nop().then_inc(weighed, 1)
            before.scalar(act)
            for h in range(HG):
                rows = other_rows(h)
                zeros = q[0][h][rows].rearrange("p (t n) -> p t n", n=P)
                done = nc.scalar.activation(zeros, k.ident[rows].unsqueeze(1).broadcast_to(list(zeros.shape)), ACT.Copy,
                                            scale=0.0)
            done.then_inc(zeroed, 1)
            act.wait_ge(w_ready, 1)
            for use in range(PROLOGUE_USES):
                if use < chunks:
                    take_projection(0, 0, use, use)
                else:
                    take_stack(0, 0, use - chunks, use)
            timeline(act, step)

        @block.vector
        def _(dve):
            for _ in range(2):
                dve.nop().then_inc(max_free, 1)
            for n in range(2):
                dve.nop().then_inc(misc_free[n], 1)

            def take_max(m, n):
                half, (c, t, part, h) = n // HALF, half_pieces[n % HALF]
                width = min(NB, (t + 1) * P - part * NB)
                dve.wait_ge(max_full, m * PASS + n + 1)
                nc.vector.tensor_reduce(peaks[:, half % 2, n % HALF:n % HALF + 1], max_bank(n)[:, 0:width], AX.X, ALU.max,
                                        negate=True).then_inc(max_free, 1)
                if n % HALF + 1 in chunk_start:
                    take_shift(m, half, c, n)

            def take_shift(m, half, c, n):
                of_chunk = peaks[:, half % 2, chunk_start[c]:chunk_start[c + 1]].rearrange(
                    "p (pair t part i) -> p pair i t part", pair=pairs, t=GT, part=c + 1)
                by_head = lambda a: a.rearrange("p (pair i) t -> p pair i t", i=2)
                hi, lo = (shift[:, :, STACK + i * GT:STACK + (i + 1) * GT] for i in range(2))
                dve.wait_ge(max_free, m * PASS + n + 3)
                if c == 0:
                    nc.vector.tensor_copy(by_head(peak[:]), of_chunk[:, :, :, :, 0]).then_inc(peak_done, 1)
                else:
                    for pair in range(pairs):
                        done = nc.vector.tensor_tensor(peak[:, 2 * pair:2 * pair + 2, :], of_chunk[:, pair, :, :, 0],
                                                       of_chunk[:, pair, :, :, 1], ALU.min)
                    done.then_inc(peak_done, 1)
                base = m * BATCH * chunks * 2 + (half * chunks + c) * 2
                dve.wait_ge(peak_done, base + 1)
                nc.vector.tensor_copy(hi.bitcast(F32R), peak[:]).then_inc(peak_done, 1)
                dve.wait_ge(peak_done, base + 2)
                nc.vector.tensor_tensor(lo, peak[:], hi, ALU.subtract).then_inc(shift_ready, 1)

            def take_lo(m, half, c, use):
                n = m * BATCH * chunks + half * chunks + c + 1
                dve.wait_ge(qk_hi, n)
                nc.vector.scalar_tensor_tensor(out=qk[1][:, c, :], in0=misc_bank(use), scalar=bias[:, 0:1], in1=f32(qk[0][:, c, :]),
                                               op0=ALU.add, op1=ALU.subtract).then_inc(qk_lo, 1)
                dve.wait_ge(qk_lo, n)
                dve.nop().then_inc(misc_free[use % 2], 1)

            def place_maxima(m, g, h):
                for n, (kind, half, c) in enumerate(misc_jobs(g)):
                    if kind == "maxima":
                        use, rows = first_use[g] + n, shift_rows(h)
                        dve.wait_ge(misc_full, m * USES + use + 1)
                        nc.vector.tensor_tensor(
                            q[half % BATCH][h][rows, chunk(c)].rearrange("p (t n) -> p t n", n=P),
                            misc_bank(use)[rows, h * P:(h + 1) * P].unsqueeze(1).broadcast_to([N_SHIFT, GT, P]),
                            tile_rows[rows], ALU.mult).then_inc(shifted, 1)
                        if h == HG - 1:
                            dve.wait_ge(shifted, m * BATCH * chunks * HG + (half * chunks + c + 1) * HG)
                            dve.nop().then_inc(misc_free[use % 2], 1)

            def shared(m, g):
                for h in range(HG):
                    if g - h >= -LEAD_MAX:
                        place_maxima(m, g - h, h)
                for n, (kind, half, c) in enumerate(misc_jobs(g)):
                    use = first_use[g] + n
                    misc = misc_bank(use)
                    if kind in ("spread", "stack"):
                        continue
                    if kind == "project":
                        take_lo(m, half, c, use)
                        continue
                    if kind == "maxima":
                        continue
                    dve.wait_ge(misc_full, m * USES + use + 1)
                    b, at = half % BATCH, half * chunks + c
                    if kind == "v":
                        nc.vector.tensor_tensor(
                            v_all[:, 2 * c:2 * c + 2, :], misc.rearrange("p (t n) -> p t n", t=2),
                            bias_v.unsqueeze(1).broadcast_to([P, 2, C]), ALU.add).then_inc(misc_free[use % 2], 1)
                    elif kind == "sums":
                        nc.vector.reciprocal(over_sum[:], misc[:, 0:GT * HG]).then_inc(inverted, 1)
                        dve.wait_ge(inverted, m * BATCH * chunks + at + 1)
                        dve.nop().then_inc(misc_free[use % 2], 1)
                    else:
                        t = b * ST + c * GT + 2 * int(kind == "out1")
                        nc.vector.tensor_tensor(k.acc[:, t:t + 2, :], k.acc[:, t:t + 2, :],
                                                misc.rearrange("p (t n) -> p t n", n=C), ALU.add).then_inc(misc_free[use % 2], 1)

            def step(m, g):
                if g + LEAD_MAX < STEPS:
                    take_max(m, g + LEAD_MAX)
                shared(m, g)
                if g in NORM_ACC_DVE:
                    wait_read(dve, m, first_use[LAST + 15] + misc_jobs(LAST + 15).index(("out1", HALVES - 2, chunks - 1)))
                    after.early_vector(dve, NORM_ACC_DVE.index(g))
                if g in NORM_X_DVE:
                    after.add_up(dve, NORM_X_DVE.index(g))

            before.rest_of_acc(dve)
            before.vector(dve)
            dve.wait_ge(consts, 128)
            nc.vector.tensor_copy(to_stack[:].rearrange("p a b -> p (a b)"), to_stack_in).then_inc(to_stack_ready, 1)
            nc.vector.tensor_copy(masks[:], masks_in)
            nc.vector.tensor_copy(ident_b[:], k.ident[:]).then_inc(prepared, 1)
            nc.vector.memset(shift[:], 0.0)
            dve.wait_ge(zeroed, 1)
            for c in range(chunks):
                take_lo(0, 0, c, c)
            nc.vector.tensor_copy(k.acc[:], bias_y.unsqueeze(1).broadcast_to([P, TT, C]))
            for b in range(BATCH):
                nc.vector.memset(v[b][:, :, :, D1:], 1.0)
            timeline(dve, step)


def build(nc, ins, out):
    with ExitStack() as ctx:
        k = Core()
        def sb(n, s, d=F32):
            return ctx.enter_context(nc.sbuf_tensor(n, s, d))
        k.x_dram = ins["x"]
        k.acc = sb("acc_sb", [P, TT, C])
        k.xT = [sb(f"xT_{h}", [P, KC, TOK], F32R) for h in ("hi", "lo")]
        k.ident = sb("ident_sb", [P, P])
        k.psum = ctx.enter_context(nc.psum_tensor("psum", [P, 8, NB], F32))
        k.x = sb("x_sb", [P, TT, C])
        half = TT // GT // BATCH
        room = sb("room_sb", [P, sum(Norm.sizes.values())])[:]
        norm1 = Norm(nc, ctx, k, "norm1", x=k.x, room=room, load=True, bank=4, ahead=half)
        norm2 = Norm(nc, ctx, k, "norm2", x=k.x, room=room)
        norm3 = Norm(nc, ctx, k, "norm3", x=k.x, room=room, bank=4, ahead=half)
        norm4 = Norm(nc, ctx, k, "norm4", x=k.x, room=room, out=out)
        attention0_stage(nc, k, "attn0", ins, norm1)
        with ExitStack() as stage:
            first, mlp = mlp_stage(nc, stage, k, "mlp0", ins["ffn0_w"], N_FFN0, norm1, norm2,
                                   hidden_scales=ins["ffn0_scales"], out_scale=ins["down_s"], early_steps=True)
            run_block(nc, norm1.rest(), first, norm1, mlp)
        attention1_stage(nc, k, "attn1", ins, norm2, norm3)
        with ExitStack() as stage:
            weigh = stage.enter_context(nc.sbuf_tensor("weigh", [P, (N_SHARED + N_EXPERT) * TT], F32))
            router, route, weigh_vector = route_stage(nc, stage, k, "route", ins["router"], weigh, norm3)
            first, moe = mlp_stage(nc, stage, k, "moe", ins["moe_w"], N_SHARED + N_EXPERT, norm3, norm4,
                                   weigh=weigh, weigh_vector=weigh_vector)
            run_block(nc, norm3.rest(), first, router, norm3, route, moe, norm4)


def kernel(**inputs):
    import itertools
    import numpy as np
    import concourse.bacc as bacc
    from concourse.bass_utils import run_bass_kernel_spmd

    given = {n: np.asarray(a) for n, a in inputs.items()}
    l0 = {n[len("L0_attn_"):]: a for n, a in given.items() if n.startswith("L0_attn_")}

    def chunks(gate, up, down):
        cut = [a.reshape(KC, P, -1, IM).transpose(2, 1, 0, 3).reshape(-1, P, KC * IM) for a in (gate, up)]
        return np.concatenate([*cut, down.reshape(-1, IM, C)], axis=2)

    def pad_hidden(a):
        return np.pad(a, [(0, N_FFN0 * IM - INTER0)] + [(0, 0)] * (a.ndim - 1))

    arrays = {"x": l0["x"].reshape(TOK, C)}
    for n in "qkvo":
        arrays[f"w{n}_codes"], arrays[f"w{n}_scales"] = l0[f"w{n}_codes"], l0[f"w{n}_scales"]
    for n in "qk":
        arrays[f"b{n}"] = l0[f"b{n}"].reshape(H0, D0).T
    arrays["bv"], arrays["bo"] = l0["bv"], l0["bo"]
    arrays["ffn0_w"] = chunks(*(pad_hidden(given[f"L0_ffn_{n}_w"]).T for n in ("gate", "up")),
                              pad_hidden(given["L0_ffn_down_w"].T))
    arrays["ffn0_scales"] = np.stack([pad_hidden(given[f"L0_ffn_{n}_s"]).reshape(N_FFN0, IM).T for n in ("gate", "up")])
    arrays["down_s"] = given["L0_ffn_down_s"]

    w_attn, b_attn = given["L1_attn_w_attn"], given["L1_attn_b_attn"]
    passes = H1 // HG
    qk = w_attn[:, :2 * C].reshape(KC, P, 2, passes, HG * D1)
    arrays["w_attn"] = qk.transpose(3, 1, 0, 2, 4).reshape(passes, P, KC * P)
    arrays["b_qk"] = b_attn[:2 * C].reshape(2, passes, HG * D1).transpose(1, 0, 2).reshape(passes, P, 1)
    arrays["w_v"] = w_attn[:, 2 * C:].reshape(KC, P, C).transpose(1, 0, 2).reshape(P, KC * C)
    arrays["b_v"] = b_attn[2 * C:]
    w_proj = given["L1_attn_w_proj"].reshape(H1 // HG, HG, D1, C)
    w_proj = np.pad(w_proj, [(0, 0), (0, 0), (0, HEAD_ROWS - D1), (0, 0)])
    arrays["w_proj"] = w_proj.reshape(H1 // HG, P, C).transpose(1, 0, 2).reshape(P, -1)
    arrays["b_proj"] = given["L1_attn_b_proj"]

    arrays["router"] = given["L1_ffn_gate_w"].T.reshape(KC, P, N_EXPERT).transpose(1, 0, 2)
    side_by_side = lambda a: a.transpose(1, 0, 2).reshape(C, N_EXPERT * IM)
    arrays["moe_w"] = np.concatenate([
        chunks(given["L1_ffn_sWg"], given["L1_ffn_sWu"], given["L1_ffn_sWd"]),
        chunks(side_by_side(given["L1_ffn_Wg"]), side_by_side(given["L1_ffn_Wu"]),
               given["L1_ffn_Wd"].reshape(N_EXPERT * IM, C))])

    arrays["ident"] = np.eye(P, dtype=np.float32)
    later = np.full((P, P), -1e30, np.float32)
    arrays["masks"] = np.stack([np.triu(later, 1), np.tril(later, -1)], axis=1)
    arrays["to_stack"] = np.zeros((P, 2, HG // 2, 2, P), np.float32)
    for which, parts in enumerate(((0, 1, 0), (0, 0, 1))):
        for h, (n, part), d in itertools.product(range(HG), enumerate(parts), range(D1)):
            arrays["to_stack"][(which * HG + h) * D1 + d, which, h // 2, part, h % 2 * STACK + n * D1 + d] = 1
    arrays["to_stack"] = arrays["to_stack"].reshape(P, -1)
    own_tile = np.tile(np.repeat(np.eye(GT, dtype=np.float32), P, axis=1), (2, 1)).reshape(2 * GT, GT, P)
    arrays["tile_rows"] = np.zeros((P, GT, P), np.float32)
    for start in (0, STACK):
        arrays["tile_rows"][start:start + 2 * GT] = own_tile
    sum_row = np.arange(HG) * HEAD_ROWS + D1
    arrays["sum_rows"] = (np.arange(P)[:, None] == sum_row).astype(np.float32)

    nc = bacc.Bacc("TRN2", target_bir_lowering=False, num_devices=1)
    arrays = {f"in_{n}": np.ascontiguousarray(a) for n, a in arrays.items()}
    aps = {n[3:]: nc.dram_tensor(n, a.shape, mybir.dt.from_np(a.dtype), kind="ExternalInput").ap()
           for n, a in arrays.items()}
    out = nc.dram_tensor("out", (TOK, C), F32, kind="ExternalOutput").ap()
    build(nc, aps, out)
    result = run_bass_kernel_spmd(nc, [arrays], core_ids=[0])
    return result.results[0]["out"].reshape(BATCH, SEQ, C)
```
